# Optimizing a Trainium2 kernel written in Bass

```python
import numpy as np
import jax
import jax.numpy as jnp

def _softmax(x, axis=-1):
    return jax.nn.softmax(x, axis=axis)

def _gelu(x):
    return jax.nn.gelu(x, approximate=True)

def _silu(x):
    return jax.nn.silu(x)

def _sigmoid(x):
    return jax.nn.sigmoid(x)

def _layernorm(x, axis=-1, eps=1e-05):
    m = jnp.mean(x, axis=axis, keepdims=True)
    v = jnp.var(x, axis=axis, keepdims=True)
    return (x - m) / jnp.sqrt(v + eps)

def _scatter_add(tgt, idx, src, axis=0):
    return tgt.at[idx].add(src)

def _segment_sum(src, seg, n):
    return jax.ops.segment_sum(src, seg, n)
kernel_name = 'mk_seq_preln_d1_jaxref_r8_2bed22'

def setup_inputs(seed: int=0):
    np.random.seed(seed)
    _w = jnp.asarray

    def _L0_attn_setup():
        import jax, jax.numpy as jnp
        import numpy as np
        from jax import lax

        def layer_norm(x, g, b, eps=1e-05):
            m = jnp.mean(x, axis=-1, keepdims=True)
            v = jnp.var(x, axis=-1, keepdims=True)
            return (x - m) * lax.rsqrt(v + eps) * g + b

        def depthwise_causal_conv(u, w, b):
            Din = u.shape[-1]
            k = w.shape[1]
            x = jnp.transpose(u, (0, 2, 1))
            x = jnp.pad(x, ((0, 0), (0, 0), (k - 1, 0)))
            out = lax.conv_general_dilated(x, w[:, None, :], window_strides=(1,), padding='VALID', dimension_numbers=('NCH', 'OIH', 'NCH'), feature_group_count=Din)
            out = out + b[None, :, None]
            return jnp.transpose(out, (0, 2, 1))

        def selective_scan(u, delta, A, Bm, Cm, D):
            dA = jnp.exp(delta[..., None] * A)
            dBu = delta[..., None] * Bm[:, :, None, :] * u[..., None]

            def step(h, xs):
                dA_t, dBu_t, C_t = xs
                h = dA_t * h + dBu_t
                y = jnp.einsum('bdn,bn->bd', h, C_t)
                return (h, y)
            Bsz, L, Din, N = dA.shape
            h0 = jnp.zeros((Bsz, Din, N), dtype=u.dtype)
            _, ys = lax.scan(step, h0, (jnp.moveaxis(dA, 1, 0), jnp.moveaxis(dBu, 1, 0), jnp.moveaxis(Cm, 1, 0)))
            y = jnp.moveaxis(ys, 0, 1)
            return y + u * D
        key = jax.random.key(seed)
        B, L, Dm = (2, 256, 128)
        Din, N, k = (2 * Dm, 16, 4)
        dt_rank = Dm // 16
        ks = jax.random.split(key, 8)
        s = 0.02
        return {'x': jax.random.normal(ks[0], (B, L, Dm), jnp.float32), 'in_proj_w': jax.random.normal(ks[1], (Dm, 2 * Din), jnp.float32) * s, 'conv_w': jax.random.normal(ks[2], (Din, k), jnp.float32) * 0.1, 'conv_b': jnp.zeros((Din,), jnp.float32), 'x_proj_w': jax.random.normal(ks[3], (Din, dt_rank + 2 * N), jnp.float32) * s, 'dt_proj_w': jax.random.normal(ks[4], (dt_rank, Din), jnp.float32) * s, 'dt_proj_b': jax.random.uniform(ks[5], (Din,), jnp.float32, -4.0, -2.0), 'A_log': jnp.log(jnp.tile(jnp.arange(1, N + 1, dtype=jnp.float32)[None, :], (Din, 1))), 'D': jnp.ones((Din,), jnp.float32), 'out_proj_w': jax.random.normal(ks[6], (Din, Dm), jnp.float32) * s, 'ln_g': jnp.ones((Dm,), jnp.float32), 'ln_b': jnp.zeros((Dm,), jnp.float32)}
    _L0_attn_in = _L0_attn_setup()

    def _L0_ffn_setup():
        import jax, jax.numpy as jnp
        import numpy as np
        B, S, D, F, E = (1, 128, 128, 512, 8)
        EPS = 1e-05

        def _sublayer(xs, g, b, W1e, b1e, W2e, b2e):
            mu = jnp.mean(xs, axis=-1, keepdims=True)
            var = jnp.mean(jnp.square(xs - mu), axis=-1, keepdims=True)
            h = (xs - mu) * jax.lax.rsqrt(var + EPS) * g + b
            return xs + jax.nn.relu(h @ W1e.T + b1e) @ W2e.T + b2e
        key = jax.random.key(seed)
        ks = jax.random.split(key, 4)
        x = jax.random.normal(ks[0], (B, S, D), jnp.float32)
        centroids = jax.random.normal(ks[1], (E, D), jnp.float32) * 0.1
        gamma = jnp.ones((E, D), jnp.float32)
        beta = jnp.zeros((E, D), jnp.float32)
        W1 = jax.random.normal(ks[2], (E, F, D), jnp.float32) * 0.02
        b1 = jnp.zeros((E, F), jnp.float32)
        W2 = jax.random.normal(ks[3], (E, D, F), jnp.float32) * 0.02
        b2 = jnp.zeros((E, D), jnp.float32)
        return {'x': x, 'centroids': centroids, 'gamma': gamma, 'beta': beta, 'W1': W1, 'b1': b1, 'W2': W2, 'b2': b2}
    _L0_ffn_in = _L0_ffn_setup()
    _d = {'L0_attn_x': _L0_attn_in['x'], 'L0_attn_in_proj_w': _L0_attn_in['in_proj_w'], 'L0_attn_conv_w': _L0_attn_in['conv_w'], 'L0_attn_conv_b': _L0_attn_in['conv_b'], 'L0_attn_x_proj_w': _L0_attn_in['x_proj_w'], 'L0_attn_dt_proj_w': _L0_attn_in['dt_proj_w'], 'L0_attn_dt_proj_b': _L0_attn_in['dt_proj_b'], 'L0_attn_A_log': _L0_attn_in['A_log'], 'L0_attn_D': _L0_attn_in['D'], 'L0_attn_out_proj_w': _L0_attn_in['out_proj_w'], 'L0_attn_ln_g': _L0_attn_in['ln_g'], 'L0_attn_ln_b': _L0_attn_in['ln_b'], 'L0_ffn_centroids': _L0_ffn_in['centroids'], 'L0_ffn_gamma': _L0_ffn_in['gamma'], 'L0_ffn_beta': _L0_ffn_in['beta'], 'L0_ffn_W1': _L0_ffn_in['W1'], 'L0_ffn_b1': _L0_ffn_in['b1'], 'L0_ffn_W2': _L0_ffn_in['W2'], 'L0_ffn_b2': _L0_ffn_in['b2']}
    _x0 = _d['L0_attn_x']
    _d['L0_attn_x'] = jax.random.normal(jax.random.fold_in(jax.random.key(seed), 1), (2, 2048, 128), dtype=_x0.dtype)
    del _x0
    return _d

def reference(L0_attn_x, L0_attn_in_proj_w, L0_attn_conv_w, L0_attn_conv_b, L0_attn_x_proj_w, L0_attn_dt_proj_w, L0_attn_dt_proj_b, L0_attn_A_log, L0_attn_D, L0_attn_out_proj_w, L0_attn_ln_g, L0_attn_ln_b, L0_ffn_centroids, L0_ffn_gamma, L0_ffn_beta, L0_ffn_W1, L0_ffn_b1, L0_ffn_W2, L0_ffn_b2):

    def _L0_attn_ref(x, in_proj_w, conv_w, conv_b, x_proj_w, dt_proj_w, dt_proj_b, A_log, D, out_proj_w, ln_g, ln_b):
        import jax, jax.numpy as jnp
        import numpy as np
        from jax import lax

        def layer_norm(x, g, b, eps=1e-05):
            m = jnp.mean(x, axis=-1, keepdims=True)
            v = jnp.var(x, axis=-1, keepdims=True)
            return (x - m) * lax.rsqrt(v + eps) * g + b

        def depthwise_causal_conv(u, w, b):
            Din = u.shape[-1]
            k = w.shape[1]
            x = jnp.transpose(u, (0, 2, 1))
            x = jnp.pad(x, ((0, 0), (0, 0), (k - 1, 0)))
            out = lax.conv_general_dilated(x, w[:, None, :], window_strides=(1,), padding='VALID', dimension_numbers=('NCH', 'OIH', 'NCH'), feature_group_count=Din)
            out = out + b[None, :, None]
            return jnp.transpose(out, (0, 2, 1))

        def selective_scan(u, delta, A, Bm, Cm, D):
            dA = jnp.exp(delta[..., None] * A)
            dBu = delta[..., None] * Bm[:, :, None, :] * u[..., None]

            def step(h, xs):
                dA_t, dBu_t, C_t = xs
                h = dA_t * h + dBu_t
                y = jnp.einsum('bdn,bn->bd', h, C_t)
                return (h, y)
            Bsz, L, Din, N = dA.shape
            h0 = jnp.zeros((Bsz, Din, N), dtype=u.dtype)
            _, ys = lax.scan(step, h0, (jnp.moveaxis(dA, 1, 0), jnp.moveaxis(dBu, 1, 0), jnp.moveaxis(Cm, 1, 0)))
            y = jnp.moveaxis(ys, 0, 1)
            return y + u * D
        residual = x
        xn = layer_norm(x, ln_g, ln_b)
        xz = xn @ in_proj_w
        Din = in_proj_w.shape[1] // 2
        u, z = (xz[..., :Din], xz[..., Din:])
        u = jax.nn.silu(depthwise_causal_conv(u, conv_w, conv_b))
        N = A_log.shape[1]
        dt_rank = x_proj_w.shape[1] - 2 * N
        dbc = u @ x_proj_w
        dt = dbc[..., :dt_rank]
        Bm = dbc[..., dt_rank:dt_rank + N]
        Cm = dbc[..., dt_rank + N:]
        delta = jax.nn.softplus(dt @ dt_proj_w + dt_proj_b)
        A = -jnp.exp(A_log)
        y = selective_scan(u, delta, A, Bm, Cm, D)
        y = y * jax.nn.silu(z)
        out = y @ out_proj_w
        return residual + out

    def _L0_ffn_ref(x, centroids, gamma, beta, W1, b1, W2, b2):
        import jax, jax.numpy as jnp
        import numpy as np
        B, S, D, F, E = (1, 128, 128, 512, 8)
        EPS = 1e-05

        def _sublayer(xs, g, b, W1e, b1e, W2e, b2e):
            mu = jnp.mean(xs, axis=-1, keepdims=True)
            var = jnp.mean(jnp.square(xs - mu), axis=-1, keepdims=True)
            h = (xs - mu) * jax.lax.rsqrt(var + EPS) * g + b
            return xs + jax.nn.relu(h @ W1e.T + b1e) @ W2e.T + b2e
        feats = x.reshape(-1, x.shape[-1])
        scores = jax.lax.stop_gradient(feats @ centroids.T)
        expert = jnp.argmax(scores, axis=1)
        onehot = jax.nn.one_hot(expert, E, dtype=feats.dtype)
        alpha = jax.nn.sigmoid(jnp.sum(feats * centroids[expert], axis=-1, keepdims=True))
        ys = jax.vmap(_sublayer, in_axes=(None, 0, 0, 0, 0, 0, 0))(feats, gamma, beta, W1, b1, W2, b2)
        y = jnp.einsum('te,etd->td', onehot, ys)
        out = alpha * y + (1.0 - alpha) * feats
        return out.reshape(x.shape)
    x = L0_attn_x
    x = x + _L0_attn_ref(_layernorm(x, axis=-1), L0_attn_in_proj_w, L0_attn_conv_w, L0_attn_conv_b, L0_attn_x_proj_w, L0_attn_dt_proj_w, L0_attn_dt_proj_b, L0_attn_A_log, L0_attn_D, L0_attn_out_proj_w, L0_attn_ln_g, L0_attn_ln_b)
    x = x + _L0_ffn_ref(_layernorm(x, axis=-1), L0_ffn_centroids, L0_ffn_gamma, L0_ffn_beta, L0_ffn_W1, L0_ffn_b1, L0_ffn_W2, L0_ffn_b2)
    return x

_drawn_inputs = setup_inputs


def setup_inputs(seed=0):
    import zlib

    import numpy as np

    out = dict(_drawn_inputs(seed))
    spreads = {'L0_attn_conv_b': (0.0, 0.8),
     'L0_attn_D': (1.0, 0.6),
     'L0_attn_ln_g': (1.0, 0.6),
     'L0_attn_ln_b': (0.0, 0.8),
     'L0_ffn_gamma': (1.0, 0.6),
     'L0_ffn_beta': (0.0, 2.0),
     'L0_ffn_b1': (0.0, 2.0),
     'L0_ffn_b2': (0.0, 2.0)}
    factors = {'L0_attn_in_proj_w': 8.0,
     'L0_attn_conv_w': 8.0,
     'L0_attn_x_proj_w': 8.0,
     'L0_attn_dt_proj_w': 8.0,
     'L0_attn_dt_proj_b': 8.0,
     'L0_attn_A_log': 8.0,
     'L0_attn_out_proj_w': 8.0,
     'L0_ffn_W1': 25.68,
     'L0_ffn_centroids': 8.0,
     'L0_ffn_W2': 8.0}
    for name, (base, spread) in spreads.items():
        noise = np.random.default_rng([zlib.crc32(name.encode()), seed]).standard_normal(out[name].shape)
        drawn = base * np.exp(spread * noise) if base else spread * noise
        out[name] = jnp.asarray(drawn.astype(out[name].dtype))
    for name, factor in factors.items():
        out[name] = (out[name] * factor).astype(out[name].dtype)
    return out
```

```python
from contextlib import ExitStack

import concourse.bass as bass
from concourse import mybir

P = 128
F32 = mybir.dt.float32
ALU = mybir.AluOpType
ACT = mybir.ActivationFunctionType
AX = mybir.AxisListType
EPS = 1e-5


def mamba_layer(nc, x, in_proj_w, conv_w, conv_b, x_proj_w, dt_proj_w, dt_proj_b, A_log, D, out_proj_w,
                ln_g, ln_b, bc_scratch, x_all, x_mid):
    B, L, DM = x.shape
    DIN, N = A_log.shape
    R = x_proj_w.shape[1] - 2 * N
    TAPS = conv_w.shape[1]
    T = B * L
    BLOCKS = T // P
    C = 512
    CHUNKS = T // C
    SEQ_CHUNKS = L // C
    CB = C // P
    HALVES = DIN // P
    S, DG = 4, 32
    Q = P // DG
    G = HALVES * Q
    J = N // S
    K = G * J
    DA_RING, H_RING = 4, 16
    PAD = TAPS - 1
    assert DM == P and N == S * J and K % H_RING == 0 and 2 * N + R <= P

    with ExitStack() as ctx:
        def sb(name, shape):
            return ctx.enter_context(nc.sbuf_tensor(name, shape, F32))

        def bank(name):
            return ctx.enter_context(nc.psum_tensor(name, [P, C], F32))

        def sem(name):
            return ctx.enter_context(nc.semaphore(name))

        win = sb("win", [P, 2 * DIN])
        conv_rep = sb("conv_rep", [P, DIN, TAPS])
        w_tap = sb("w_tap", [P, TAPS, DIN])
        conv_b_half = sb("conv_b_half", [P, HALVES])
        w_xproj = sb("w_xproj", [P, HALVES, P])
        w_dt = sb("w_dt", [P, DIN])
        dt_bias = sb("dt_bias", [P, HALVES])
        a_log = sb("a_log", [P, HALVES, N])
        a_neg = sb("a_neg", [P, HALVES, N])
        a_rep = sb("a_rep", [P, G, J])
        d_skip = sb("d_skip", [P, HALVES])
        w_out = sb("w_out", [P, HALVES, DM])
        g_col = sb("g_col", [P, 1])
        b_col = sb("b_col", [P, 1])
        ident = sb("ident", [P, P])
        spread = sb("spread", [P, Q, P])
        gather = sb("gather", [P, DG])
        started = sb("started", [P, 1])
        stats = sb("stats", [P, BLOCKS, 6])
        mv = sb("mv", [P, BLOCKS, 2])
        var_eps = sb("var_eps", [P, BLOCKS])
        neg_half = sb("neg_half", [P, BLOCKS])
        rstd = sb("rstd", [P, BLOCKS])
        var2 = sb("var2", [P, BLOCKS])
        rstd2 = sb("rstd2", [P, BLOCKS])
        scale_n = sb("scale_n", [P, BLOCKS])
        scale_b = sb("scale_b", [P, BLOCKS])
        shift_b = sb("shift_b", [P, BLOCKS])
        xh = sb("xh", [P, CB, P])
        xn_t = sb("xn_t", [P, B * (PAD + L)])
        pre = sb("pre", [P, HALVES, C])
        th = sb("th", [P, HALVES, C])
        tz = sb("tz", [P, HALVES, C])
        u = sb("u", [P, 2, HALVES, C])
        zg = sb("zg", [P, 2, HALVES, C])
        w = sb("w", [P, 2, HALVES, C])
        delta = sb("delta", [P, HALVES, C])
        delta_rep = sb("delta_rep", [P, G, C])
        bc = sb("bc", [P, C])
        bc_rep = sb("bc_rep", [P, 2, 2 * J, C])
        da = sb("da", [P, DA_RING, C])
        h = sb("h", [P, H_RING, C])
        carry = sb("carry", [P, CHUNKS + B, K])
        yg = sb("yg", [P, HALVES, C])
        base = sb("base", [P, CB, P])

        w_ps = [bank("w_ps0"), bank("w_ps1")]
        dbu = [bank("dbu0"), bank("dbu1")]
        y_ps = [bank("y_ps0"), bank("y_ps1")]
        pa = [bank("pa0"), bank("pa1")]

        x_in = sem("x_in")
        weights_in = sem("weights_in")
        iota_done = sem("iota_done")
        zeroed = sem("zeroed")
        wtap_ready = sem("wtap_ready")
        aneg_ready = sem("aneg_ready")
        arep_mm = sem("arep_mm")
        arep_ready = sem("arep_ready")
        stats_done = sem("stats_done")
        aggr_done = sem("aggr_done")
        vareps_ready = sem("vareps_ready")
        rstd_ready = sem("rstd_ready")
        var2_ready = sem("var2_ready")
        rstd2_ready = sem("rstd2_ready")
        norm_ready = sem("norm_ready")
        halfbias_ready = sem("halfbias_ready")
        xh_ready = sem("xh_ready")
        tr_done = sem("tr_done")
        xn_ready = sem("xn_ready")
        umm_done = sem("umm_done")
        uact_done = sem("uact_done")
        u_ready = sem("u_ready")
        zmm_done = sem("zmm_done")
        zact_done = sem("zact_done")
        zg_done = sem("zg_done")
        xpmm_done = sem("xpmm_done")
        bc_ready = sem("bc_ready")
        scr_written = sem("scr_written")
        bcrep_landed = sem("bcrep_landed")
        dmm_done = sem("dmm_done")
        dact_done = sem("dact_done")
        e_ready = sem("e_ready")
        ln_ready = sem("ln_ready")
        g_ready = sem("g_ready")
        d1_done = sem("d1_done")
        d2_done = sem("d2_done")
        delta_ready = sem("delta_ready")
        w_ready = sem("w_ready")
        drep0_landed = sem("drep0_landed")
        drep1_landed = sem("drep1_landed")
        wrep_ready = sem("wrep_ready")
        exp_done = sem("exp_done")
        mul_done = sem("mul_done")
        scan_done = sem("scan_done")
        carry_saved = sem("carry_saved")
        hc_done = sem("hc_done")
        nsum_done = sem("nsum_done")
        yv_done = sem("yv_done")
        yg_done = sem("yg_done")
        op_done = sem("op_done")
        base_ready = sem("base_ready")
        x1_done = sem("x1_done")
        mid_out = sem("mid_out")
        ts_done = sem("ts_done")
        gather_step = sem("gather_step")
        consts_ready = sem("consts_ready")
        drep_landed = [drep0_landed, drep1_landed]
        WEIGHT_LOADS = 9 + 3 * HALVES

        def at(i, n):
            return bass.ds(i, n)

        def slot(f):
            return f + f // SEQ_CHUNKS

        def xn_cols(f, shift):
            return at(f * C + (f // SEQ_CHUNKS) * PAD + shift, C)

        def walk(eng, body):
            body(0, True, False)
            with eng.Fori(1, CHUNKS - 1) as f:
                body(f, True, True)
            body(CHUNKS - 1, False, True)

        block = ctx.enter_context(nc.Block())

        @block.sync
        def _(sp):
            x_v = x.rearrange("b (n p) d -> p (b n) d", p=P)
            for i in range(4):
                sp.dma_start(x_all[:, 8 * i:8 * i + 8, :], x_v[:, 8 * i:8 * i + 8, :]).then_inc(x_in, 16)
            sp.wait_ge(zeroed, 1)
            sp.dma_start(w_xproj[:, :, 0:2 * N], x_proj_w[:, R:].rearrange("(h p) n -> p h n", p=P)).then_inc(weights_in, 16)
            sp.dma_start(w_xproj[:, :, 2 * N:2 * N + R], x_proj_w[:, 0:R].rearrange("(h p) n -> p h n", p=P)).then_inc(weights_in, 16)
            sp.dma_start(w_dt[2 * N:2 * N + R, :], dt_proj_w).then_inc(weights_in, 16)

            def bc_replicate(n):
                sp.wait_ge(bc_ready, n + 1)
                if not isinstance(n, int) or n >= 1:
                    sp.wait_ge(bcrep_landed, 64 * n)
                sp.dma_start(bc_scratch, bc[0:2 * N, :]).then_inc(scr_written, 16)
                sp.wait_ge(scr_written, 16 * n + 16)
                if not isinstance(n, int) or n >= 2:
                    sp.wait_ge(consts_ready, 1)
                    sp.wait_ge(mul_done, K * n - K)
                    sp.wait_ge(hc_done, K * n - K)
                src = bc_scratch.rearrange("(j s) t -> s j t", s=S)
                for st in range(S):
                    dst = bc_rep[DG * st:DG * st + DG, at(n % 2, 1), :, :].rearrange("p o j t -> p (o j) t")
                    sp.dma_start(dst, src[st:st + 1, :, :].broadcast_to([DG, 2 * J, C])).then_inc(bcrep_landed, 16)

            def delta_replicate(n, half):
                sp.wait_ge(consts_ready, 1)
                if half == 0:
                    sp.wait_ge(delta_ready, n + 1)
                if not isinstance(n, int) or n >= 1:
                    sp.wait_ge(exp_done, K * n - K + (K // HALVES) * (half + 1))
                for st in range(S):
                    for q in range(Q):
                        sp.dma_start(delta_rep[DG * st:DG * st + DG, Q * half + q, :],
                                     delta[DG * q:DG * q + DG, half, :]).then_inc(drep_landed[half], 16)

            bc_replicate(0)
            delta_replicate(0, 0)
            delta_replicate(0, 1)

            def body(f, prepare, finish):
                if prepare:
                    sp.wait_ge(consts_ready, 1)
                    bc_replicate(f + 1)
                    delta_replicate(f + 1, 0)
                    delta_replicate(f + 1, 1)
            body(0, True, False)
            with sp.Fori(1, CHUNKS - 1) as f:
                body(f, True, True)
            sp.wait_ge(x1_done, CHUNKS)
            if x_mid is not None:
                sp.dma_start(x_mid.rearrange("b (n p) d -> p (b n) d", p=P), x_all[:, :, :]).then_inc(mid_out, 16)
                sp.wait_ge(mid_out, 16)

        @block.gpsimd
        def _(pool):
            g = nc.gpsimd
            g.memset(w_xproj[:, :, :], 0.0)
            g.memset(w_dt[:, :], 0.0).then_inc(zeroed, 1)
            g.memset(neg_half[:, :], -0.5)
            g.memset(ident[:, :], 0.0)
            g.memset(spread[:, :, :], 0.0)
            g.memset(gather[:, :], 0.0)
            g.memset(carry[:, :, :], 0.0)
            for b in range(B):
                last = g.memset(xn_t[:, b * (PAD + L):b * (PAD + L) + PAD], 0.0)
            last.then_inc(iota_done, 1)
            pool.wait_ge(iota_done, 1)
            g.affine_select(out=ident[:, :], in_=ident[:, :], compare_op=ALU.not_equal, fill=1.0, base=0,
                            pattern=[[-1, P]], channel_multiplier=1)
            for q in range(Q):
                v = spread[:, q, :].rearrange("p (s d) -> p s d", s=S)
                g.affine_select(out=v, in_=v, compare_op=ALU.not_equal, fill=1.0, base=-DG * q,
                                pattern=[[0, S], [-1, DG]], channel_multiplier=1)
            for st in range(S):
                g.affine_select(out=gather[:, :], in_=gather[:, :], compare_op=ALU.not_equal, fill=1.0, base=-DG * st,
                                pattern=[[-1, DG]], channel_multiplier=1).then_inc(gather_step, 1)
                pool.wait_ge(gather_step, st + 1)
            g.memset(started[:, :], 0.0).then_inc(consts_ready, 1)
            pool.wait_ge(weights_in, 16 * WEIGHT_LOADS)
            for k in range(TAPS):
                last = g.tensor_tensor(w_tap[:, k, :], win[:, 0:DIN], conv_rep[:, :, k], ALU.mult)
            last.then_inc(wtap_ready, 1)
            pool.wait_ge(vareps_ready, 1)
            g.tensor_tensor(rstd[:, :], var_eps[:, :], neg_half[:, :], ALU.pow).then_inc(rstd_ready, 1)
            pool.wait_ge(var2_ready, 1)
            g.tensor_tensor(rstd2[:, :], var2[:, :], neg_half[:, :], ALU.pow).then_inc(rstd2_ready, 1)

            def softplus_sum(n):
                flat = delta[:, :, :]
                pool.wait_ge(g_ready, n + 1)
                pool.wait_ge(ln_ready, n + 1)
                g.tensor_tensor(flat, pre[:, :, :], flat, ALU.subtract).then_inc(d1_done, 1)
                pool.wait_ge(d1_done, n + 1)
                g.tensor_tensor(flat, flat, tz[:, :, :], ALU.add).then_inc(d2_done, 1)
                pool.wait_ge(d2_done, n + 1)
                g.tensor_tensor(flat, flat, th[:, :, :], ALU.add).then_inc(delta_ready, 1)

            softplus_sum(0)

            def body(f, prepare, finish):
                for gr in range(G):
                    if gr == 4 and prepare:
                        softplus_sum(f + 1)
                    pool.wait_ge(scan_done, K * f + J * gr + J)
                    first = (J * gr) % H_RING
                    g.tensor_copy(carry[:, at(slot(f) + 1, 1), J * gr:J * gr + J].rearrange("p o k -> p (o k)"),
                                  h[:, first:first + J, C - 1]).then_inc(carry_saved, J)
                    pool.wait_ge(consts_ready, 1)
                    pool.wait_ge(carry_saved, K * f + J * gr + J)
                    if gr == 0:
                        pool.wait_ge(bcrep_landed, 64 * f + 64)
                    for j in range(J):
                        hk = h[:, first + j, :]
                        c_rep = bc_rep[:, at(f % 2, 1), J + j, :].rearrange("p o t -> p (o t)")
                        g.tensor_tensor(hk, hk, c_rep, ALU.mult).then_inc(hc_done, 1)
            walk(pool, body)

        @block.vector
        def _(dve):
            v = nc.vector
            for i in range(BLOCKS):
                if i % 8 == 0:
                    dve.wait_ge(x_in, 64)
                last = v.bn_stats(stats[:, i, :], x_all[:, i, :])
            last.then_inc(stats_done, 1)
            dve.wait_ge(stats_done, 1)
            for i in range(BLOCKS):
                last = v.bn_aggr(mv[:, i, :], stats[:, i, :])
            last.then_inc(aggr_done, 1)
            dve.wait_ge(aggr_done, 1)
            v.tensor_scalar(var_eps[:, :], mv[:, :, 1], EPS, None, ALU.add).then_inc(vareps_ready, 1)
            dve.wait_ge(rstd_ready, 1)
            v.tensor_tensor(scale_n[:, :], mv[:, :, 1], rstd[:, :], ALU.mult).then_inc(ts_done, 1)
            dve.wait_ge(ts_done, 1)
            v.tensor_tensor(var2[:, :], scale_n[:, :], rstd[:, :], ALU.mult).then_inc(ts_done, 1)
            dve.wait_ge(ts_done, 2)
            v.tensor_scalar(var2[:, :], var2[:, :], EPS, None, ALU.add).then_inc(var2_ready, 1)
            v.tensor_scalar(scale_b[:, :], rstd[:, :], 1.0, None, ALU.add)
            v.scalar_tensor_tensor(out=shift_b[:, :], in0=mv[:, :, 0], scalar=-1.0, in1=rstd[:, :],
                                   op0=ALU.mult, op1=ALU.mult)
            dve.wait_ge(rstd2_ready, 1)
            v.tensor_tensor(scale_n[:, :], rstd[:, :], rstd2[:, :], ALU.mult).then_inc(norm_ready, 1)
            dve.wait_ge(norm_ready, 1)
            dve.wait_ge(weights_in, 16 * WEIGHT_LOADS)
            v.tensor_scalar(conv_b_half[:, :], conv_b_half[:, :], 0.5, None, ALU.mult).then_inc(halfbias_ready, 1)
            dve.wait_ge(aneg_ready, 1)
            v.tensor_scalar(a_neg[:, :, :], a_neg[:, :, :], -1.0, None, ALU.mult).then_inc(aneg_ready, 1)
            dve.wait_ge(arep_mm, 1)
            for gr in range(G):
                for st in range(S):
                    src = pa[1][DG * st:DG * st + DG, N * gr:N * gr + N].rearrange("p (j s) -> p j s", s=S)
                    last = v.tensor_copy(a_rep[DG * st:DG * st + DG, gr, :], src[:, :, st])
            last.then_inc(arep_ready, 1)

            def normalise(n):
                if not isinstance(n, int) or n >= 1:
                    dve.wait_ge(tr_done, n)
                for b in range(CB):
                    m = mv[:, at(n * CB + b, 1), 0]
                    sc = scale_n[:, at(n * CB + b, 1)]
                    last = v.tensor_scalar(xh[:, b, :], x_all[:, at(n * CB + b, 1), :].rearrange("p o d -> p (o d)"),
                                           m, sc, ALU.subtract, ALU.mult)
                last.then_inc(xh_ready, 1)

            def silu_u(n):
                dve.wait_ge(uact_done, 2 * n + 2)
                v.scalar_tensor_tensor(out=u[:, at(n % 2, 1), :, :].rearrange("p o h t -> p (o h t)"),
                                       in0=th[:, :, :].rearrange("p h t -> p (h t)"), scalar=1.0,
                                       in1=pre[:, :, :].rearrange("p h t -> p (h t)"),
                                       op0=ALU.add, op1=ALU.mult).then_inc(u_ready, 1)

            def silu_z(n):
                for half in range(HALVES):
                    dve.wait_ge(zact_done, 2 * n + half + 1)
                    v.scalar_tensor_tensor(out=zg[:, at(n % 2, 1), half, :].rearrange("p o t -> p (o t)"),
                                           in0=tz[:, half, :], scalar=1.0, in1=pa[1 - half][:, :],
                                           op0=ALU.add, op1=ALU.mult).then_inc(zg_done, 1)

            def log1p_grid(n):
                dve.wait_ge(e_ready, n + 1)
                if not isinstance(n, int) or n >= 1:
                    dve.wait_ge(drep0_landed, 16 * S * Q * n)
                    dve.wait_ge(drep1_landed, 16 * S * Q * n)
                    dve.wait_ge(w_ready, n)
                v.tensor_scalar(delta[:, :, :], tz[:, :, :], 1.0, 1.0, ALU.add, ALU.subtract).then_inc(g_ready, 1)

            def delta_u(n):
                dve.wait_ge(delta_ready, n + 1)
                v.tensor_tensor(w[:, at(n % 2, 1), :, :].rearrange("p o h t -> p (o h) t"), delta[:, :, :],
                                u[:, at(n % 2, 1), :, :].rearrange("p o h t -> p (o h) t"), ALU.mult).then_inc(w_ready, 1)

            def gate(f, half):
                dve.wait_ge(nsum_done, 4 * f + 2 * half + 2)
                if half == 0 and (not isinstance(f, int) or f >= 1):
                    dve.wait_ge(op_done, f)
                v.scalar_tensor_tensor(out=yg[:, half, :], in0=u[:, at(f % 2, 1), half, :].rearrange("p o t -> p (o t)"),
                                       scalar=d_skip[:, half:half + 1], in1=y_ps[half][:, :],
                                       op0=ALU.mult, op1=ALU.add).then_inc(yv_done, 1)
                dve.wait_ge(yv_done, 2 * f + half + 1)
                v.scalar_tensor_tensor(out=yg[:, half, :], in0=yg[:, half, :], scalar=0.5,
                                       in1=zg[:, at(f % 2, 1), half, :].rearrange("p o t -> p (o t)"),
                                       op0=ALU.mult, op1=ALU.mult).then_inc(yg_done, 1)

            def residual(f):
                dve.wait_ge(op_done, f + 1)
                dve.wait_ge(base_ready, f + 1)
                v.tensor_tensor(x_all[:, at(f * CB, CB), :], pa[0][:, :].rearrange("p (b d) -> p b d", b=CB),
                                base[:, :, :], ALU.add).then_inc(x1_done, 1)

            def mul(f, k):
                gr, j = divmod(k, J)
                if j == 0:
                    dve.wait_ge(wrep_ready, G * f + gr + 1)
                if k == 0:
                    dve.wait_ge(bcrep_landed, 64 * f + 64)
                if not isinstance(f, int) or K * f + k >= 2:
                    dve.wait_ge(scan_done, K * f + k - 1)
                v.tensor_tensor(dbu[k % 2][:, :], w_ps[gr % 2][:, :],
                                bc_rep[:, at(f % 2, 1), j, :].rearrange("p o t -> p (o t)"),
                                ALU.mult).then_inc(mul_done, 1)

            def scan(f, k):
                gr, j = divmod(k, J)
                dve.wait_ge(exp_done, K * f + k + 1)
                dve.wait_ge(mul_done, K * f + k + 1)
                if k % 8 == 0 and (not isinstance(f, int) or 4 * f + k // 8 >= 2):
                    dve.wait_ge(nsum_done, 4 * f + k // 8 - 1)
                if j == 0 and (not isinstance(f, int) or f >= 1):
                    dve.wait_ge(carry_saved, K * f - K + J * gr + J)
                v.tensor_tensor_scan(h[:, k % H_RING, :], da[:, k % DA_RING, :], dbu[k % 2][:, :],
                                     carry[:, at(slot(f), 1), k], ALU.mult, ALU.add).then_inc(scan_done, 1)

            normalise(0)
            silu_u(0)
            silu_z(0)
            log1p_grid(0)
            delta_u(0)

            def body(f, prepare, finish):
                for k in range(K):
                    if prepare and k == 0:
                        normalise(f + 1)
                    if finish and k == 8:
                        gate(f - 1, 1)
                    if prepare and k == 10:
                        silu_u(f + 1)
                    if prepare and k == 12:
                        silu_z(f + 1)
                    if finish and k == 16:
                        residual(f - 1)
                    if prepare and k == 20:
                        log1p_grid(f + 1)
                    if k == 24:
                        gate(f, 0)
                    if prepare and k == 29:
                        delta_u(f + 1)
                    mul(f, k)
                    if k:
                        scan(f, k - 1)
                scan(f, K - 1)
            walk(dve, body)
            gate(CHUNKS - 1, 1)
            residual(CHUNKS - 1)

        @block.scalar
        def _(act):
            a = nc.scalar
            act.dma_start(win[:, :], in_proj_w).then_inc(weights_in, 16)
            act.dma_start(conv_rep[:, :, :].rearrange("p d k -> p (d k)"),
                          conv_w.rearrange("(o d) k -> o (d k)", o=1).broadcast_to([P, DIN * TAPS])).then_inc(weights_in, 16)
            for dst, src in ((conv_b_half, conv_b), (dt_bias, dt_proj_b), (d_skip, D)):
                for half in range(HALVES):
                    act.dma_start(dst[:, half:half + 1], src[P * half:P * half + P].rearrange("(p o) -> p o", o=1))\
                       .then_inc(weights_in, 16)
            act.dma_start(a_log[:, :, :], A_log.rearrange("(h p) n -> p h n", p=P)).then_inc(weights_in, 16)
            act.dma_start(w_out[:, :, :], out_proj_w.rearrange("(h p) n -> p h n", p=P)).then_inc(weights_in, 16)
            act.dma_start(g_col[:, :], ln_g.rearrange("(p o) -> p o", o=1)).then_inc(weights_in, 16)
            act.dma_start(b_col[:, :], ln_b.rearrange("(p o) -> p o", o=1)).then_inc(weights_in, 16)
            act.wait_ge(weights_in, 16 * WEIGHT_LOADS)
            a.activation(a_neg[:, :, :], a_log[:, :, :], ACT.Exp).then_inc(aneg_ready, 1)
            act.wait_ge(halfbias_ready, 1)

            def norm_out(n):
                act.wait_ge(tr_done, n + 1)
                a.activation(xn_t[:, xn_cols(n, PAD)], pa[0][:, :], ACT.Identity, scale=g_col[:, :],
                             bias=b_col[:, :]).then_inc(xn_ready, 1)

            def tanh_u(n):
                for half in range(HALVES):
                    act.wait_ge(umm_done, 2 * n + half + 1)
                    if half == 0 and (not isinstance(n, int) or n >= 1):
                        act.wait_ge(delta_ready, n)
                    a.activation(pre[:, half, :], pa[1 - half][:, :], ACT.Identity, scale=0.5,
                                 bias=conv_b_half[:, half:half + 1])
                    a.activation(th[:, half, :], pa[1 - half][:, :], ACT.Tanh, scale=0.5,
                                 bias=conv_b_half[:, half:half + 1]).then_inc(uact_done, 1)

            def tanh_z(n):
                for half in range(HALVES):
                    act.wait_ge(zmm_done, 2 * n + half + 1)
                    a.activation(tz[:, half, :], pa[1 - half][:, :], ACT.Tanh, scale=0.5).then_inc(zact_done, 1)

            def bc_out(n):
                act.wait_ge(xpmm_done, n + 1)
                if not isinstance(n, int) or n >= 1:
                    act.wait_ge(scr_written, 16 * n)
                    act.wait_ge(dmm_done, 2 * n)
                a.activation(bc[:, :], pa[1][:, :], ACT.Identity).then_inc(bc_ready, 1)

            def softplus_parts(n):
                act.wait_ge(u_ready, n + 1)
                for half in range(HALVES):
                    act.wait_ge(dmm_done, 2 * n + half + 1)
                    a.activation(pre[:, half, :], pa[1 - half][:, :], ACT.Abs, bias=dt_bias[:, half:half + 1])
                    a.activation(th[:, half, :], pa[1 - half][:, :], ACT.Relu,
                                 bias=dt_bias[:, half:half + 1]).then_inc(dact_done, 1)
                act.wait_ge(dact_done, 2 * n + 2)
                act.wait_ge(zg_done, 2 * n + 2)
                a.activation(tz[:, :, :], pre[:, :, :], ACT.Exp, scale=-1.0).then_inc(e_ready, 1)
                act.wait_ge(e_ready, n + 1)
                a.activation(pre[:, :, :], tz[:, :, :], ACT.Ln, bias=1.0).then_inc(ln_ready, 1)

            def base_out(f):
                if not isinstance(f, int) or f >= 1:
                    act.wait_ge(x1_done, f)
                for b in range(CB):
                    i = f * CB + b
                    last = a.activation(base[:, b, :], x_all[:, at(i, 1), :].rearrange("p o d -> p (o d)"), ACT.Identity,
                                        scale=scale_b[:, at(i, 1)], bias=shift_b[:, at(i, 1)])
                last.then_inc(base_ready, 1)

            def exp_tile(f, k):
                gr, j = divmod(k, J)
                if gr % Q == 0 and j == 0:
                    act.wait_ge(drep_landed[gr // Q], 16 * S * Q * f + 16 * S * Q)
                if not isinstance(f, int) or K * f + k >= DA_RING:
                    act.wait_ge(scan_done, K * f + k - DA_RING + 1)
                a.activation(da[:, k % DA_RING, :], delta_rep[:, gr, :], ACT.Exp,
                             scale=a_rep[:, gr, j:j + 1]).then_inc(exp_done, 1)

            norm_out(0)
            tanh_u(0)
            tanh_z(0)
            bc_out(0)
            softplus_parts(0)
            act.wait_ge(arep_ready, 1)

            def body(f, prepare, finish):
                for k in range(K):
                    exp_tile(f, k)
                    if prepare and k == 3:
                        norm_out(f + 1)
                    if prepare and k == 7:
                        tanh_u(f + 1)
                        tanh_z(f + 1)
                    if prepare and k == 11:
                        bc_out(f + 1)
                    if finish and k == 13:
                        base_out(f - 1)
                    if prepare and k == 16:
                        softplus_parts(f + 1)
            walk(act, body)
            base_out(CHUNKS - 1)

        @block.tensor
        def _(pe):
            t = nc.tensor

            def transpose_x(n):
                pe.wait_ge(xh_ready, n + 1)
                if not isinstance(n, int) or n >= 1:
                    pe.wait_ge(dact_done, 2 * n)
                for b in range(CB):
                    last = t.transpose(pa[0][:, P * b:P * b + P], xh[:, b, :], ident[:, :])
                last.then_inc(tr_done, 1)

            def project_u(n):
                pe.wait_ge(xn_ready, n + 1)
                for half in range(HALVES):
                    for k in range(TAPS):
                        last = t.matmul(pa[1 - half][:, :], w_tap[:, k, P * half:P * half + P], xn_t[:, xn_cols(n, k)],
                                        start=(k == 0), stop=(k == TAPS - 1))
                    last.then_inc(umm_done, 1)

            def project_z(n):
                for half in range(HALVES):
                    pe.wait_ge(uact_done, 2 * n + half + 1)
                    t.matmul(pa[1 - half][:, :], win[:, DIN + P * half:DIN + P * half + P], xn_t[:, xn_cols(n, PAD)],
                             start=True, stop=True).then_inc(zmm_done, 1)

            def project_bc_dt(n):
                pe.wait_ge(u_ready, n + 1)
                pe.wait_ge(zg_done, 2 * n + 1)
                for half in range(HALVES):
                    last = t.matmul(pa[1][:, :], w_xproj[:, half, :],
                                    u[:, at(n % 2, 1), half, :].rearrange("p o t -> p (o t)"),
                                    start=(half == 0), stop=(half == HALVES - 1))
                last.then_inc(xpmm_done, 1)

            def project_delta(n):
                pe.wait_ge(bc_ready, n + 1)
                pe.wait_ge(zg_done, 2 * n + 2)
                if not isinstance(n, int) or n >= 2:
                    pe.wait_ge(x1_done, n - 1)
                for half in range(HALVES):
                    t.matmul(pa[1 - half][:, :], w_dt[:, P * half:P * half + P], bc[:, :],
                             start=True, stop=True).then_inc(dmm_done, 1)

            def spread_w(f, gr):
                half, q = divmod(gr, Q)
                if gr == 0:
                    pe.wait_ge(w_ready, f + 1)
                if not isinstance(f, int) or f >= 1 or gr >= 2:
                    pe.wait_ge(mul_done, K * f + J * gr - J)
                t.matmul(w_ps[gr % 2][:, :], spread[:, q, :], w[:, at(f % 2, 1), half, :].rearrange("p o t -> p (o t)"),
                         start=True, stop=True).then_inc(wrep_ready, 1)

            def sum_states(f, pair):
                half = pair // 2
                pe.wait_ge(hc_done, K * f + 8 * pair + 8)
                if pair % 2 == 0 and (not isinstance(f, int) or f >= 1):
                    pe.wait_ge(yv_done, 2 * f - 1 + half)
                for j in range(J):
                    for i in range(2):
                        q = 2 * (pair % 2) + i
                        k = J * (2 * pair + i) + j
                        last = t.matmul(y_ps[half][DG * q:DG * q + DG, :], gather[:, :], h[:, k % H_RING, :],
                                        start=(j == 0), stop=(j == J - 1))
                last.then_inc(nsum_done, 1)

            def project_out(f):
                pe.wait_ge(yg_done, 2 * f + 2)
                for b in range(CB):
                    for half in range(HALVES):
                        last = t.matmul(pa[0][:, P * b:P * b + P], yg[:, half, P * b:P * b + P], w_out[:, half, :],
                                        start=(half == 0), stop=(half == HALVES - 1))
                last.then_inc(op_done, 1)

            pe.wait_ge(consts_ready, 1)
            pe.wait_ge(wtap_ready, 1)
            pe.wait_ge(aneg_ready, 2)
            for gr in range(G):
                last = t.matmul(pa[1][:, N * gr:N * gr + N], spread[:, gr % Q, :], a_neg[:, gr // Q, :], start=True, stop=True)
            last.then_inc(arep_mm, 1)
            pe.wait_ge(arep_ready, 1)
            transpose_x(0)
            project_u(0)
            project_z(0)
            project_bc_dt(0)
            project_delta(0)
            spread_w(0, 0)

            def body(f, prepare, finish):
                for gr in range(G):
                    if gr + 1 < G:
                        spread_w(f, gr + 1)
                    if finish and gr == 1:
                        sum_states(f - 1, 3)
                    if gr >= 3 and gr % 2:
                        sum_states(f, (gr - 3) // 2)
                    if prepare and gr == 0:
                        transpose_x(f + 1)
                    if prepare and gr == 1:
                        project_u(f + 1)
                        project_z(f + 1)
                    if prepare and gr == 2:
                        project_bc_dt(f + 1)
                    if finish and gr == 3:
                        if prepare:
                            pe.wait_ge(zg_done, 2 * f + 4)
                        project_out(f - 1)
                    if prepare and gr == 3:
                        project_delta(f + 1)
                if prepare:
                    spread_w(f + 1, 0)
            walk(pe, body)
            sum_states(CHUNKS - 1, 3)
            project_out(CHUNKS - 1)


def expert_layer(nc, x_ext, centroids, gamma, beta, W1, b1, W2, b2, sorted_rows, out):
    F32, I32 = mybir.dt.float32, mybir.dt.int32
    U32 = mybir.dt.uint32
    E, F, D = W1.shape
    BLOCKS = x_ext.shape[1]
    T = BLOCKS * P
    EXT = x_ext.shape[2]
    MEAN, SCALE_N, SCALE_B, SHIFT_B, ALPHA, ROW = range(D, D + 6)
    MAX_TILES = (T + E * (P - 1)) // P
    FC = F // P
    CB = 512 // P
    CHUNKS = BLOCKS // CB
    UNUSED = 1 << 20
    IndexOn = bass.IndirectOffsetOnAxis

    with ExitStack() as ctx:
        def sb(name, shape, dt=F32):
            return ctx.enter_context(nc.sbuf_tensor(name, shape, dt))

        def sem(name):
            return ctx.enter_context(nc.semaphore(name))

        w1_in = sb("w1_in", [P, E, FC, D])
        w2_in = sb("w2_in", [P, E, F])
        w1_raw = sb("w1_raw", [P, E, F])
        w1_t = sb("w1_t", [P, E, F])
        w2_t = sb("w2_t", [P, E, FC, D])
        bias1 = sb("bias1", [P, E, F])
        bias2 = sb("bias2", [P, E, D])
        small_in = sb("small_in", [E, 3, D])
        small_t = sb("small_t", [P, 3, E])
        zero_rows = sb("zero_rows", [P, EXT])
        f_ident = sb("f_ident", [P, P])
        before = sb("before", [P, P])
        ones = sb("ones", [P, P])
        io_e = sb("io_e", [P, E], I32)
        io_b = sb("io_b", [P, BLOCKS], I32)
        io_j = sb("io_j", [P, MAX_TILES], I32)
        e_of = sb("e_of", [P, E])
        rows_of = sb("rows_of", [P, BLOCKS])
        tile_of = sb("tile_of", [P, MAX_TILES])
        f_stats = sb("f_stats", [P, BLOCKS, 6])
        f_mv = sb("f_mv", [P, BLOCKS, 2])
        f_var = sb("f_var", [P, BLOCKS])
        f_var2 = sb("f_var2", [P, BLOCKS])
        f_half = sb("f_half", [P, BLOCKS])
        f_rstd = sb("f_rstd", [P, BLOCKS])
        f_rstd2 = sb("f_rstd2", [P, BLOCKS])
        feats = sb("feats", [P, BLOCKS, D])
        feats_t = sb("feats_t", [P, 2, CB * P])
        score = sb("score", [P, BLOCKS, E])
        best = sb("best", [P, BLOCKS])
        less = sb("less", [P, BLOCKS, E])
        first = sb("first", [P, BLOCKS])
        onehot = sb("onehot", [P, BLOCKS, E])
        neg_exp = sb("neg_exp", [P, BLOCKS])
        block_count = sb("block_count", [P, E, BLOCKS])
        upto = sb("upto", [P, E, BLOCKS])
        more = sb("more", [P, E, BLOCKS])
        tiles = sb("tiles", [P, E])
        tiles_upto = sb("tiles_upto", [P, E])
        start = sb("start", [P, E])
        offset = sb("offset", [P, E, BLOCKS])
        place = sb("place", [P, BLOCKS, E])
        slot_f = sb("slot_f", [P, BLOCKS])
        slot_i = sb("slot_i", [P, BLOCKS], U32)
        passed = sb("passed", [P, MAX_TILES, E])
        expert_f = sb("expert_f", [P, MAX_TILES])
        expert_i = sb("expert_i", [P, MAX_TILES], I32)
        rows = sb("rows", [P, MAX_TILES, EXT])
        xhat = sb("xhat", [P, 2, D])
        xhat_t = sb("xhat_t", [P, 2, P])
        hidden = sb("hidden", [P, 2, F])
        hidden_t = sb("hidden_t", [P, 2, F])
        base2 = sb("base2", [P, 2, D])
        y2 = sb("y2", [P, 2, D])
        done_rows = sb("done_rows", [P, MAX_TILES, D])
        bk = [ctx.enter_context(nc.psum_tensor(f"f_bank{i}", [P, 512], F32)) for i in range(8)]

        w1_landed = sem("f_w1_landed")
        w2_landed = sem("f_w2_landed")
        bias_landed = sem("f_bias_landed")
        small_landed = sem("f_small_landed")
        zero_ready = sem("f_zero_ready")
        zero_landed = sem("f_zero_landed")
        setup_done = sem("f_setup_done")
        consts_done = sem("f_consts_done")
        smallt_mm = sem("f_smallt_mm")
        smallt_ready = sem("f_smallt_ready")
        wtr_done = sem("f_wtr_done")
        wev_done = sem("f_wev_done")
        fst_done = sem("f_fst_done")
        fmv_done = sem("f_fmv_done")
        fvar_done = sem("f_fvar_done")
        frstd_done = sem("f_frstd_done")
        fv1 = sem("f_fv1")
        fvar2_done = sem("f_fvar2_done")
        frstd2_done = sem("f_frstd2_done")
        fscale_done = sem("f_fscale_done")
        fsn_done = sem("f_fsn_done")
        feats_ready = sem("f_feats_ready")
        ftr_done = sem("f_ftr_done")
        ftev_done = sem("f_ftev_done")
        score_done = sem("f_score_done")
        route = sem("f_route")
        onehot_ready = sem("f_onehot_ready")
        prefix_done = sem("f_prefix_done")
        slot_ready = sem("f_slot_ready")
        expert_ready = sem("f_expert_ready")
        ext_ready = sem("f_ext_ready")
        negexp_done = sem("f_negexp_done")
        bias_mm = sem("f_bias_mm")
        bias_ready = sem("f_bias_ready")
        scattered = sem("f_scattered")
        rows_landed = sem("f_rows_landed")
        xhat_ready = sem("f_xhat_ready")
        xt_done = sem("f_xt_done")
        xtev_done = sem("f_xtev_done")
        mm1_done = sem("f_mm1_done")
        hid_ready = sem("f_hid_ready")
        ht_done = sem("f_ht_done")
        relu_done = sem("f_relu_done")
        mm2_done = sem("f_mm2_done")
        base2_ready = sem("f_base2_ready")
        y2_ready = sem("f_y2_ready")
        done_ready = sem("f_done_ready")
        out_written = sem("f_out_written")

        block = ctx.enter_context(nc.Block())
        N_T = MAX_TILES

        def walk_tiles(eng, step):
            step(0, 0, behind=False)
            step(1, 1)
            step(2, 0)
            pairs = (N_T - 2) // 2
            with eng.Fori(1, pairs) as k:
                step(2 * k + 1, 1)
                step(2 * k + 2, 0)
            for i in range(2 * pairs + 1, N_T):
                step(i, i % 2, ahead=i + 1 < N_T)

        @block.sync
        def _(sp):
            sp.dma_start(w1_in[:, :, :, :], W1.rearrange("e (c p) d -> p e c d", p=P)).then_inc(w1_landed, 16)
            sp.dma_start(w2_in[:, :, :], W2.rearrange("e d f -> d e f")).then_inc(w2_landed, 16)
            sp.dma_start(bias1[:, :, :].rearrange("p e f -> p (e f)"),
                         b1.rearrange("(o e) f -> o (e f)", o=1).broadcast_to([P, E * F])).then_inc(bias_landed, 16)
            sp.dma_start(bias2[:, :, :].rearrange("p e d -> p (e d)"),
                         b2.rearrange("(o e) d -> o (e d)", o=1).broadcast_to([P, E * D])).then_inc(bias_landed, 16)
            sp.wait_ge(zero_ready, 1)
            for i in range(MAX_TILES):
                sp.dma_start(sorted_rows[P * i:P * i + P, :], zero_rows[:, :]).then_inc(zero_landed, 16)
            sp.wait_ge(scattered, 16 * BLOCKS)
            for i in range(0, MAX_TILES, 13):
                n = min(13, MAX_TILES - i)
                sp.dma_start(rows[:, i:i + n, :], sorted_rows[P * i:P * (i + n), :].rearrange("(j p) d -> p j d", p=P))\
                  .then_inc(rows_landed, 16)
            sp.wait_ge(out_written, 16 * N_T)

        @block.gpsimd
        def _(pool):
            g = nc.gpsimd
            g.memset(zero_rows[:, :], 0.0).then_inc(setup_done, 1)
            g.memset(f_half[:, :], -0.5)
            g.memset(f_ident[:, :], 0.0)
            g.memset(before[:, :], 1.0)
            g.memset(ones[:, :], 1.0)
            g.memset(x_ext[:, :, ROW + 1:], 0.0)
            g.iota(io_e[:, :], [[1, E]], base=0, channel_multiplier=0)
            g.iota(io_b[:, :], [[P, BLOCKS]], base=0, channel_multiplier=0)
            g.iota(io_j[:, :], [[1, MAX_TILES]], base=0, channel_multiplier=0)
            g.iota(x_ext[:, :, ROW].bitcast(I32), [[P, BLOCKS]], base=0, channel_multiplier=1).then_inc(setup_done, 1)
            pool.wait_ge(setup_done, 2)
            g.memset(zero_rows[:, ROW:ROW + 1].bitcast(I32), UNUSED).then_inc(zero_ready, 1)
            g.affine_select(out=f_ident[:, :], in_=f_ident[:, :], compare_op=ALU.not_equal, fill=1.0, base=0,
                            pattern=[[-1, P]], channel_multiplier=1)
            g.affine_select(out=before[:, :], in_=before[:, :], compare_op=ALU.is_gt, fill=0.0, base=0,
                            pattern=[[1, P]], channel_multiplier=-1).then_inc(consts_done, 1)
            pool.wait_ge(fvar_done, 1)
            g.tensor_tensor(f_rstd[:, :], f_var[:, :], f_half[:, :], ALU.pow).then_inc(frstd_done, 1)
            pool.wait_ge(fvar2_done, 1)
            g.tensor_tensor(f_rstd2[:, :], f_var2[:, :], f_half[:, :], ALU.pow).then_inc(frstd2_done, 1)
            pool.wait_ge(slot_ready, 1)
            pool.wait_ge(ext_ready, 1)
            pool.wait_ge(fsn_done, 1)
            pool.wait_ge(fscale_done, 2)
            pool.wait_ge(zero_landed, 16 * MAX_TILES)
            for i in range(BLOCKS):
                g.indirect_dma_start(out=sorted_rows, out_offset=IndexOn(slot_i[:, i:i + 1], 0),
                                     in_=x_ext[:, i, :], in_offset=None).then_inc(scattered, 16)
            for i in range(N_T):
                pool.wait_ge(done_ready, i + 1)
                if i % 13 == 0:
                    pool.wait_ge(rows_landed, 48)
                g.indirect_dma_start(out=out, out_offset=IndexOn(rows[:, i, ROW:ROW + 1].bitcast(U32), 0),
                                     in_=done_rows[:, i, :], in_offset=None, bounds_check=T - 1,
                                     oob_is_err=False).then_inc(out_written, 16)

        def e_at(reg):
            return bass.ds(reg, 1)

        @block.vector
        def _(dve):
            v = nc.vector
            for i in range(BLOCKS):
                last = v.bn_stats(f_stats[:, i, :], x_ext[:, i, 0:D])
            last.then_inc(fst_done, 1)
            dve.wait_ge(fst_done, 1)
            for i in range(BLOCKS):
                last = v.bn_aggr(f_mv[:, i, :], f_stats[:, i, :])
            last.then_inc(fmv_done, 1)
            dve.wait_ge(fmv_done, 1)
            v.tensor_scalar(f_var[:, :], f_mv[:, :, 1], EPS, None, ALU.add).then_inc(fvar_done, 1)
            v.tensor_copy(x_ext[:, :, MEAN], f_mv[:, :, 0])
            dve.wait_ge(frstd_done, 1)
            v.tensor_tensor(f_var2[:, :], f_mv[:, :, 1], f_rstd[:, :], ALU.mult).then_inc(fv1, 1)
            dve.wait_ge(fv1, 1)
            v.tensor_tensor(f_var2[:, :], f_var2[:, :], f_rstd[:, :], ALU.mult).then_inc(fv1, 1)
            dve.wait_ge(fv1, 2)
            v.tensor_scalar(f_var2[:, :], f_var2[:, :], EPS, None, ALU.add).then_inc(fvar2_done, 1)
            v.tensor_scalar(x_ext[:, :, SCALE_B], f_rstd[:, :], 1.0, None, ALU.add).then_inc(fscale_done, 1)
            v.scalar_tensor_tensor(out=x_ext[:, :, SHIFT_B], in0=f_mv[:, :, 0], scalar=-1.0, in1=f_rstd[:, :],
                                   op0=ALU.mult, op1=ALU.mult).then_inc(fscale_done, 1)
            for i in range(BLOCKS):
                last = v.tensor_scalar(feats[:, i, :], x_ext[:, i, 0:D], f_mv[:, i, 0:1], f_rstd[:, i:i + 1],
                                       ALU.subtract, ALU.mult)
                if i % CB == CB - 1:
                    last.then_inc(feats_ready, 1)
            dve.wait_ge(frstd2_done, 1)
            v.tensor_tensor(x_ext[:, :, SCALE_N], f_rstd[:, :], f_rstd2[:, :], ALU.mult).then_inc(fsn_done, 1)
            dve.wait_ge(setup_done, 2)
            v.tensor_copy(e_of[:, :], io_e[:, :])
            v.tensor_copy(rows_of[:, :], io_b[:, :])
            v.tensor_copy(tile_of[:, :], io_j[:, :]).then_inc(route, 1)

            steps = [1]

            def then(ins):
                steps[0] += 1
                ins.then_inc(route, 1)
                dve.wait_ge(route, steps[0])

            def over_blocks(ap):
                return ap.unsqueeze(1).broadcast_to([P, BLOCKS, E])

            def over_experts(ap, n):
                return ap.unsqueeze(2).broadcast_to([P, n, E])

            dve.wait_ge(score_done, CHUNKS)
            dve.wait_ge(route, 1)
            then(v.tensor_copy(score[:, :, :].rearrange("p b e -> p (b e)"), bk[6][:, 0:BLOCKS * E]))
            then(v.tensor_reduce(best[:, :], score[:, :, :], AX.X, ALU.max))
            then(v.tensor_tensor(less[:, :, :], score[:, :, :], over_experts(best[:, :], BLOCKS), ALU.is_lt))
            then(v.scalar_tensor_tensor(out=less[:, :, :], in0=less[:, :, :], scalar=float(E), in1=over_blocks(e_of[:, :]),
                                        op0=ALU.mult, op1=ALU.add))
            then(v.tensor_reduce(first[:, :], less[:, :, :], AX.X, ALU.min))
            v.tensor_tensor(onehot[:, :, :], over_blocks(e_of[:, :]), over_experts(first[:, :], BLOCKS),
                            ALU.is_equal).then_inc(onehot_ready, 1)
            dve.wait_ge(prefix_done, 2)
            then(v.tensor_copy(block_count[:, :, :], bk[5][:, 0:BLOCKS * E].rearrange("p (b e) -> p e b", e=E)))
            for e in range(E):
                last = v.tensor_tensor_scan(upto[:, e, :], ones[:, 0:BLOCKS], block_count[:, e, :], 0.0, ALU.mult, ALU.add)
            then(last)
            then(v.tensor_tensor(more[:, :, :], upto[:, :, BLOCKS - 1:BLOCKS].broadcast_to([P, E, BLOCKS]),
                                 rows_of[:, :].unsqueeze(1).broadcast_to([P, E, BLOCKS]), ALU.is_gt))
            then(v.tensor_reduce(tiles[:, :], more[:, :, :], AX.X, ALU.add))
            then(v.tensor_tensor_scan(tiles_upto[:, :], ones[:, 0:E], tiles[:, :], 0.0, ALU.mult, ALU.add))
            then(v.tensor_tensor(start[:, :], tiles_upto[:, :], tiles[:, :], ALU.subtract))
            then(v.tensor_scalar(start[:, :], start[:, :], float(P), None, ALU.mult))
            then(v.tensor_tensor(offset[:, :, :], upto[:, :, :], block_count[:, :, :], ALU.subtract))
            then(v.tensor_tensor(offset[:, :, :], offset[:, :, :], start[:, :].unsqueeze(2).broadcast_to([P, E, BLOCKS]), ALU.add))
            then(v.tensor_tensor(place[:, :, :], bk[4][:, 0:BLOCKS * E].rearrange("p (b e) -> p b e", e=E),
                                 offset[:, :, :].rearrange("p e b -> p b e"), ALU.add))
            then(v.tensor_tensor(place[:, :, :], place[:, :, :], onehot[:, :, :], ALU.mult))
            then(v.tensor_reduce(slot_f[:, :], place[:, :, :], AX.X, ALU.add))
            v.tensor_copy(slot_i[:, :], slot_f[:, :]).then_inc(slot_ready, 1)
            dve.wait_ge(negexp_done, 1)
            then(v.tensor_scalar(neg_exp[:, :], neg_exp[:, :], 1.0, None, ALU.add))
            v.reciprocal(x_ext[:, :, ALPHA], neg_exp[:, :]).then_inc(ext_ready, 1)
            then(v.tensor_tensor(passed[:, :, :], tiles_upto[:, :].unsqueeze(1).broadcast_to([P, MAX_TILES, E]),
                                 over_experts(tile_of[:, :], MAX_TILES), ALU.is_le))
            then(v.tensor_reduce(expert_f[:, :], passed[:, :, :], AX.X, ALU.add))
            then(v.tensor_scalar(expert_f[:, :], expert_f[:, :], float(E - 1), None, ALU.min))
            v.tensor_copy(expert_i[:, :], expert_f[:, :]).then_inc(expert_ready, 1)
            dve.wait_ge(bias_landed, 32)
            for e in range(E):
                dve.wait_ge(bias_mm, e + 1)
                v.tensor_tensor(bias1[:, e, :], bk[2 + e % 2][:, :], bias1[:, e, :], ALU.add).then_inc(bias_ready, 1)
            dve.wait_ge(bias_ready, E)
            dve.wait_ge(expert_ready, 1)

            def normalise(i, r):
                if not isinstance(i, int) or i >= 2:
                    dve.wait_ge(xt_done, i - 1)
                v.tensor_scalar(xhat[:, r, :], rows[:, e_at(i), 0:D].rearrange("p o d -> p (o d)"),
                                rows[:, e_at(i), MEAN], rows[:, e_at(i), SCALE_N], ALU.subtract, ALU.mult)\
                 .then_inc(xhat_ready, 1)

            def add_bias(i, r):
                e = dve.value_load(expert_i[0:1, e_at(i)], min_val=0, max_val=E - 1)
                dve.wait_ge(mm1_done, i + 1)
                if not isinstance(i, int) or i >= 2:
                    dve.wait_ge(ht_done, i - 1)
                v.tensor_tensor(hidden[:, r, :], bk[2 + r][:, :], bias1[:, e_at(e), :].rearrange("p o f -> p (o f)"),
                                ALU.add).then_inc(hid_ready, 1)

            def finish(i, r):
                e = dve.value_load(expert_i[0:1, e_at(i)], min_val=0, max_val=E - 1)
                dve.wait_ge(mm2_done, i + 1)
                v.tensor_tensor(y2[:, r, :], bk[6 + r][:, 0:D], bias2[:, e_at(e), :].rearrange("p o f -> p (o f)"),
                                ALU.add).then_inc(y2_ready, 1)
                dve.wait_ge(y2_ready, i + 1)
                dve.wait_ge(base2_ready, i + 1)
                v.scalar_tensor_tensor(out=done_rows[:, e_at(i), :].rearrange("p o f -> p (o f)"), in0=y2[:, r, :],
                                       scalar=rows[:, e_at(i), ALPHA], in1=base2[:, r, :],
                                       op0=ALU.mult, op1=ALU.add).then_inc(done_ready, 1)

            dve.wait_ge(rows_landed, 48)

            def step(i, r, ahead=True, behind=True):
                if ahead:
                    normalise(i + 1, 1 - r)
                add_bias(i, r)
                if behind:
                    finish(i - 1, 1 - r)
            normalise(0, 0)
            walk_tiles(dve, step)
            finish(N_T - 1, (N_T - 1) % 2)

        @block.scalar
        def _(act):
            a = nc.scalar
            for i, src in enumerate((centroids, gamma, beta)):
                act.dma_start(small_in[:, i, :], src).then_inc(small_landed, 16)
            act.wait_ge(smallt_mm, 1)
            a.activation(small_t[:, :, :].rearrange("p i e -> p (i e)"), bk[7][:, 0:3 * E], ACT.Identity)\
             .then_inc(smallt_ready, 1)
            act.wait_ge(smallt_ready, 1)
            for n in range(2 * E):
                e = n // 2
                act.wait_ge(wtr_done, n + 1)
                if n % 2 == 0:
                    a.activation(w1_raw[:, e, :], bk[0][:, :], ACT.Identity)
                    a.activation(w1_t[:, e, :], bk[0][:, :], ACT.Identity, scale=small_t[:, 1, e:e + 1]).then_inc(wev_done, 1)
                else:
                    a.activation(w2_t[:, e, :, :].rearrange("p c d -> p (c d)"), bk[1][:, :], ACT.Identity).then_inc(wev_done, 1)
            for c in range(CHUNKS):
                act.wait_ge(ftr_done, c + 1)
                if c >= 2:
                    act.wait_ge(score_done, c - 1)
                a.activation(feats_t[:, c % 2, :], bk[4 + c % 2][:, :], ACT.Identity).then_inc(ftev_done, 1)
            act.wait_ge(route, 3)
            a.activation(neg_exp[:, :], best[:, :], ACT.Exp, scale=-1.0).then_inc(negexp_done, 1)
            act.wait_ge(rows_landed, 48)

            def to_columns(i, r):
                act.wait_ge(xt_done, i + 1)
                if not isinstance(i, int) or i >= 2:
                    act.wait_ge(mm1_done, i - 1)
                a.activation(xhat_t[:, r, :], bk[r][:, 0:P], ACT.Identity).then_inc(xtev_done, 1)

            def residual(i, r):
                if not isinstance(i, int) or i >= 2:
                    act.wait_ge(done_ready, i - 1)
                a.activation(base2[:, r, :], rows[:, e_at(i), 0:D].rearrange("p o d -> p (o d)"), ACT.Identity,
                             scale=rows[:, e_at(i), SCALE_B], bias=rows[:, e_at(i), SHIFT_B]).then_inc(base2_ready, 1)

            def relu(i, r):
                act.wait_ge(ht_done, i + 1)
                if not isinstance(i, int) or i >= 2:
                    act.wait_ge(mm2_done, i - 1)
                a.activation(hidden_t[:, r, :], bk[4 + r][:, :], ACT.Relu).then_inc(relu_done, 1)

            def step(i, r, ahead=True, behind=True):
                if ahead:
                    to_columns(i + 1, 1 - r)
                residual(i, r)
                relu(i, r)
            to_columns(0, 0)
            walk_tiles(act, step)

        @block.tensor
        def _(pe):
            t = nc.tensor
            pe.wait_ge(consts_done, 1)
            pe.wait_ge(small_landed, 48)
            for i in range(3):
                last = t.transpose(bk[7][:, E * i:E * i + E], small_in[:, i, :], f_ident[0:E, 0:E])
            last.then_inc(smallt_mm, 1)
            for n in range(2 * E):
                e = n // 2
                if n >= 2:
                    pe.wait_ge(wev_done, n - 1)
                if n == 0:
                    pe.wait_ge(w1_landed, 16)
                    pe.wait_ge(w2_landed, 16)
                for c in range(FC):
                    src = w1_in[:, e, c, :] if n % 2 == 0 else w2_in[:, e, P * c:P * c + P]
                    last = t.transpose(bk[n % 2][:, P * c:P * c + P], src, f_ident[:, :])
                last.then_inc(wtr_done, 1)

            def score_blocks(c):
                pe.wait_ge(ftev_done, c + 1)
                if c == 0:
                    pe.wait_ge(smallt_ready, 1)
                for b in range(CB):
                    i = CB * c + b
                    last = t.matmul(bk[6][:, E * i:E * i + E], feats_t[:, c % 2, P * b:P * b + P], small_t[:, 0, :],
                                    start=True, stop=True)
                last.then_inc(score_done, 1)
            for c in range(CHUNKS):
                pe.wait_ge(feats_ready, c + 1)
                if c >= 2:
                    pe.wait_ge(ftev_done, c - 1)
                for b in range(CB):
                    last = t.transpose(bk[4 + c % 2][:, P * b:P * b + P], feats[:, CB * c + b, :], f_ident[:, :])
                last.then_inc(ftr_done, 1)
                if c:
                    score_blocks(c - 1)
            score_blocks(CHUNKS - 1)
            pe.wait_ge(onehot_ready, 1)
            flat = onehot[:, :, :].rearrange("p b e -> p (b e)")
            t.matmul(bk[4][:, 0:BLOCKS * E], before[:, :], flat, start=True, stop=True).then_inc(prefix_done, 1)
            t.matmul(bk[5][:, 0:BLOCKS * E], ones[:, :], flat, start=True, stop=True).then_inc(prefix_done, 1)
            pe.wait_ge(wev_done, 2 * E)
            for e in range(E):
                if e >= 2:
                    pe.wait_ge(bias_ready, e - 1)
                t.matmul(bk[2 + e % 2][:, :], small_t[:, 2, e:e + 1].broadcast_to([P, P]), w1_raw[:, e, :],
                         start=True, stop=True).then_inc(bias_mm, 1)
            pe.wait_ge(bias_ready, E)
            pe.wait_ge(expert_ready, 1)

            def rows_t(i, r):
                pe.wait_ge(xhat_ready, i + 1)
                if not isinstance(i, int) or i >= 2:
                    pe.wait_ge(xtev_done, i - 1)
                t.transpose(bk[r][:, 0:P], xhat[:, r, :], f_ident[:, :]).then_inc(xt_done, 1)

            def up(i, r):
                e = pe.value_load(expert_i[0:1, e_at(i)], min_val=0, max_val=E - 1)
                pe.wait_ge(xtev_done, i + 1)
                if not isinstance(i, int) or i >= 2:
                    pe.wait_ge(hid_ready, i - 1)
                t.matmul(bk[2 + r][:, :], xhat_t[:, r, :], w1_t[:, e_at(e), :].rearrange("p o f -> p (o f)"),
                         start=True, stop=True).then_inc(mm1_done, 1)

            def hidden_columns(i, r):
                pe.wait_ge(hid_ready, i + 1)
                if not isinstance(i, int) or i >= 2:
                    pe.wait_ge(relu_done, i - 1)
                for c in range(FC):
                    last = t.transpose(bk[4 + r][:, P * c:P * c + P], hidden[:, r, P * c:P * c + P], f_ident[:, :])
                last.then_inc(ht_done, 1)

            def down(i, r):
                e = pe.value_load(expert_i[0:1, e_at(i)], min_val=0, max_val=E - 1)
                pe.wait_ge(relu_done, i + 1)
                if not isinstance(i, int) or i >= 2:
                    pe.wait_ge(y2_ready, i - 1)
                for c in range(FC):
                    last = t.matmul(bk[6 + r][:, 0:D], hidden_t[:, r, P * c:P * c + P],
                                    w2_t[:, e_at(e), c, :].rearrange("p o f -> p (o f)"), start=(c == 0), stop=(c == FC - 1))
                last.then_inc(mm2_done, 1)

            def step(i, r, ahead=True, behind=True):
                up(i, r)
                if ahead:
                    rows_t(i + 1, 1 - r)
                if behind:
                    down(i - 1, 1 - r)
                hidden_columns(i, r)
            rows_t(0, 0)
            walk_tiles(pe, step)
            down(N_T - 1, (N_T - 1) % 2)


def program(nc, mamba_inputs, ffn_inputs, out):
    x = mamba_inputs[0]
    T, DM = x.shape[0] * x.shape[1], x.shape[2]
    E = ffn_inputs[0].shape[0]
    EXT = DM + 8
    tiles = (T + E * (P - 1)) // P
    bc_scratch = nc.dram_tensor("bc_scratch", (32, 512), F32, kind="Internal").ap()
    sorted_rows = nc.dram_tensor("sorted_rows", (tiles * P, EXT), F32, kind="Internal").ap()
    with nc.sbuf_tensor("x_ext", [P, T // P, EXT], F32) as x_ext:
        mamba_layer(nc, *mamba_inputs, bc_scratch, x_ext[:, :, 0:DM], None)
        expert_layer(nc, x_ext, *ffn_inputs, sorted_rows, out)


_MAMBA = ['x', 'in_proj_w', 'conv_w', 'conv_b', 'x_proj_w', 'dt_proj_w', 'dt_proj_b', 'A_log', 'D', 'out_proj_w',
          'ln_g', 'ln_b']
_FFN = ['centroids', 'gamma', 'beta', 'W1', 'b1', 'W2', 'b2']


def kernel(**inputs):
    import numpy as _np
    import concourse.bacc as _bacc
    from concourse.bass_utils import run_bass_kernel_spmd as _run

    nc = _bacc.Bacc("TRN2", target_bir_lowering=False, num_devices=1)
    arrays = {}

    def declare(name):
        a = _np.ascontiguousarray(inputs[name])
        arrays["in_" + name] = a
        return nc.dram_tensor("in_" + name, a.shape, F32, kind="ExternalInput").ap()
    mamba_inputs = [declare("L0_attn_" + n) for n in _MAMBA]
    ffn_inputs = [declare("L0_ffn_" + n) for n in _FFN]
    shape = inputs["L0_attn_x"].shape
    out = nc.dram_tensor("out", (shape[0] * shape[1], shape[2]), F32, kind="ExternalOutput").ap()
    program(nc, mamba_inputs, ffn_inputs, out)
    r = _run(nc, [arrays], core_ids=[0])
    return r.results[0]["out"].reshape(shape)
```

```python
from contextlib import ExitStack

import concourse.bass as bass
from concourse import mybir

P = 128
F32 = mybir.dt.float32
ALU = mybir.AluOpType
ACT = mybir.ActivationFunctionType
AX = mybir.AxisListType
EPS = 1e-5


def mamba_layer(nc, x, in_proj_w, conv_w, conv_b, x_proj_w, dt_proj_w, dt_proj_b, A_log, D, out_proj_w,
                ln_g, ln_b, bc_scratch, x_all, x_mid):
    B, L, DM = x.shape
    DIN, N = A_log.shape
    R = x_proj_w.shape[1] - 2 * N
    TAPS = conv_w.shape[1]
    T = B * L
    BLOCKS = T // P
    C = 512
    CHUNKS = T // C
    SEQ_CHUNKS = L // C
    CB = C // P
    HALVES = DIN // P
    S, DG = 4, 32
    Q = P // DG
    G = HALVES * Q
    J = N // S
    K = G * J
    DA_RING, H_RING = 8, 16
    UZ = 3
    PAD = TAPS - 1
    EARLY = 2 * CB
    assert DM == P and N == S * J and K % H_RING == 0 and 2 * N + R <= P

    with ExitStack() as ctx:
        def sb(name, shape):
            return ctx.enter_context(nc.sbuf_tensor(name, shape, F32))

        def bank(name):
            return ctx.enter_context(nc.psum_tensor(name, [P, C], F32))

        def sem(name):
            return ctx.enter_context(nc.semaphore(name))

        win = sb("win", [P, 2 * DIN])
        w_tap = sb("w_tap", [P, TAPS, DIN])
        conv_b_half = sb("conv_b_half", [P, HALVES])
        w_xproj = sb("w_xproj", [P, HALVES, P])
        w_dt = sb("w_dt", [P, DIN])
        dt_bias = sb("dt_bias", [P, HALVES])
        a_log = sb("a_log", [P, HALVES, N])
        a_neg = sb("a_neg", [P, HALVES, N])
        a_rep = sb("a_rep", [P, G, J])
        d_skip = sb("d_skip", [P, HALVES])
        w_out = sb("w_out", [P, HALVES, DM])
        g_col = sb("g_col", [P, 1])
        b_col = sb("b_col", [P, 1])
        ident = sb("ident", [P, P])
        spread = sb("spread", [P, Q, P])
        gather = sb("gather", [P, DG])
        started = sb("started", [P, 1])
        stats = sb("stats", [P, BLOCKS, 6])
        mv = sb("mv", [P, BLOCKS, 2])
        var_eps = sb("var_eps", [P, BLOCKS])
        neg_half = sb("neg_half", [P, BLOCKS])
        rstd = sb("rstd", [P, BLOCKS])
        var2 = sb("var2", [P, BLOCKS])
        rstd2 = sb("rstd2", [P, BLOCKS])
        scale_n = sb("scale_n", [P, BLOCKS])
        scale_b = sb("scale_b", [P, BLOCKS])
        shift_b = sb("shift_b", [P, BLOCKS])
        xh = sb("xh", [P, CB, P])
        xn_t = sb("xn_t", [P, B * (PAD + L)])
        ln = sb("ln", [P, HALVES, C])
        relu = sb("relu", [P, HALVES, C])
        e = sb("e", [P, HALVES, C])
        u = sb("u", [P, UZ, HALVES, C])
        zg = sb("zg", [P, UZ, HALVES, C])
        w = sb("w", [P, 2, HALVES, C])
        delta = sb("delta", [P, HALVES, C])
        conv_rep = delta[:, :, :].rearrange("p h t -> p (h t)").rearrange("p (d k) -> p d k", k=TAPS)
        delta_rep = sb("delta_rep", [P, G, C])
        bc = sb("bc", [P, C])
        bc_rep = sb("bc_rep", [P, 2, 2 * J, C])
        da = sb("da", [P, DA_RING, C])
        h = sb("h", [P, H_RING, C])
        carry = sb("carry", [P, CHUNKS + B, K])
        yg = sb("yg", [P, HALVES, C])
        base = sb("base", [P, CB, P])

        w_ps = [bank("w_ps0"), bank("w_ps1")]
        dbu = [bank("dbu0"), bank("dbu1")]
        y_ps = [bank("y_ps0"), bank("y_ps1")]
        pa = [bank("pa0"), bank("pa1")]

        x_in = [sem(f"x_in{i}") for i in range(BLOCKS // 8)]
        weights_in = sem("weights_in")
        iota_done = sem("iota_done")
        zeroed = sem("zeroed")
        wtap_ready = sem("wtap_ready")
        aneg_ready = sem("aneg_ready")
        arep_mm = sem("arep_mm")
        arep_ready = sem("arep_ready")
        stats_done = sem("stats_done")
        aggr_done = sem("aggr_done")
        vareps_ready = sem("vareps_ready")
        rstd_ready = sem("rstd_ready")
        var2_ready = sem("var2_ready")
        rstd2_ready = sem("rstd2_ready")
        norm_ready = sem("norm_ready")
        halfbias_ready = sem("halfbias_ready")
        xh_ready = sem("xh_ready")
        tr_done = sem("tr_done")
        xn_ready = sem("xn_ready")
        umm_done = sem("umm_done")
        uact_done = sem("uact_done")
        u_ready = sem("u_ready")
        zmm_done = sem("zmm_done")
        zact_done = sem("zact_done")
        zg_done = sem("zg_done")
        xpmm_done = sem("xpmm_done")
        bc_ready = sem("bc_ready")
        scr_written = sem("scr_written")
        bcrep_landed = sem("bcrep_landed")
        dmm_done = sem("dmm_done")
        dact_done = sem("dact_done")
        e_ready = sem("e_ready")
        ln_ready = sem("ln_ready")
        g_ready = sem("g_ready")
        d1_done = sem("d1_done")
        d2_done = sem("d2_done")
        delta_ready = sem("delta_ready")
        w_ready = sem("w_ready")
        drep0_landed = sem("drep0_landed")
        drep1_landed = sem("drep1_landed")
        wrep_ready = sem("wrep_ready")
        exp_done = sem("exp_done")
        mul_done = sem("mul_done")
        scan_done = sem("scan_done")
        carry_saved = sem("carry_saved")
        hc_done = sem("hc_done")
        nsum_done = sem("nsum_done")
        yv_done = sem("yv_done")
        yg_done = sem("yg_done")
        op_done = sem("op_done")
        base_ready = sem("base_ready")
        x1_done = sem("x1_done")
        mid_out = sem("mid_out")
        ts_done = sem("ts_done")
        gather_step = sem("gather_step")
        consts_ready = sem("consts_ready")
        drep_landed = [drep0_landed, drep1_landed]
        WEIGHT_LOADS = 9 + 3 * HALVES

        def at(i, n):
            return bass.ds(i, n)

        def slot(f):
            return f + f // SEQ_CHUNKS

        def xn_cols(f, shift):
            return at(f * C + (f // SEQ_CHUNKS) * PAD + shift, C)

        def walk(eng, body):
            body(0, first=True, second=True, finish=False)
            with eng.Fori(1, CHUNKS - 2) as f:
                body(f, first=True, second=True, finish=True)
            body(CHUNKS - 2, first=False, second=True, finish=True)
            body(CHUNKS - 1, first=False, second=False, finish=True)

        block = ctx.enter_context(nc.Block())

        @block.sync
        def _(sp):
            x_v = x.rearrange("b (n p) d -> p (b n) d", p=P)
            for i in range(BLOCKS // 8):
                sp.dma_start(x_all[:, 8 * i:8 * i + 8, :], x_v[:, 8 * i:8 * i + 8, :]).then_inc(x_in[i], 16)
            sp.wait_ge(zeroed, 1)
            sp.dma_start(w_xproj[:, :, 0:2 * N], x_proj_w[:, R:].rearrange("(h p) n -> p h n", p=P)).then_inc(weights_in, 16)
            sp.dma_start(w_xproj[:, :, 2 * N:2 * N + R], x_proj_w[:, 0:R].rearrange("(h p) n -> p h n", p=P)).then_inc(weights_in, 16)
            sp.dma_start(w_dt[2 * N:2 * N + R, :], dt_proj_w).then_inc(weights_in, 16)

            def bc_replicate(n):
                sp.wait_ge(bc_ready, n + 1)
                if not isinstance(n, int) or n >= 1:
                    sp.wait_ge(bcrep_landed, 64 * n)
                sp.dma_start(bc_scratch, bc[0:2 * N, :]).then_inc(scr_written, 16)
                sp.wait_ge(scr_written, 16 * n + 16)
                if not isinstance(n, int) or n >= 2:
                    sp.wait_ge(consts_ready, 1)
                    sp.wait_ge(mul_done, K * n - K)
                    sp.wait_ge(hc_done, K * n - K)
                src = bc_scratch.rearrange("(j s) t -> s j t", s=S)
                for st in range(S):
                    dst = bc_rep[DG * st:DG * st + DG, at(n % 2, 1), :, :].rearrange("p o j t -> p (o j) t")
                    sp.dma_start(dst, src[st:st + 1, :, :].broadcast_to([DG, 2 * J, C])).then_inc(bcrep_landed, 16)

            def delta_replicate(n, half):
                sp.wait_ge(consts_ready, 1)
                if half == 0:
                    sp.wait_ge(delta_ready, n + 1)
                if not isinstance(n, int) or n >= 1:
                    sp.wait_ge(exp_done, K * n - K + (K // HALVES) * (half + 1))
                for st in range(S):
                    for q in range(Q):
                        sp.dma_start(delta_rep[DG * st:DG * st + DG, Q * half + q, :],
                                     delta[DG * q:DG * q + DG, half, :]).then_inc(drep_landed[half], 16)

            bc_replicate(0)
            delta_replicate(0, 0)
            delta_replicate(0, 1)

            def body(f, first, second, finish):
                if second:
                    sp.wait_ge(consts_ready, 1)
                    bc_replicate(f + 1)
                    delta_replicate(f + 1, 0)
                    delta_replicate(f + 1, 1)
            walk(sp, body)
            sp.wait_ge(x1_done, CHUNKS)
            if x_mid is not None:
                sp.dma_start(x_mid.rearrange("b (n p) d -> p (b n) d", p=P), x_all[:, :, :]).then_inc(mid_out, 16)
                sp.wait_ge(mid_out, 16)

        @block.gpsimd
        def _(pool):
            g = nc.gpsimd
            g.memset(w_xproj[:, :, :], 0.0)
            g.memset(w_dt[:, :], 0.0).then_inc(zeroed, 1)
            g.memset(neg_half[:, :], -0.5)
            g.memset(ident[:, :], 0.0)
            g.memset(spread[:, :, :], 0.0)
            g.memset(gather[:, :], 0.0)
            g.memset(carry[:, :, :], 0.0)
            for b in range(B):
                last = g.memset(xn_t[:, b * (PAD + L):b * (PAD + L) + PAD], 0.0)
            last.then_inc(iota_done, 1)
            pool.wait_ge(iota_done, 1)
            g.affine_select(out=ident[:, :], in_=ident[:, :], compare_op=ALU.not_equal, fill=1.0, base=0,
                            pattern=[[-1, P]], channel_multiplier=1)
            for q in range(Q):
                v = spread[:, q, :].rearrange("p (s d) -> p s d", s=S)
                g.affine_select(out=v, in_=v, compare_op=ALU.not_equal, fill=1.0, base=-DG * q,
                                pattern=[[0, S], [-1, DG]], channel_multiplier=1)
            for st in range(S):
                g.affine_select(out=gather[:, :], in_=gather[:, :], compare_op=ALU.not_equal, fill=1.0, base=-DG * st,
                                pattern=[[-1, DG]], channel_multiplier=1).then_inc(gather_step, 1)
                pool.wait_ge(gather_step, st + 1)
            g.memset(started[:, :], 0.0).then_inc(consts_ready, 1)
            def inverse_roots(part, lo, hi):
                pool.wait_ge(vareps_ready, part + 1)
                g.tensor_tensor(rstd[:, lo:hi], var_eps[:, lo:hi], neg_half[:, lo:hi], ALU.pow).then_inc(rstd_ready, 1)
                pool.wait_ge(var2_ready, part + 1)
                g.tensor_tensor(rstd2[:, lo:hi], var2[:, lo:hi], neg_half[:, lo:hi], ALU.pow).then_inc(rstd2_ready, 1)
            inverse_roots(0, 0, EARLY)
            pool.wait_ge(weights_in, 16 * WEIGHT_LOADS)
            for k in range(TAPS):
                last = g.tensor_tensor(w_tap[:, k, :], win[:, 0:DIN], conv_rep[:, :, k], ALU.mult)
            last.then_inc(wtap_ready, 1)
            inverse_roots(1, EARLY, BLOCKS)

            def softplus_sum(n):
                flat = delta[:, :, :]
                pool.wait_ge(g_ready, n + 1)
                pool.wait_ge(ln_ready, n + 1)
                g.tensor_tensor(flat, ln[:, :, :], flat, ALU.subtract).then_inc(d1_done, 1)
                pool.wait_ge(d1_done, n + 1)
                g.tensor_tensor(flat, flat, e[:, :, :], ALU.add).then_inc(d2_done, 1)
                pool.wait_ge(d2_done, n + 1)
                g.tensor_tensor(flat, flat, relu[:, :, :], ALU.add).then_inc(delta_ready, 1)

            softplus_sum(0)

            def body(f, first, second, finish):
                for gr in range(G):
                    if gr == 2 and second:
                        softplus_sum(f + 1)
                    pool.wait_ge(scan_done, K * f + J * gr + J)
                    at0 = (J * gr) % H_RING
                    g.tensor_copy(carry[:, at(slot(f) + 1, 1), J * gr:J * gr + J].rearrange("p o k -> p (o k)"),
                                  h[:, at0:at0 + J, C - 1]).then_inc(carry_saved, J)
                    pool.wait_ge(consts_ready, 1)
                    pool.wait_ge(carry_saved, K * f + J * gr + J)
                    if gr == 0:
                        pool.wait_ge(bcrep_landed, 64 * f + 64)
                    for j in range(J):
                        hk = h[:, at0 + j, :]
                        c_rep = bc_rep[:, at(f % 2, 1), J + j, :].rearrange("p o t -> p (o t)")
                        g.tensor_tensor(hk, hk, c_rep, ALU.mult).then_inc(hc_done, 1)
            walk(pool, body)

        @block.vector
        def _(dve):
            v = nc.vector
            def normalise(n):
                if not isinstance(n, int) or n >= 1:
                    dve.wait_ge(tr_done, n)
                for b in range(CB):
                    m = mv[:, at(n * CB + b, 1), 0]
                    sc = scale_n[:, at(n * CB + b, 1)]
                    last = v.tensor_scalar(xh[:, b, :], x_all[:, at(n * CB + b, 1), :].rearrange("p o d -> p (o d)"),
                                           m, sc, ALU.subtract, ALU.mult)
                last.then_inc(xh_ready, 1)

            def statistics(part, lo, hi):
                for i in range(lo, hi):
                    if i % 8 == 0:
                        dve.wait_ge(x_in[i // 8], 16)
                    last = v.bn_stats(stats[:, i, :], x_all[:, i, :])
                last.then_inc(stats_done, 1)
                dve.wait_ge(stats_done, part + 1)
                for i in range(lo, hi):
                    last = v.bn_aggr(mv[:, i, :], stats[:, i, :])
                last.then_inc(aggr_done, 1)
                dve.wait_ge(aggr_done, part + 1)
                v.tensor_scalar(var_eps[:, lo:hi], mv[:, lo:hi, 1], EPS, None, ALU.add).then_inc(vareps_ready, 1)
                dve.wait_ge(rstd_ready, part + 1)
                v.tensor_tensor(scale_n[:, lo:hi], mv[:, lo:hi, 1], rstd[:, lo:hi], ALU.mult).then_inc(ts_done, 1)
                dve.wait_ge(ts_done, 2 * part + 1)
                v.tensor_tensor(var2[:, lo:hi], scale_n[:, lo:hi], rstd[:, lo:hi], ALU.mult).then_inc(ts_done, 1)
                dve.wait_ge(ts_done, 2 * part + 2)
                v.tensor_scalar(var2[:, lo:hi], var2[:, lo:hi], EPS, None, ALU.add).then_inc(var2_ready, 1)
                v.tensor_scalar(scale_b[:, lo:hi], rstd[:, lo:hi], 1.0, None, ALU.add)
                v.scalar_tensor_tensor(out=shift_b[:, lo:hi], in0=mv[:, lo:hi, 0], scalar=-1.0, in1=rstd[:, lo:hi],
                                       op0=ALU.mult, op1=ALU.mult)
                dve.wait_ge(rstd2_ready, part + 1)
                v.tensor_tensor(scale_n[:, lo:hi], rstd[:, lo:hi], rstd2[:, lo:hi], ALU.mult).then_inc(norm_ready, 1)
                dve.wait_ge(norm_ready, part + 1)
            statistics(0, 0, EARLY)
            normalise(0)
            dve.wait_ge(weights_in, 16 * WEIGHT_LOADS)
            v.tensor_scalar(conv_b_half[:, :], conv_b_half[:, :], 0.5, None, ALU.mult).then_inc(halfbias_ready, 1)
            dve.wait_ge(aneg_ready, 1)
            v.tensor_scalar(a_neg[:, :, :], a_neg[:, :, :], -1.0, None, ALU.mult).then_inc(aneg_ready, 1)
            dve.wait_ge(arep_mm, 1)
            for gr in range(G):
                for st in range(S):
                    src = dbu[0][DG * st:DG * st + DG, N * gr:N * gr + N].rearrange("p (j s) -> p j s", s=S)
                    last = v.tensor_copy(a_rep[DG * st:DG * st + DG, gr, :], src[:, :, st])
            last.then_inc(arep_ready, 1)

            def chunk_copy(buf, n):
                return buf[:, at(n % UZ, 1), :, :].rearrange("p o h t -> p (o h t)")

            def silu_u(n):
                dve.wait_ge(uact_done, 2 * n + 2)
                v.scalar_tensor_tensor(out=chunk_copy(u, n), in0=chunk_copy(zg, n), scalar=1.0, in1=chunk_copy(u, n),
                                       op0=ALU.add, op1=ALU.mult).then_inc(u_ready, 1)

            def silu_z(n):
                for half in range(HALVES):
                    z = zg[:, at(n % UZ, 1), half, :].rearrange("p o t -> p (o t)")
                    dve.wait_ge(zact_done, 2 * n + half + 1)
                    v.scalar_tensor_tensor(out=z, in0=z, scalar=1.0, in1=pa[half][:, :],
                                           op0=ALU.add, op1=ALU.mult).then_inc(zg_done, 1)

            def log1p_grid(n):
                dve.wait_ge(e_ready, n + 1)
                if not isinstance(n, int) or n >= 1:
                    dve.wait_ge(drep0_landed, 16 * S * Q * n)
                    dve.wait_ge(drep1_landed, 16 * S * Q * n)
                    dve.wait_ge(w_ready, n)
                v.tensor_scalar(delta[:, :, :], e[:, :, :], 1.0, 1.0, ALU.add, ALU.subtract).then_inc(g_ready, 1)

            def delta_u(n):
                dve.wait_ge(delta_ready, n + 1)
                v.tensor_tensor(w[:, at(n % 2, 1), :, :].rearrange("p o h t -> p (o h) t"), delta[:, :, :],
                                u[:, at(n % UZ, 1), :, :].rearrange("p o h t -> p (o h) t"), ALU.mult).then_inc(w_ready, 1)

            def gate(f, half):
                dve.wait_ge(nsum_done, 4 * f + 2 * half + 2)
                if half == 0 and (not isinstance(f, int) or f >= 1):
                    dve.wait_ge(op_done, f)
                v.scalar_tensor_tensor(out=yg[:, half, :], in0=u[:, at(f % UZ, 1), half, :].rearrange("p o t -> p (o t)"),
                                       scalar=d_skip[:, half:half + 1], in1=y_ps[half][:, :],
                                       op0=ALU.mult, op1=ALU.add).then_inc(yv_done, 1)
                dve.wait_ge(yv_done, 2 * f + half + 1)
                v.scalar_tensor_tensor(out=yg[:, half, :], in0=yg[:, half, :], scalar=0.5,
                                       in1=zg[:, at(f % UZ, 1), half, :].rearrange("p o t -> p (o t)"),
                                       op0=ALU.mult, op1=ALU.mult).then_inc(yg_done, 1)

            def residual(f):
                dve.wait_ge(op_done, f + 1)
                dve.wait_ge(base_ready, f + 1)
                v.tensor_tensor(x_all[:, at(f * CB, CB), :], pa[1][:, :].rearrange("p (b d) -> p b d", b=CB),
                                base[:, :, :], ALU.add).then_inc(x1_done, 1)

            def mul(f, k):
                gr, j = divmod(k, J)
                if j == 0:
                    dve.wait_ge(wrep_ready, G * f + gr + 1)
                if k == 0:
                    dve.wait_ge(bcrep_landed, 64 * f + 64)
                if not isinstance(f, int) or K * f + k >= 2:
                    dve.wait_ge(scan_done, K * f + k - 1)
                v.tensor_tensor(dbu[k % 2][:, :], w_ps[gr % 2][:, :],
                                bc_rep[:, at(f % 2, 1), j, :].rearrange("p o t -> p (o t)"),
                                ALU.mult).then_inc(mul_done, 1)

            def scan(f, k):
                gr, j = divmod(k, J)
                dve.wait_ge(exp_done, K * f + k + 1)
                dve.wait_ge(mul_done, K * f + k + 1)
                if k % 8 == 0 and (not isinstance(f, int) or 4 * f + k // 8 >= 2):
                    dve.wait_ge(nsum_done, 4 * f + k // 8 - 1)
                if j == 0 and (not isinstance(f, int) or f >= 1):
                    dve.wait_ge(carry_saved, K * f - K + J * gr + J)
                v.tensor_tensor_scan(h[:, k % H_RING, :], da[:, k % DA_RING, :], dbu[k % 2][:, :],
                                     carry[:, at(slot(f), 1), k], ALU.mult, ALU.add).then_inc(scan_done, 1)

            silu_u(0)
            silu_z(0)
            normalise(1)
            statistics(1, EARLY, BLOCKS)
            log1p_grid(0)
            silu_u(1)
            silu_z(1)
            delta_u(0)

            def body(f, first, second, finish):
                for k in range(0, K, 2):
                    if first and k == 0:
                        normalise(f + 2)
                    if second and k == 8:
                        log1p_grid(f + 1)
                    if finish and k == 10:
                        gate(f - 1, 1)
                    if second and k == 22:
                        delta_u(f + 1)
                    if finish and k == 22:
                        residual(f - 1)
                    if first and k == 24:
                        silu_u(f + 2)
                    if k == 26:
                        gate(f, 0)
                    if first and k == 30:
                        silu_z(f + 2)
                    mul(f, k)
                    mul(f, k + 1)
                    scan(f, k)
                    scan(f, k + 1)
            walk(dve, body)
            gate(CHUNKS - 1, 1)
            residual(CHUNKS - 1)

        @block.scalar
        def _(act):
            a = nc.scalar
            act.dma_start(win[:, :], in_proj_w).then_inc(weights_in, 16)
            act.dma_start(delta[:, :, :].rearrange("p h t -> p (h t)"),
                          conv_w.rearrange("(o d) k -> o (d k)", o=1).broadcast_to([P, DIN * TAPS])).then_inc(weights_in, 16)
            for dst, src in ((conv_b_half, conv_b), (dt_bias, dt_proj_b), (d_skip, D)):
                for half in range(HALVES):
                    act.dma_start(dst[:, half:half + 1], src[P * half:P * half + P].rearrange("(p o) -> p o", o=1))\
                       .then_inc(weights_in, 16)
            act.dma_start(a_log[:, :, :], A_log.rearrange("(h p) n -> p h n", p=P)).then_inc(weights_in, 16)
            act.dma_start(w_out[:, :, :], out_proj_w.rearrange("(h p) n -> p h n", p=P)).then_inc(weights_in, 16)
            act.dma_start(g_col[:, :], ln_g.rearrange("(p o) -> p o", o=1)).then_inc(weights_in, 16)
            act.dma_start(b_col[:, :], ln_b.rearrange("(p o) -> p o", o=1)).then_inc(weights_in, 16)
            act.wait_ge(weights_in, 16 * WEIGHT_LOADS)
            a.activation(a_neg[:, :, :], a_log[:, :, :], ACT.Exp).then_inc(aneg_ready, 1)
            act.wait_ge(halfbias_ready, 1)

            def norm_out(n):
                act.wait_ge(tr_done, n + 1)
                a.activation(xn_t[:, xn_cols(n, PAD)], pa[0][:, :], ACT.Identity, scale=g_col[:, :],
                             bias=b_col[:, :]).then_inc(xn_ready, 1)

            def tanh_u(n, half):
                pre = u[:, at(n % UZ, 1), half, :].rearrange("p o t -> p (o t)")
                th = zg[:, at(n % UZ, 1), half, :].rearrange("p o t -> p (o t)")
                act.wait_ge(consts_ready, 1)
                act.wait_ge(umm_done, 2 * n + half + 1)
                if not isinstance(n, int) or n >= UZ:
                    act.wait_ge(yg_done, 2 * (n - UZ) + half + 1)
                a.activation(pre, pa[1 - half][:, :], ACT.Identity, scale=0.5, bias=conv_b_half[:, half:half + 1])
                a.activation(th, pa[1 - half][:, :], ACT.Tanh, scale=0.5,
                             bias=conv_b_half[:, half:half + 1]).then_inc(uact_done, 1)

            def tanh_z(n, half):
                act.wait_ge(consts_ready, 1)
                act.wait_ge(zmm_done, 2 * n + half + 1)
                act.wait_ge(u_ready, n + 1)
                a.activation(zg[:, at(n % UZ, 1), half, :].rearrange("p o t -> p (o t)"), pa[half][:, :],
                             ACT.Tanh, scale=0.5).then_inc(zact_done, 1)

            def bc_out(n):
                act.wait_ge(xpmm_done, n + 1)
                if not isinstance(n, int) or n >= 1:
                    act.wait_ge(scr_written, 16 * n)
                    act.wait_ge(dmm_done, 2 * n)
                a.activation(bc[:, :], pa[1][:, :], ACT.Identity).then_inc(bc_ready, 1)

            def softplus_parts(n):
                for half in range(HALVES):
                    act.wait_ge(dmm_done, 2 * n + half + 1)
                    if half == 0 and (not isinstance(n, int) or n >= 1):
                        act.wait_ge(delta_ready, n)
                    a.activation(ln[:, half, :], pa[1 - half][:, :], ACT.Abs, bias=dt_bias[:, half:half + 1])
                    a.activation(relu[:, half, :], pa[1 - half][:, :], ACT.Relu,
                                 bias=dt_bias[:, half:half + 1]).then_inc(dact_done, 1)
                act.wait_ge(dact_done, 2 * n + 2)
                a.activation(e[:, :, :], ln[:, :, :], ACT.Exp, scale=-1.0).then_inc(e_ready, 1)
                act.wait_ge(e_ready, n + 1)
                a.activation(ln[:, :, :], e[:, :, :], ACT.Ln, bias=1.0).then_inc(ln_ready, 1)

            def base_out(f):
                if not isinstance(f, int) or f >= 1:
                    act.wait_ge(x1_done, f)
                for b in range(CB):
                    i = f * CB + b
                    last = a.activation(base[:, b, :], x_all[:, at(i, 1), :].rearrange("p o d -> p (o d)"), ACT.Identity,
                                        scale=scale_b[:, at(i, 1)], bias=shift_b[:, at(i, 1)])
                last.then_inc(base_ready, 1)

            def exp_tile(f, k):
                gr, j = divmod(k, J)
                if gr % Q == 0 and j == 0:
                    act.wait_ge(drep_landed[gr // Q], 16 * S * Q * f + 16 * S * Q)
                if not isinstance(f, int) or K * f + k >= DA_RING:
                    act.wait_ge(scan_done, K * f + k - DA_RING + 1)
                a.activation(da[:, k % DA_RING, :], delta_rep[:, gr, :], ACT.Exp,
                             scale=a_rep[:, gr, j:j + 1]).then_inc(exp_done, 1)

            norm_out(0)
            tanh_u(0, 0)
            tanh_u(0, 1)
            tanh_z(0, 0)
            tanh_z(0, 1)
            bc_out(0)
            norm_out(1)
            softplus_parts(0)
            tanh_u(1, 0)
            tanh_u(1, 1)
            tanh_z(1, 0)
            tanh_z(1, 1)
            act.wait_ge(arep_ready, 1)

            def body(f, first, second, finish):
                for k in range(K):
                    exp_tile(f, k)
                    if second and k == 5:
                        bc_out(f + 1)
                    if first and k == 5:
                        norm_out(f + 2)
                    if second and k == 9:
                        softplus_parts(f + 1)
                    if finish and k == 13:
                        base_out(f - 1)
                    if first and k == 16:
                        tanh_u(f + 2, 0)
                    if first and k == 24:
                        tanh_u(f + 2, 1)
                    if first and k == 30:
                        tanh_z(f + 2, 0)
                        tanh_z(f + 2, 1)
            walk(act, body)
            base_out(CHUNKS - 1)

        @block.tensor
        def _(pe):
            t = nc.tensor

            def transpose_x(n):
                pe.wait_ge(xh_ready, n + 1)
                if not isinstance(n, int) or n >= 1:
                    pe.wait_ge(zg_done, 2 * n - 1)
                for b in range(CB):
                    last = t.transpose(pa[0][:, P * b:P * b + P], xh[:, b, :], ident[:, :])
                last.then_inc(tr_done, 1)

            def project_u(n, half):
                pe.wait_ge(xn_ready, n + 1)
                if not isinstance(n, int) or n >= 1:
                    pe.wait_ge(dact_done, 2 * n + half - 1)
                for k in range(TAPS):
                    last = t.matmul(pa[1 - half][:, :], w_tap[:, k, P * half:P * half + P], xn_t[:, xn_cols(n, k)],
                                    start=(k == 0), stop=(k == TAPS - 1))
                last.then_inc(umm_done, 1)

            def project_z(n):
                pe.wait_ge(uact_done, 2 * n + 2)
                for half in range(HALVES):
                    if half == 1 and (not isinstance(n, int) or n >= 3):
                        pe.wait_ge(x1_done, n - 2)
                    t.matmul(pa[half][:, :], win[:, DIN + P * half:DIN + P * half + P], xn_t[:, xn_cols(n, PAD)],
                             start=True, stop=True).then_inc(zmm_done, 1)

            def project_bc_dt(n):
                pe.wait_ge(u_ready, n + 1)
                pe.wait_ge(zg_done, 2 * n + 2)
                for half in range(HALVES):
                    last = t.matmul(pa[1][:, :], w_xproj[:, half, :],
                                    u[:, at(n % UZ, 1), half, :].rearrange("p o t -> p (o t)"),
                                    start=(half == 0), stop=(half == HALVES - 1))
                last.then_inc(xpmm_done, 1)

            def project_delta(n, first):
                pe.wait_ge(bc_ready, n + 1)
                for half in range(HALVES):
                    if half == 1 and first:
                        pe.wait_ge(xn_ready, n + 2)
                    t.matmul(pa[1 - half][:, :], w_dt[:, P * half:P * half + P], bc[:, :],
                             start=True, stop=True).then_inc(dmm_done, 1)

            def spread_w(f, gr):
                half, q = divmod(gr, Q)
                if gr == 0:
                    pe.wait_ge(w_ready, f + 1)
                if not isinstance(f, int) or f >= 1 or gr >= 2:
                    pe.wait_ge(mul_done, K * f + J * gr - J)
                t.matmul(w_ps[gr % 2][:, :], spread[:, q, :], w[:, at(f % 2, 1), half, :].rearrange("p o t -> p (o t)"),
                         start=True, stop=True).then_inc(wrep_ready, 1)

            def sum_states(f, pair):
                half = pair // 2
                pe.wait_ge(hc_done, K * f + 8 * pair + 8)
                if pair % 2 == 0 and (not isinstance(f, int) or f >= 1):
                    pe.wait_ge(yv_done, 2 * f - 1 + half)
                for j in range(J):
                    for i in range(2):
                        q = 2 * (pair % 2) + i
                        k = J * (2 * pair + i) + j
                        last = t.matmul(y_ps[half][DG * q:DG * q + DG, :], gather[:, :], h[:, k % H_RING, :],
                                        start=(j == 0), stop=(j == J - 1))
                last.then_inc(nsum_done, 1)

            def project_out(f):
                pe.wait_ge(yg_done, 2 * f + 2)
                for b in range(CB):
                    for half in range(HALVES):
                        last = t.matmul(pa[1][:, P * b:P * b + P], yg[:, half, P * b:P * b + P], w_out[:, half, :],
                                        start=(half == 0), stop=(half == HALVES - 1))
                last.then_inc(op_done, 1)

            pe.wait_ge(consts_ready, 1)
            transpose_x(0)
            pe.wait_ge(aneg_ready, 2)
            for gr in range(G):
                last = t.matmul(dbu[0][:, N * gr:N * gr + N], spread[:, gr % Q, :], a_neg[:, gr // Q, :], start=True, stop=True)
            last.then_inc(arep_mm, 1)
            pe.wait_ge(wtap_ready, 1)
            project_u(0, 0)
            project_u(0, 1)
            project_z(0)
            project_bc_dt(0)
            transpose_x(1)
            project_delta(0, first=True)
            project_u(1, 0)
            project_u(1, 1)
            project_z(1)
            spread_w(0, 0)

            def body(f, first, second, finish):
                for gr in range(G):
                    if gr + 1 < G:
                        spread_w(f, gr + 1)
                    elif second:
                        spread_w(f + 1, 0)
                    if second and gr == 0:
                        project_bc_dt(f + 1)
                        if first:
                            transpose_x(f + 2)
                        project_delta(f + 1, first)
                    if finish and gr == 1:
                        sum_states(f - 1, 3)
                    if first and gr == 2:
                        project_u(f + 2, 0)
                    if first and gr == 4:
                        project_u(f + 2, 1)
                    if finish and gr == 4:
                        if first:
                            pe.wait_ge(uact_done, 2 * f + 5)
                        elif second:
                            pe.wait_ge(dact_done, 2 * f + 3)
                        else:
                            pe.wait_ge(x1_done, f - 1)
                        project_out(f - 1)
                    if gr >= 3 and gr % 2:
                        sum_states(f, (gr - 3) // 2)
                    if first and gr == 6:
                        project_z(f + 2)
            walk(pe, body)
            sum_states(CHUNKS - 1, 3)
            pe.wait_ge(x1_done, CHUNKS - 1)
            project_out(CHUNKS - 1)


def expert_layer(nc, x_ext, centroids, gamma, beta, W1, b1, W2, b2, sorted_rows, out):
    F32, I32 = mybir.dt.float32, mybir.dt.int32
    U32 = mybir.dt.uint32
    E, F, D = W1.shape
    BLOCKS = x_ext.shape[1]
    T = BLOCKS * P
    EXT = x_ext.shape[2]
    MEAN, SCALE_N, SCALE_B, SHIFT_B, ALPHA, ROW = range(D, D + 6)
    MAX_TILES = (T + E * (P - 1)) // P
    FC = F // P
    CB = 512 // P
    CHUNKS = BLOCKS // CB
    UNUSED = 1 << 20
    IndexOn = bass.IndirectOffsetOnAxis

    with ExitStack() as ctx:
        def sb(name, shape, dt=F32):
            return ctx.enter_context(nc.sbuf_tensor(name, shape, dt))

        def sem(name):
            return ctx.enter_context(nc.semaphore(name))

        w1_in = sb("w1_in", [P, E, FC, D])
        w2_in = sb("w2_in", [P, E, F])
        w1_raw = sb("w1_raw", [P, E, F])
        w1_t = sb("w1_t", [P, E, F])
        w2_t = sb("w2_t", [P, E, FC, D])
        bias1 = sb("bias1", [P, E, F])
        bias2 = sb("bias2", [P, E, D])
        small_in = sb("small_in", [E, 3, D])
        small_t = sb("small_t", [P, 3, E])
        zero_rows = sb("zero_rows", [P, EXT])
        f_ident = sb("f_ident", [P, P])
        before = sb("before", [P, P])
        ones = sb("ones", [P, P])
        io_e = sb("io_e", [P, E], I32)
        io_b = sb("io_b", [P, BLOCKS], I32)
        io_j = sb("io_j", [P, MAX_TILES], I32)
        e_of = sb("e_of", [P, E])
        rows_of = sb("rows_of", [P, BLOCKS])
        tile_of = sb("tile_of", [P, MAX_TILES])
        f_stats = sb("f_stats", [P, BLOCKS, 6])
        f_mv = sb("f_mv", [P, BLOCKS, 2])
        f_var = sb("f_var", [P, BLOCKS])
        f_var2 = sb("f_var2", [P, BLOCKS])
        f_half = sb("f_half", [P, BLOCKS])
        f_rstd = sb("f_rstd", [P, BLOCKS])
        f_rstd2 = sb("f_rstd2", [P, BLOCKS])
        feats = sb("feats", [P, BLOCKS, D])
        feats_t = sb("feats_t", [P, 2, CB * P])
        score = sb("score", [P, BLOCKS, E])
        best = sb("best", [P, BLOCKS])
        less = sb("less", [P, BLOCKS, E])
        first = sb("first", [P, BLOCKS])
        onehot = sb("onehot", [P, BLOCKS, E])
        neg_exp = sb("neg_exp", [P, BLOCKS])
        block_count = sb("block_count", [P, E, BLOCKS])
        upto = sb("upto", [P, E, BLOCKS])
        more = sb("more", [P, E, BLOCKS])
        tiles = sb("tiles", [P, E])
        tiles_upto = sb("tiles_upto", [P, E])
        start = sb("start", [P, E])
        offset = sb("offset", [P, E, BLOCKS])
        place = sb("place", [P, BLOCKS, E])
        slot_f = sb("slot_f", [P, BLOCKS])
        slot_i = sb("slot_i", [P, BLOCKS], U32)
        passed = sb("passed", [P, MAX_TILES, E])
        expert_f = sb("expert_f", [P, MAX_TILES])
        expert_i = sb("expert_i", [P, MAX_TILES], I32)
        rows = sb("rows", [P, MAX_TILES, EXT])
        xhat = sb("xhat", [P, 2, D])
        xhat_t = sb("xhat_t", [P, 2, P])
        hidden = sb("hidden", [P, 2, F])
        hidden_t = sb("hidden_t", [P, 2, F])
        base2 = sb("base2", [P, 2, D])
        y2 = sb("y2", [P, 2, D])
        done_rows = sb("done_rows", [P, MAX_TILES, D])
        bk = [ctx.enter_context(nc.psum_tensor(f"f_bank{i}", [P, 512], F32)) for i in range(8)]

        w1_landed = sem("f_w1_landed")
        w2_landed = sem("f_w2_landed")
        bias_landed = sem("f_bias_landed")
        small_landed = sem("f_small_landed")
        zero_ready = sem("f_zero_ready")
        zero_landed = sem("f_zero_landed")
        setup_done = sem("f_setup_done")
        consts_done = sem("f_consts_done")
        smallt_mm = sem("f_smallt_mm")
        smallt_ready = sem("f_smallt_ready")
        wtr_done = sem("f_wtr_done")
        wev_done = sem("f_wev_done")
        fst_done = sem("f_fst_done")
        fmv_done = sem("f_fmv_done")
        fvar_done = sem("f_fvar_done")
        frstd_done = sem("f_frstd_done")
        fv1 = sem("f_fv1")
        fvar2_done = sem("f_fvar2_done")
        frstd2_done = sem("f_frstd2_done")
        fscale_done = sem("f_fscale_done")
        fsn_done = sem("f_fsn_done")
        feats_ready = sem("f_feats_ready")
        ftr_done = sem("f_ftr_done")
        ftev_done = sem("f_ftev_done")
        score_done = sem("f_score_done")
        route = sem("f_route")
        onehot_ready = sem("f_onehot_ready")
        prefix_done = sem("f_prefix_done")
        slot_ready = sem("f_slot_ready")
        expert_ready = sem("f_expert_ready")
        ext_ready = sem("f_ext_ready")
        negexp_done = sem("f_negexp_done")
        bias_mm = sem("f_bias_mm")
        bias_ready = sem("f_bias_ready")
        scattered = sem("f_scattered")
        rows_landed = sem("f_rows_landed")
        xhat_ready = sem("f_xhat_ready")
        xt_done = sem("f_xt_done")
        xtev_done = sem("f_xtev_done")
        mm1_done = sem("f_mm1_done")
        hid_ready = sem("f_hid_ready")
        ht_done = sem("f_ht_done")
        relu_done = sem("f_relu_done")
        mm2_done = sem("f_mm2_done")
        base2_ready = sem("f_base2_ready")
        y2_ready = sem("f_y2_ready")
        done_ready = sem("f_done_ready")
        out_written = sem("f_out_written")

        block = ctx.enter_context(nc.Block())
        N_T = MAX_TILES

        def walk_tiles(eng, step):
            step(0, 0, behind=False)
            step(1, 1)
            step(2, 0)
            pairs = (N_T - 2) // 2
            with eng.Fori(1, pairs) as k:
                step(2 * k + 1, 1)
                step(2 * k + 2, 0)
            for i in range(2 * pairs + 1, N_T):
                step(i, i % 2, ahead=i + 1 < N_T)

        @block.sync
        def _(sp):
            sp.dma_start(w1_in[:, :, :, :], W1.rearrange("e (c p) d -> p e c d", p=P)).then_inc(w1_landed, 16)
            sp.dma_start(w2_in[:, :, :], W2.rearrange("e d f -> d e f")).then_inc(w2_landed, 16)
            sp.dma_start(bias1[:, :, :].rearrange("p e f -> p (e f)"),
                         b1.rearrange("(o e) f -> o (e f)", o=1).broadcast_to([P, E * F])).then_inc(bias_landed, 16)
            sp.dma_start(bias2[:, :, :].rearrange("p e d -> p (e d)"),
                         b2.rearrange("(o e) d -> o (e d)", o=1).broadcast_to([P, E * D])).then_inc(bias_landed, 16)
            sp.wait_ge(zero_ready, 1)
            for i in range(MAX_TILES):
                sp.dma_start(sorted_rows[P * i:P * i + P, :], zero_rows[:, :]).then_inc(zero_landed, 16)
            sp.wait_ge(scattered, 16 * BLOCKS)
            for i in range(0, MAX_TILES, 13):
                n = min(13, MAX_TILES - i)
                sp.dma_start(rows[:, i:i + n, :], sorted_rows[P * i:P * (i + n), :].rearrange("(j p) d -> p j d", p=P))\
                  .then_inc(rows_landed, 16)
            sp.wait_ge(out_written, 16 * N_T)

        @block.gpsimd
        def _(pool):
            g = nc.gpsimd
            g.memset(zero_rows[:, :], 0.0).then_inc(setup_done, 1)
            g.memset(f_half[:, :], -0.5)
            g.memset(f_ident[:, :], 0.0)
            g.memset(before[:, :], 1.0)
            g.memset(ones[:, :], 1.0)
            g.memset(x_ext[:, :, ROW + 1:], 0.0)
            g.iota(io_e[:, :], [[1, E]], base=0, channel_multiplier=0)
            g.iota(io_b[:, :], [[P, BLOCKS]], base=0, channel_multiplier=0)
            g.iota(io_j[:, :], [[1, MAX_TILES]], base=0, channel_multiplier=0)
            g.iota(x_ext[:, :, ROW].bitcast(I32), [[P, BLOCKS]], base=0, channel_multiplier=1).then_inc(setup_done, 1)
            pool.wait_ge(setup_done, 2)
            g.memset(zero_rows[:, ROW:ROW + 1].bitcast(I32), UNUSED).then_inc(zero_ready, 1)
            g.affine_select(out=f_ident[:, :], in_=f_ident[:, :], compare_op=ALU.not_equal, fill=1.0, base=0,
                            pattern=[[-1, P]], channel_multiplier=1)
            g.affine_select(out=before[:, :], in_=before[:, :], compare_op=ALU.is_gt, fill=0.0, base=0,
                            pattern=[[1, P]], channel_multiplier=-1).then_inc(consts_done, 1)
            pool.wait_ge(fvar_done, 1)
            g.tensor_tensor(f_rstd[:, :], f_var[:, :], f_half[:, :], ALU.pow).then_inc(frstd_done, 1)
            pool.wait_ge(fvar2_done, 1)
            g.tensor_tensor(f_rstd2[:, :], f_var2[:, :], f_half[:, :], ALU.pow).then_inc(frstd2_done, 1)
            pool.wait_ge(slot_ready, 1)
            pool.wait_ge(ext_ready, 1)
            pool.wait_ge(fsn_done, 1)
            pool.wait_ge(fscale_done, 2)
            pool.wait_ge(zero_landed, 16 * MAX_TILES)
            for i in range(BLOCKS):
                g.indirect_dma_start(out=sorted_rows, out_offset=IndexOn(slot_i[:, i:i + 1], 0),
                                     in_=x_ext[:, i, :], in_offset=None).then_inc(scattered, 16)
            for i in range(N_T):
                pool.wait_ge(done_ready, i + 1)
                if i % 13 == 0:
                    pool.wait_ge(rows_landed, 48)
                g.indirect_dma_start(out=out, out_offset=IndexOn(rows[:, i, ROW:ROW + 1].bitcast(U32), 0),
                                     in_=done_rows[:, i, :], in_offset=None, bounds_check=T - 1,
                                     oob_is_err=False).then_inc(out_written, 16)

        def e_at(reg):
            return bass.ds(reg, 1)

        @block.vector
        def _(dve):
            v = nc.vector
            for i in range(BLOCKS):
                last = v.bn_stats(f_stats[:, i, :], x_ext[:, i, 0:D])
            last.then_inc(fst_done, 1)
            dve.wait_ge(fst_done, 1)
            for i in range(BLOCKS):
                last = v.bn_aggr(f_mv[:, i, :], f_stats[:, i, :])
            last.then_inc(fmv_done, 1)
            dve.wait_ge(fmv_done, 1)
            v.tensor_scalar(f_var[:, :], f_mv[:, :, 1], EPS, None, ALU.add).then_inc(fvar_done, 1)
            v.tensor_copy(x_ext[:, :, MEAN], f_mv[:, :, 0])
            dve.wait_ge(frstd_done, 1)
            v.tensor_tensor(f_var2[:, :], f_mv[:, :, 1], f_rstd[:, :], ALU.mult).then_inc(fv1, 1)
            dve.wait_ge(fv1, 1)
            v.tensor_tensor(f_var2[:, :], f_var2[:, :], f_rstd[:, :], ALU.mult).then_inc(fv1, 1)
            dve.wait_ge(fv1, 2)
            v.tensor_scalar(f_var2[:, :], f_var2[:, :], EPS, None, ALU.add).then_inc(fvar2_done, 1)
            v.tensor_scalar(x_ext[:, :, SCALE_B], f_rstd[:, :], 1.0, None, ALU.add).then_inc(fscale_done, 1)
            v.scalar_tensor_tensor(out=x_ext[:, :, SHIFT_B], in0=f_mv[:, :, 0], scalar=-1.0, in1=f_rstd[:, :],
                                   op0=ALU.mult, op1=ALU.mult).then_inc(fscale_done, 1)
            for i in range(BLOCKS):
                last = v.tensor_scalar(feats[:, i, :], x_ext[:, i, 0:D], f_mv[:, i, 0:1], f_rstd[:, i:i + 1],
                                       ALU.subtract, ALU.mult)
                if i % CB == CB - 1:
                    last.then_inc(feats_ready, 1)
            dve.wait_ge(frstd2_done, 1)
            v.tensor_tensor(x_ext[:, :, SCALE_N], f_rstd[:, :], f_rstd2[:, :], ALU.mult).then_inc(fsn_done, 1)
            dve.wait_ge(setup_done, 2)
            v.tensor_copy(e_of[:, :], io_e[:, :])
            v.tensor_copy(rows_of[:, :], io_b[:, :])
            v.tensor_copy(tile_of[:, :], io_j[:, :]).then_inc(route, 1)

            steps = [1]

            def then(ins):
                steps[0] += 1
                ins.then_inc(route, 1)
                dve.wait_ge(route, steps[0])

            def over_blocks(ap):
                return ap.unsqueeze(1).broadcast_to([P, BLOCKS, E])

            def over_experts(ap, n):
                return ap.unsqueeze(2).broadcast_to([P, n, E])

            dve.wait_ge(score_done, CHUNKS)
            dve.wait_ge(route, 1)
            then(v.tensor_copy(score[:, :, :].rearrange("p b e -> p (b e)"), bk[6][:, 0:BLOCKS * E]))
            then(v.tensor_reduce(best[:, :], score[:, :, :], AX.X, ALU.max))
            then(v.tensor_tensor(less[:, :, :], score[:, :, :], over_experts(best[:, :], BLOCKS), ALU.is_lt))
            then(v.scalar_tensor_tensor(out=less[:, :, :], in0=less[:, :, :], scalar=float(E), in1=over_blocks(e_of[:, :]),
                                        op0=ALU.mult, op1=ALU.add))
            then(v.tensor_reduce(first[:, :], less[:, :, :], AX.X, ALU.min))
            v.tensor_tensor(onehot[:, :, :], over_blocks(e_of[:, :]), over_experts(first[:, :], BLOCKS),
                            ALU.is_equal).then_inc(onehot_ready, 1)
            dve.wait_ge(prefix_done, 2)
            then(v.tensor_copy(block_count[:, :, :], bk[5][:, 0:BLOCKS * E].rearrange("p (b e) -> p e b", e=E)))
            for e in range(E):
                last = v.tensor_tensor_scan(upto[:, e, :], ones[:, 0:BLOCKS], block_count[:, e, :], 0.0, ALU.mult, ALU.add)
            then(last)
            then(v.tensor_tensor(more[:, :, :], upto[:, :, BLOCKS - 1:BLOCKS].broadcast_to([P, E, BLOCKS]),
                                 rows_of[:, :].unsqueeze(1).broadcast_to([P, E, BLOCKS]), ALU.is_gt))
            then(v.tensor_reduce(tiles[:, :], more[:, :, :], AX.X, ALU.add))
            then(v.tensor_tensor_scan(tiles_upto[:, :], ones[:, 0:E], tiles[:, :], 0.0, ALU.mult, ALU.add))
            then(v.tensor_tensor(start[:, :], tiles_upto[:, :], tiles[:, :], ALU.subtract))
            then(v.tensor_scalar(start[:, :], start[:, :], float(P), None, ALU.mult))
            then(v.tensor_tensor(offset[:, :, :], upto[:, :, :], block_count[:, :, :], ALU.subtract))
            then(v.tensor_tensor(offset[:, :, :], offset[:, :, :], start[:, :].unsqueeze(2).broadcast_to([P, E, BLOCKS]), ALU.add))
            then(v.tensor_tensor(place[:, :, :], bk[4][:, 0:BLOCKS * E].rearrange("p (b e) -> p b e", e=E),
                                 offset[:, :, :].rearrange("p e b -> p b e"), ALU.add))
            then(v.tensor_tensor(place[:, :, :], place[:, :, :], onehot[:, :, :], ALU.mult))
            then(v.tensor_reduce(slot_f[:, :], place[:, :, :], AX.X, ALU.add))
            v.tensor_copy(slot_i[:, :], slot_f[:, :]).then_inc(slot_ready, 1)
            dve.wait_ge(negexp_done, 1)
            then(v.tensor_scalar(neg_exp[:, :], neg_exp[:, :], 1.0, None, ALU.add))
            v.reciprocal(x_ext[:, :, ALPHA], neg_exp[:, :]).then_inc(ext_ready, 1)
            then(v.tensor_tensor(passed[:, :, :], tiles_upto[:, :].unsqueeze(1).broadcast_to([P, MAX_TILES, E]),
                                 over_experts(tile_of[:, :], MAX_TILES), ALU.is_le))
            then(v.tensor_reduce(expert_f[:, :], passed[:, :, :], AX.X, ALU.add))
            then(v.tensor_scalar(expert_f[:, :], expert_f[:, :], float(E - 1), None, ALU.min))
            v.tensor_copy(expert_i[:, :], expert_f[:, :]).then_inc(expert_ready, 1)
            dve.wait_ge(bias_landed, 32)
            for e in range(E):
                dve.wait_ge(bias_mm, e + 1)
                v.tensor_tensor(bias1[:, e, :], bk[2 + e % 2][:, :], bias1[:, e, :], ALU.add).then_inc(bias_ready, 1)
            dve.wait_ge(bias_ready, E)
            dve.wait_ge(expert_ready, 1)

            def normalise(i, r):
                if not isinstance(i, int) or i >= 2:
                    dve.wait_ge(xt_done, i - 1)
                v.tensor_scalar(xhat[:, r, :], rows[:, e_at(i), 0:D].rearrange("p o d -> p (o d)"),
                                rows[:, e_at(i), MEAN], rows[:, e_at(i), SCALE_N], ALU.subtract, ALU.mult)\
                 .then_inc(xhat_ready, 1)

            def add_bias(i, r):
                e = dve.value_load(expert_i[0:1, e_at(i)], min_val=0, max_val=E - 1)
                dve.wait_ge(mm1_done, i + 1)
                if not isinstance(i, int) or i >= 2:
                    dve.wait_ge(ht_done, i - 1)
                v.tensor_tensor(hidden[:, r, :], bk[2 + r][:, :], bias1[:, e_at(e), :].rearrange("p o f -> p (o f)"),
                                ALU.add).then_inc(hid_ready, 1)

            def finish(i, r):
                e = dve.value_load(expert_i[0:1, e_at(i)], min_val=0, max_val=E - 1)
                dve.wait_ge(mm2_done, i + 1)
                v.tensor_tensor(y2[:, r, :], bk[6 + r][:, 0:D], bias2[:, e_at(e), :].rearrange("p o f -> p (o f)"),
                                ALU.add).then_inc(y2_ready, 1)
                dve.wait_ge(y2_ready, i + 1)
                dve.wait_ge(base2_ready, i + 1)
                v.scalar_tensor_tensor(out=done_rows[:, e_at(i), :].rearrange("p o f -> p (o f)"), in0=y2[:, r, :],
                                       scalar=rows[:, e_at(i), ALPHA], in1=base2[:, r, :],
                                       op0=ALU.mult, op1=ALU.add).then_inc(done_ready, 1)

            dve.wait_ge(rows_landed, 48)

            def step(i, r, ahead=True, behind=True):
                if ahead:
                    normalise(i + 1, 1 - r)
                add_bias(i, r)
                if behind:
                    finish(i - 1, 1 - r)
            normalise(0, 0)
            walk_tiles(dve, step)
            finish(N_T - 1, (N_T - 1) % 2)

        @block.scalar
        def _(act):
            a = nc.scalar
            for i, src in enumerate((centroids, gamma, beta)):
                act.dma_start(small_in[:, i, :], src).then_inc(small_landed, 16)
            act.wait_ge(smallt_mm, 1)
            a.activation(small_t[:, :, :].rearrange("p i e -> p (i e)"), bk[7][:, 0:3 * E], ACT.Identity)\
             .then_inc(smallt_ready, 1)
            act.wait_ge(smallt_ready, 1)
            for n in range(2 * E):
                e = n // 2
                act.wait_ge(wtr_done, n + 1)
                if n % 2 == 0:
                    a.activation(w1_raw[:, e, :], bk[0][:, :], ACT.Identity)
                    a.activation(w1_t[:, e, :], bk[0][:, :], ACT.Identity, scale=small_t[:, 1, e:e + 1]).then_inc(wev_done, 1)
                else:
                    a.activation(w2_t[:, e, :, :].rearrange("p c d -> p (c d)"), bk[1][:, :], ACT.Identity).then_inc(wev_done, 1)
            for c in range(CHUNKS):
                act.wait_ge(ftr_done, c + 1)
                if c >= 2:
                    act.wait_ge(score_done, c - 1)
                a.activation(feats_t[:, c % 2, :], bk[4 + c % 2][:, :], ACT.Identity).then_inc(ftev_done, 1)
            act.wait_ge(route, 3)
            a.activation(neg_exp[:, :], best[:, :], ACT.Exp, scale=-1.0).then_inc(negexp_done, 1)
            act.wait_ge(rows_landed, 48)

            def to_columns(i, r):
                act.wait_ge(xt_done, i + 1)
                if not isinstance(i, int) or i >= 2:
                    act.wait_ge(mm1_done, i - 1)
                a.activation(xhat_t[:, r, :], bk[r][:, 0:P], ACT.Identity).then_inc(xtev_done, 1)

            def residual(i, r):
                if not isinstance(i, int) or i >= 2:
                    act.wait_ge(done_ready, i - 1)
                a.activation(base2[:, r, :], rows[:, e_at(i), 0:D].rearrange("p o d -> p (o d)"), ACT.Identity,
                             scale=rows[:, e_at(i), SCALE_B], bias=rows[:, e_at(i), SHIFT_B]).then_inc(base2_ready, 1)

            def relu(i, r):
                act.wait_ge(ht_done, i + 1)
                if not isinstance(i, int) or i >= 2:
                    act.wait_ge(mm2_done, i - 1)
                a.activation(hidden_t[:, r, :], bk[4 + r][:, :], ACT.Relu).then_inc(relu_done, 1)

            def step(i, r, ahead=True, behind=True):
                if ahead:
                    to_columns(i + 1, 1 - r)
                residual(i, r)
                relu(i, r)
            to_columns(0, 0)
            walk_tiles(act, step)

        @block.tensor
        def _(pe):
            t = nc.tensor
            pe.wait_ge(consts_done, 1)
            pe.wait_ge(small_landed, 48)
            for i in range(3):
                last = t.transpose(bk[7][:, E * i:E * i + E], small_in[:, i, :], f_ident[0:E, 0:E])
            last.then_inc(smallt_mm, 1)
            for n in range(2 * E):
                e = n // 2
                if n >= 2:
                    pe.wait_ge(wev_done, n - 1)
                if n == 0:
                    pe.wait_ge(w1_landed, 16)
                    pe.wait_ge(w2_landed, 16)
                for c in range(FC):
                    src = w1_in[:, e, c, :] if n % 2 == 0 else w2_in[:, e, P * c:P * c + P]
                    last = t.transpose(bk[n % 2][:, P * c:P * c + P], src, f_ident[:, :])
                last.then_inc(wtr_done, 1)

            def score_blocks(c):
                pe.wait_ge(ftev_done, c + 1)
                if c == 0:
                    pe.wait_ge(smallt_ready, 1)
                for b in range(CB):
                    i = CB * c + b
                    last = t.matmul(bk[6][:, E * i:E * i + E], feats_t[:, c % 2, P * b:P * b + P], small_t[:, 0, :],
                                    start=True, stop=True)
                last.then_inc(score_done, 1)
            for c in range(CHUNKS):
                pe.wait_ge(feats_ready, c + 1)
                if c >= 2:
                    pe.wait_ge(ftev_done, c - 1)
                for b in range(CB):
                    last = t.transpose(bk[4 + c % 2][:, P * b:P * b + P], feats[:, CB * c + b, :], f_ident[:, :])
                last.then_inc(ftr_done, 1)
                if c:
                    score_blocks(c - 1)
            score_blocks(CHUNKS - 1)
            pe.wait_ge(onehot_ready, 1)
            flat = onehot[:, :, :].rearrange("p b e -> p (b e)")
            t.matmul(bk[4][:, 0:BLOCKS * E], before[:, :], flat, start=True, stop=True).then_inc(prefix_done, 1)
            t.matmul(bk[5][:, 0:BLOCKS * E], ones[:, :], flat, start=True, stop=True).then_inc(prefix_done, 1)
            pe.wait_ge(wev_done, 2 * E)
            for e in range(E):
                if e >= 2:
                    pe.wait_ge(bias_ready, e - 1)
                t.matmul(bk[2 + e % 2][:, :], small_t[:, 2, e:e + 1].broadcast_to([P, P]), w1_raw[:, e, :],
                         start=True, stop=True).then_inc(bias_mm, 1)
            pe.wait_ge(bias_ready, E)
            pe.wait_ge(expert_ready, 1)

            def rows_t(i, r):
                pe.wait_ge(xhat_ready, i + 1)
                if not isinstance(i, int) or i >= 2:
                    pe.wait_ge(xtev_done, i - 1)
                t.transpose(bk[r][:, 0:P], xhat[:, r, :], f_ident[:, :]).then_inc(xt_done, 1)

            def up(i, r):
                e = pe.value_load(expert_i[0:1, e_at(i)], min_val=0, max_val=E - 1)
                pe.wait_ge(xtev_done, i + 1)
                if not isinstance(i, int) or i >= 2:
                    pe.wait_ge(hid_ready, i - 1)
                t.matmul(bk[2 + r][:, :], xhat_t[:, r, :], w1_t[:, e_at(e), :].rearrange("p o f -> p (o f)"),
                         start=True, stop=True).then_inc(mm1_done, 1)

            def hidden_columns(i, r):
                pe.wait_ge(hid_ready, i + 1)
                if not isinstance(i, int) or i >= 2:
                    pe.wait_ge(relu_done, i - 1)
                for c in range(FC):
                    last = t.transpose(bk[4 + r][:, P * c:P * c + P], hidden[:, r, P * c:P * c + P], f_ident[:, :])
                last.then_inc(ht_done, 1)

            def down(i, r):
                e = pe.value_load(expert_i[0:1, e_at(i)], min_val=0, max_val=E - 1)
                pe.wait_ge(relu_done, i + 1)
                if not isinstance(i, int) or i >= 2:
                    pe.wait_ge(y2_ready, i - 1)
                for c in range(FC):
                    last = t.matmul(bk[6 + r][:, 0:D], hidden_t[:, r, P * c:P * c + P],
                                    w2_t[:, e_at(e), c, :].rearrange("p o f -> p (o f)"), start=(c == 0), stop=(c == FC - 1))
                last.then_inc(mm2_done, 1)

            def step(i, r, ahead=True, behind=True):
                up(i, r)
                if ahead:
                    rows_t(i + 1, 1 - r)
                if behind:
                    down(i - 1, 1 - r)
                hidden_columns(i, r)
            rows_t(0, 0)
            walk_tiles(pe, step)
            down(N_T - 1, (N_T - 1) % 2)


def program(nc, mamba_inputs, ffn_inputs, out):
    x = mamba_inputs[0]
    T, DM = x.shape[0] * x.shape[1], x.shape[2]
    E = ffn_inputs[0].shape[0]
    EXT = DM + 8
    tiles = (T + E * (P - 1)) // P
    bc_scratch = nc.dram_tensor("bc_scratch", (32, 512), F32, kind="Internal").ap()
    sorted_rows = nc.dram_tensor("sorted_rows", (tiles * P, EXT), F32, kind="Internal").ap()
    with nc.sbuf_tensor("x_ext", [P, T // P, EXT], F32) as x_ext:
        mamba_layer(nc, *mamba_inputs, bc_scratch, x_ext[:, :, 0:DM], None)
        expert_layer(nc, x_ext, *ffn_inputs, sorted_rows, out)


_MAMBA = ['x', 'in_proj_w', 'conv_w', 'conv_b', 'x_proj_w', 'dt_proj_w', 'dt_proj_b', 'A_log', 'D', 'out_proj_w',
          'ln_g', 'ln_b']
_FFN = ['centroids', 'gamma', 'beta', 'W1', 'b1', 'W2', 'b2']


def kernel(**inputs):
    import numpy as _np
    import concourse.bacc as _bacc
    from concourse.bass_utils import run_bass_kernel_spmd as _run

    nc = _bacc.Bacc("TRN2", target_bir_lowering=False, num_devices=1)
    arrays = {}

    def declare(name):
        a = _np.ascontiguousarray(inputs[name])
        arrays["in_" + name] = a
        return nc.dram_tensor("in_" + name, a.shape, F32, kind="ExternalInput").ap()
    mamba_inputs = [declare("L0_attn_" + n) for n in _MAMBA]
    ffn_inputs = [declare("L0_ffn_" + n) for n in _FFN]
    shape = inputs["L0_attn_x"].shape
    out = nc.dram_tensor("out", (shape[0] * shape[1], shape[2]), F32, kind="ExternalOutput").ap()
    program(nc, mamba_inputs, ffn_inputs, out)
    r = _run(nc, [arrays], core_ids=[0])
    return r.results[0]["out"].reshape(shape)
```

```python
from contextlib import ExitStack

import concourse.bass as bass
from concourse import mybir

P = 128
F32 = mybir.dt.float32
ALU = mybir.AluOpType
ACT = mybir.ActivationFunctionType
AX = mybir.AxisListType
EPS = 1e-5


def mamba_layer(nc, x, in_proj_w, conv_w, conv_b, x_proj_w, dt_proj_w, dt_proj_b, A_log, D, out_proj_w,
                ln_g, ln_b, W1, W2, w1_turned, w2_turned, bc_scratch, x_all, small, small_t, score, x1_mv):
    B, L, DM = x.shape
    DIN, N = A_log.shape
    R = x_proj_w.shape[1] - 2 * N
    TAPS = conv_w.shape[1]
    T = B * L
    BLOCKS = T // P
    C = 512
    CHUNKS = T // C
    SEQ_CHUNKS = L // C
    CB = C // P
    HALVES = DIN // P
    S, DG = 4, 32
    Q = P // DG
    G = HALVES * Q
    J = N // S
    K = G * J
    DA_RING, H_RING = 8, 16
    UZ = 3
    PAD = TAPS - 1
    EARLY = 2 * CB
    assert DM == P and N == S * J and K % H_RING == 0 and 2 * N + R <= P

    with ExitStack() as ctx:
        def sb(name, shape):
            return ctx.enter_context(nc.sbuf_tensor(name, shape, F32))

        def bank(name):
            return ctx.enter_context(nc.psum_tensor(name, [P, C], F32))

        def sem(name):
            return ctx.enter_context(nc.semaphore(name))

        win = sb("win", [P, 2 * DIN])
        w_tap = sb("w_tap", [P, TAPS, DIN])
        conv_b_half = sb("conv_b_half", [P, HALVES])
        w_xproj = sb("w_xproj", [P, HALVES, P])
        w_dt = sb("w_dt", [P, DIN])
        dt_bias = sb("dt_bias", [P, HALVES])
        a_log = sb("a_log", [P, HALVES, N])
        a_neg = sb("a_neg", [P, HALVES, N])
        a_rep = sb("a_rep", [P, G, J])
        d_skip = sb("d_skip", [P, HALVES])
        w_out = sb("w_out", [P, HALVES, DM])
        g_col = sb("g_col", [P, 1])
        b_col = sb("b_col", [P, 1])
        ident = sb("ident", [P, P])
        spread = sb("spread", [P, Q, P])
        gather = sb("gather", [P, DG])
        c_mean = sb("c_mean", [W1.shape[0], 1])
        started = sb("started", [P, 1])
        stats = sb("stats", [P, BLOCKS, 6])
        mv = sb("mv", [P, BLOCKS, 2])
        var_eps = sb("var_eps", [P, BLOCKS])
        neg_half = sb("neg_half", [P, BLOCKS])
        rstd = sb("rstd", [P, BLOCKS])
        var2 = sb("var2", [P, BLOCKS])
        rstd2 = sb("rstd2", [P, BLOCKS])
        scale_n = sb("scale_n", [P, BLOCKS])
        scale_b = sb("scale_b", [P, BLOCKS])
        shift_n = sb("shift_n", [P, BLOCKS])
        shift_b = sb("shift_b", [P, BLOCKS])
        xh = sb("xh", [P, CB, P])
        xn_t = sb("xn_t", [P, B * (PAD + L)])
        ln = sb("ln", [P, HALVES, C])
        relu = sb("relu", [P, HALVES, C])
        e = sb("e", [P, HALVES, C])
        u = sb("u", [P, UZ, HALVES, C])
        zg = sb("zg", [P, UZ, HALVES, C])
        w = sb("w", [P, 2, HALVES, C])
        delta = sb("delta", [P, HALVES, C])
        conv_rep = delta[:, :, :].rearrange("p h t -> p (h t)").rearrange("p (d k) -> p d k", k=TAPS)
        delta_rep = sb("delta_rep", [P, G, C])
        bc = sb("bc", [P, C])
        bc_rep = sb("bc_rep", [P, 2, 2 * J, C])
        da = sb("da", [P, DA_RING, C])
        h = sb("h", [P, H_RING, C])
        carry = sb("carry", [P, CHUNKS + B, K])
        du = sb("du", [P, HALVES, C])
        yg = sb("yg", [P, HALVES, C])
        base = sb("base", [P, CB, P])
        small_in = base[0:W1.shape[0], 0:3, :]

        w_ps = [bank("w_ps0"), bank("w_ps1")]
        dbu = [bank("dbu0"), bank("dbu1")]
        y_ps = [bank("y_ps0"), bank("y_ps1")]
        pa = [bank("pa0"), bank("pa1")]

        x_in = [sem(f"x_in{i}") for i in range(BLOCKS // 8)]
        weights_in = sem("weights_in")
        small_landed = sem("small_landed")
        centred = sem("centred")
        small_mm = sem("small_mm")
        small_ready = sem("small_ready")
        xtr_done = sem("xtr_done")
        xt_ready = sem("xt_ready")
        score_mm = sem("score_mm")
        score_out = sem("score_out")
        x1stats_done = sem("x1stats_done")
        w1_in = sem("w1_in")
        w2_in = sem("w2_in")
        wtr_done = sem("wtr_done")
        wev_done = sem("wev_done")
        w1_out = sem("w1_out")
        w2_out = sem("w2_out")
        iota_done = sem("iota_done")
        zeroed = sem("zeroed")
        wtap_ready = sem("wtap_ready")
        aneg_ready = sem("aneg_ready")
        arep_mm = sem("arep_mm")
        arep_ready = sem("arep_ready")
        stats_done = sem("stats_done")
        aggr_done = sem("aggr_done")
        vareps_ready = sem("vareps_ready")
        rstd_ready = sem("rstd_ready")
        var2_ready = sem("var2_ready")
        rstd2_ready = sem("rstd2_ready")
        norm_ready = sem("norm_ready")
        halfbias_ready = sem("halfbias_ready")
        xh_ready = sem("xh_ready")
        tr_done = sem("tr_done")
        xn_ready = sem("xn_ready")
        umm_done = sem("umm_done")
        uact_done = sem("uact_done")
        u_ready = sem("u_ready")
        zmm_done = sem("zmm_done")
        zact_done = sem("zact_done")
        zg_done = sem("zg_done")
        xpmm_done = sem("xpmm_done")
        bc_ready = sem("bc_ready")
        scr_written = sem("scr_written")
        bcrep_landed = sem("bcrep_landed")
        dmm_done = sem("dmm_done")
        dact_done = sem("dact_done")
        e_ready = sem("e_ready")
        ln_ready = sem("ln_ready")
        g_ready = sem("g_ready")
        d1_done = sem("d1_done")
        one_plus_ready = sem("one_plus_ready")
        delta_ready = sem("delta_ready")
        w_ready = sem("w_ready")
        drep_landed = [sem(f"drep_landed{gr}") for gr in range(G)]
        wrep_ready = sem("wrep_ready")
        exp_done = sem("exp_done")
        mul_done = sem("mul_done")
        scan_done = sem("scan_done")
        carry_saved = sem("carry_saved")
        hc_done = sem("hc_done")
        nsum_done = sem("nsum_done")
        du_ready = sem("du_ready")
        yg_done = sem("yg_done")
        op_done = sem("op_done")
        base_ready = sem("base_ready")
        x1_done = sem("x1_done")
        ts_done = sem("ts_done")
        gather_step = sem("gather_step")
        consts_ready = sem("consts_ready")
        WEIGHT_LOADS = 9 + 3 * HALVES

        E, F, _ = W1.shape
        FC = F // P
        assert F == C and E == 2 * J and CHUNKS % 2 == 0
        w1_stage = bc_rep[:, 0, :, :]
        w2_stage = xn_t[:, 0:E * F].rearrange("p (e f) -> p e f", e=E)
        x_t = w[:, 0, :, :]
        SCORED = (CHUNKS - 2) * CB
        SCORE_AT = 2 * P
        assert SCORE_AT + SCORED * E <= C

        def turned_in(f, gr):
            if f == CHUNKS - 2 and 3 <= gr < 7:
                return range(2 * (gr - 3), 2 * (gr - 3) + 2)
            if f == CHUNKS - 1 and gr >= 4:
                return range(E + 2 * (gr - 4), E + 2 * (gr - 4) + 2)
            return ()

        def scored_in(f, gr):
            return range(3 * gr, min(3 * gr + 3, SCORED // 2 + 1)) if f == CHUNKS - 1 and gr <= 4 else ()

        def at(i, n):
            return bass.ds(i, n)

        def slot(f):
            return f + f // SEQ_CHUNKS

        def xn_cols(f, shift):
            return at(f * C + (f // SEQ_CHUNKS) * PAD + shift, C)

        def walk(eng, body):
            body(0, first=True, second=True, finish=False)
            with eng.Fori(1, CHUNKS - 2) as f:
                body(f, first=True, second=True, finish=True)
            body(CHUNKS - 2, first=False, second=True, finish=True)
            body(CHUNKS - 1, first=False, second=False, finish=True)

        block = ctx.enter_context(nc.Block())

        @block.sync
        def _(sp):
            x_v = x.rearrange("b (n p) d -> p (b n) d", p=P)
            for i in range(BLOCKS // 8):
                sp.dma_start(x_all[:, 8 * i:8 * i + 8, :], x_v[:, 8 * i:8 * i + 8, :]).then_inc(x_in[i], 16)
            sp.wait_ge(zeroed, 1)
            sp.dma_start(w_xproj[:, :, 0:2 * N], x_proj_w[:, R:].rearrange("(h p) n -> p h n", p=P)).then_inc(weights_in, 16)
            sp.dma_start(w_xproj[:, :, 2 * N:2 * N + R], x_proj_w[:, 0:R].rearrange("(h p) n -> p h n", p=P)).then_inc(weights_in, 16)
            sp.dma_start(w_dt[2 * N:2 * N + R, :], dt_proj_w).then_inc(weights_in, 16)


            def bc_replicate(n):
                sp.wait_ge(bc_ready, n + 1)
                if not isinstance(n, int) or n >= 1:
                    sp.wait_ge(bcrep_landed, 64 * n)
                sp.dma_start(bc_scratch, bc[0:2 * N, :]).then_inc(scr_written, 16)
                sp.wait_ge(scr_written, 16 * n + 16)
                if not isinstance(n, int) or n >= 2:
                    sp.wait_ge(consts_ready, 1)
                    sp.wait_ge(mul_done, K * n - K)
                    sp.wait_ge(hc_done, K * n - K)
                src = bc_scratch.rearrange("(j s) t -> s j t", s=S)
                for st in range(S):
                    dst = bc_rep[DG * st:DG * st + DG, at(n % 2, 1), :, :].rearrange("p o j t -> p (o j) t")
                    sp.dma_start(dst, src[st:st + 1, :, :].broadcast_to([DG, 2 * J, C])).then_inc(bcrep_landed, 16)

            def delta_replicate(n):
                sp.wait_ge(consts_ready, 1)
                sp.wait_ge(delta_ready, n + 1)
                for gr in range(G):
                    half, q = divmod(gr, Q)
                    if not isinstance(n, int) or n >= 1:
                        sp.wait_ge(exp_done, K * n - K + J * gr + J)
                    for st in range(S):
                        sp.dma_start(delta_rep[DG * st:DG * st + DG, gr, :],
                                     delta[DG * q:DG * q + DG, half, :]).then_inc(drep_landed[gr], 16)

            bc_replicate(0)
            delta_replicate(0)

            def body(f, first, second, finish):
                if second and not first:
                    sp.wait_ge(zmm_done, 2 * CHUNKS)
                    sp.dma_start(w2_stage, W2.rearrange("e d f -> d e f")).then_inc(w2_in, 16)
                if second:
                    sp.wait_ge(consts_ready, 1)
                    bc_replicate(f + 1)
                    delta_replicate(f + 1)
            walk(sp, body)
            sp.wait_ge(mul_done, K * (CHUNKS - 1))
            sp.wait_ge(hc_done, K * (CHUNKS - 1))
            sp.dma_start(w1_stage.rearrange("p e (c d) -> p e c d", c=FC),
                         W1.rearrange("e (c p) d -> p e c d", p=P)).then_inc(w1_in, 16)
            sp.wait_ge(wev_done, E)
            sp.dma_start(w2_turned, w2_stage).then_inc(w2_out, 16)
            sp.wait_ge(wev_done, 2 * E)
            sp.dma_start(w1_turned, w1_stage).then_inc(w1_out, 16)
            sp.wait_ge(w1_out, 16)
            sp.wait_ge(w2_out, 16)
            sp.wait_ge(x1_done, CHUNKS)

        @block.gpsimd
        def _(pool):
            g = nc.gpsimd
            g.memset(w_xproj[:, :, :], 0.0)
            g.memset(w_dt[:, :], 0.0).then_inc(zeroed, 1)
            g.memset(neg_half[:, :], -0.5)
            g.memset(ident[:, :], 0.0)
            g.memset(spread[:, :, :], 0.0)
            g.memset(gather[:, :], 0.0)
            g.memset(carry[:, :, :], 0.0)
            for b in range(B):
                last = g.memset(xn_t[:, b * (PAD + L):b * (PAD + L) + PAD], 0.0)
            last.then_inc(iota_done, 1)
            pool.wait_ge(iota_done, 1)
            g.affine_select(out=ident[:, :], in_=ident[:, :], compare_op=ALU.not_equal, fill=1.0, base=0,
                            pattern=[[-1, P]], channel_multiplier=1)
            for q in range(Q):
                v = spread[:, q, :].rearrange("p (s d) -> p s d", s=S)
                g.affine_select(out=v, in_=v, compare_op=ALU.not_equal, fill=1.0, base=-DG * q,
                                pattern=[[0, S], [-1, DG]], channel_multiplier=1)
            for st in range(S):
                g.affine_select(out=gather[:, :], in_=gather[:, :], compare_op=ALU.not_equal, fill=1.0, base=-DG * st,
                                pattern=[[-1, DG]], channel_multiplier=1).then_inc(gather_step, 1)
                pool.wait_ge(gather_step, st + 1)
            g.memset(started[:, :], 0.0).then_inc(consts_ready, 1)
            def inverse_roots(part, lo, hi):
                pool.wait_ge(vareps_ready, part + 1)
                g.tensor_tensor(rstd[:, lo:hi], var_eps[:, lo:hi], neg_half[:, lo:hi], ALU.pow).then_inc(rstd_ready, 1)
                pool.wait_ge(var2_ready, part + 1)
                g.tensor_tensor(rstd2[:, lo:hi], var2[:, lo:hi], neg_half[:, lo:hi], ALU.pow).then_inc(rstd2_ready, 1)
            inverse_roots(0, 0, EARLY)
            pool.wait_ge(weights_in, 16 * WEIGHT_LOADS)
            for k in range(TAPS):
                last = g.tensor_tensor(w_tap[:, k, :], win[:, 0:DIN], conv_rep[:, :, k], ALU.mult)
            last.then_inc(wtap_ready, 1)
            inverse_roots(1, EARLY, BLOCKS)

            def softplus_sum(n):
                flat = delta[:, :, :]
                pool.wait_ge(g_ready, n + 1)
                g.tensor_tensor(flat, e[:, :, :], flat, ALU.subtract).then_inc(d1_done, 1)
                pool.wait_ge(d1_done, n + 1)
                g.tensor_tensor(flat, flat, relu[:, :, :], ALU.add).then_inc(delta_ready, 1)

            def body(f, first, second, finish):
                for gr in range(G):
                    if gr == 4 and second:
                        softplus_sum(f + 1)
                    pool.wait_ge(scan_done, K * f + J * gr + J)
                    at0 = (J * gr) % H_RING
                    g.tensor_copy(carry[:, at(slot(f) + 1, 1), J * gr:J * gr + J].rearrange("p o k -> p (o k)"),
                                  h[:, at0:at0 + J, C - 1]).then_inc(carry_saved, J)
                    pool.wait_ge(consts_ready, 1)
                    pool.wait_ge(carry_saved, K * f + J * gr + J)
                    if gr == 0:
                        pool.wait_ge(bcrep_landed, 64 * f + 64)
                    for j in range(J):
                        hk = h[:, at0 + j, :]
                        c_rep = bc_rep[:, at(f % 2, 1), J + j, :].rearrange("p o t -> p (o t)")
                        g.tensor_tensor(hk, hk, c_rep, ALU.mult).then_inc(hc_done, 1)
            walk(pool, body)

        @block.vector
        def _(dve):
            v = nc.vector
            def variances(part, lo, hi):
                for i in range(lo, hi):
                    if i % 8 == 0:
                        dve.wait_ge(x_in[i // 8], 16)
                    last = v.bn_stats(stats[:, i, :], x_all[:, i, :])
                last.then_inc(stats_done, 1)
                dve.wait_ge(stats_done, part + 1)
                for i in range(lo, hi):
                    last = v.bn_aggr(mv[:, i, :], stats[:, i, :])
                last.then_inc(aggr_done, 1)
                dve.wait_ge(aggr_done, part + 1)
                v.tensor_scalar(var_eps[:, lo:hi], mv[:, lo:hi, 1], EPS, None, ALU.add).then_inc(vareps_ready, 1)

            def inner_variances(part, lo, hi):
                dve.wait_ge(rstd_ready, part + 1)
                v.tensor_tensor(scale_n[:, lo:hi], mv[:, lo:hi, 1], rstd[:, lo:hi], ALU.mult).then_inc(ts_done, 1)
                dve.wait_ge(ts_done, 3 * part + 1)
                v.tensor_tensor(var2[:, lo:hi], scale_n[:, lo:hi], rstd[:, lo:hi], ALU.mult).then_inc(ts_done, 1)
                dve.wait_ge(ts_done, 3 * part + 2)
                v.tensor_scalar(var2[:, lo:hi], var2[:, lo:hi], EPS, None, ALU.add).then_inc(var2_ready, 1)
                v.tensor_scalar(scale_b[:, lo:hi], rstd[:, lo:hi], 1.0, None, ALU.add)
                v.scalar_tensor_tensor(out=shift_b[:, lo:hi], in0=mv[:, lo:hi, 0], scalar=-1.0, in1=rstd[:, lo:hi],
                                       op0=ALU.mult, op1=ALU.mult)

            def norm_factors(part, lo, hi):
                dve.wait_ge(rstd2_ready, part + 1)
                v.tensor_tensor(scale_n[:, lo:hi], rstd[:, lo:hi], rstd2[:, lo:hi], ALU.mult).then_inc(ts_done, 1)
                dve.wait_ge(ts_done, 3 * part + 3)
                v.scalar_tensor_tensor(out=shift_n[:, lo:hi], in0=mv[:, lo:hi, 0], scalar=-1.0, in1=scale_n[:, lo:hi],
                                       op0=ALU.mult, op1=ALU.mult).then_inc(norm_ready, 1)

            variances(0, 0, EARLY)
            inner_variances(0, 0, EARLY)
            norm_factors(0, 0, EARLY)
            dve.wait_ge(weights_in, 16 * WEIGHT_LOADS)
            v.tensor_scalar(conv_b_half[:, :], conv_b_half[:, :], 0.5, None, ALU.mult).then_inc(halfbias_ready, 1)
            dve.wait_ge(aneg_ready, 1)
            v.tensor_scalar(a_neg[:, :, :], a_neg[:, :, :], -1.0, None, ALU.mult).then_inc(aneg_ready, 1)
            variances(1, EARLY, BLOCKS)

            def chunk_copy(buf, n):
                return buf[:, at(n % UZ, 1), :, :].rearrange("p o h t -> p (o h t)")

            def silu_u(n):
                dve.wait_ge(uact_done, 2 * n + 2)
                v.scalar_tensor_tensor(out=chunk_copy(u, n), in0=chunk_copy(zg, n), scalar=1.0, in1=chunk_copy(u, n),
                                       op0=ALU.add, op1=ALU.mult).then_inc(u_ready, 1)

            def silu_z(n, banks=pa):
                for half in range(HALVES):
                    z = zg[:, at(n % UZ, 1), half, :].rearrange("p o t -> p (o t)")
                    dve.wait_ge(zact_done, 2 * n + half + 1)
                    v.scalar_tensor_tensor(out=z, in0=z, scalar=1.0, in1=banks[half][:, :],
                                           op0=ALU.add, op1=ALU.mult).then_inc(zg_done, 1)

            def log1p_error(n):
                dve.wait_ge(one_plus_ready, n + 1)
                dve.wait_ge(ln_ready, n + 1)
                v.scalar_tensor_tensor(out=delta[:, :, :], in0=delta[:, :, :], scalar=1.0, in1=ln[:, :, :],
                                       op0=ALU.subtract, op1=ALU.subtract).then_inc(g_ready, 1)

            def delta_u(n):
                dve.wait_ge(delta_ready, n + 1)
                v.tensor_tensor(w[:, at(n % 2, 1), :, :].rearrange("p o h t -> p (o h) t"), delta[:, :, :],
                                u[:, at(n % UZ, 1), :, :].rearrange("p o h t -> p (o h) t"), ALU.mult).then_inc(w_ready, 1)

            def gate(f, half):
                dve.wait_ge(nsum_done, 4 * f + 2 * half + 2)
                if half == 0 and (not isinstance(f, int) or f >= 1):
                    dve.wait_ge(op_done, f)
                v.scalar_tensor_tensor(out=yg[:, half, :], in0=y_ps[half][:, :], scalar=0.5,
                                       in1=zg[:, at(f % UZ, 1), half, :].rearrange("p o t -> p (o t)"),
                                       op0=ALU.mult, op1=ALU.mult).then_inc(yg_done, 1)

            def mul(f, k):
                gr, j = divmod(k, J)
                if j == 0:
                    dve.wait_ge(wrep_ready, G * f + gr + 1)
                if k == 0:
                    dve.wait_ge(bcrep_landed, 64 * f + 64)
                if not isinstance(f, int) or K * f + k >= 2:
                    dve.wait_ge(scan_done, K * f + k - 1)
                v.tensor_tensor(dbu[k % 2][:, :], w_ps[gr % 2][:, :],
                                bc_rep[:, at(f % 2, 1), j, :].rearrange("p o t -> p (o t)"),
                                ALU.mult).then_inc(mul_done, 1)

            def scan(f, k):
                gr, j = divmod(k, J)
                dve.wait_ge(exp_done, K * f + k + 1)
                dve.wait_ge(mul_done, K * f + k + 1)
                if k % 8 == 0 and (not isinstance(f, int) or 4 * f + k // 8 >= 2):
                    dve.wait_ge(nsum_done, 4 * f + k // 8 - 1)
                if j == 0 and (not isinstance(f, int) or f >= 1):
                    dve.wait_ge(carry_saved, K * f - K + J * gr + J)
                v.tensor_tensor_scan(h[:, k % H_RING, :], da[:, k % DA_RING, :], dbu[k % 2][:, :],
                                     carry[:, at(slot(f), 1), k], ALU.mult, ALU.add).then_inc(scan_done, 1)

            silu_u(0)
            inner_variances(1, EARLY, BLOCKS)
            norm_factors(1, EARLY, BLOCKS)
            dve.wait_ge(small_landed, 48)
            v.tensor_reduce(c_mean[:, :], small_in[:, 0, :], AX.X, ALU.add).then_inc(centred, 1)
            dve.wait_ge(centred, 1)
            v.tensor_scalar(c_mean[:, :], c_mean[:, :], 1.0 / DM, None, ALU.mult).then_inc(centred, 1)
            dve.wait_ge(centred, 2)
            v.tensor_scalar(small_in[:, 0, :], small_in[:, 0, :], c_mean[:, 0:1], None, ALU.subtract).then_inc(centred, 1)
            log1p_error(0)
            dve.wait_ge(g_ready, 1)
            v.tensor_tensor(delta[:, :, :], e[:, :, :], delta[:, :, :], ALU.subtract).then_inc(d1_done, 1)
            dve.wait_ge(d1_done, 1)
            v.tensor_tensor(delta[:, :, :], delta[:, :, :], relu[:, :, :], ALU.add).then_inc(delta_ready, 1)
            delta_u(0)
            silu_z(0, y_ps)
            dve.wait_ge(arep_mm, 1)
            for gr in range(G):
                for st in range(S):
                    src = dbu[0][DG * st:DG * st + DG, N * gr:N * gr + N].rearrange("p (j s) -> p j s", s=S)
                    last = v.tensor_copy(a_rep[DG * st:DG * st + DG, gr, :], src[:, :, st])
            last.then_inc(arep_ready, 1)
            silu_u(1)
            silu_z(1)

            def body(f, first, second, finish):
                for k in range(0, K, 2):
                    if second and k == 18:
                        log1p_error(f + 1)
                    if finish and k == 10:
                        gate(f - 1, 1)
                    if second and k == 26:
                        delta_u(f + 1)
                    if first and k == 24:
                        silu_u(f + 2)
                    if k == 26:
                        gate(f, 0)
                    if first and k == 28:
                        silu_z(f + 2)
                    mul(f, k)
                    mul(f, k + 1)
                    scan(f, k)
                    scan(f, k + 1)
            walk(dve, body)
            dve.wait_ge(x1_done, CHUNKS - 2)
            for i in range(SCORED):
                last = v.bn_stats(stats[:, i, :], x_all[:, i, :])
            last.then_inc(x1stats_done, 1)
            gate(CHUNKS - 1, 1)
            dve.wait_ge(x1stats_done, 1)
            for i in range(SCORED):
                v.bn_aggr(x1_mv[:, i, :], stats[:, i, :])

        @block.scalar
        def _(act):
            a = nc.scalar
            act.dma_start(win[:, :], in_proj_w).then_inc(weights_in, 16)
            act.dma_start(delta[:, :, :].rearrange("p h t -> p (h t)"),
                          conv_w.rearrange("(o d) k -> o (d k)", o=1).broadcast_to([P, DIN * TAPS])).then_inc(weights_in, 16)
            for dst, src in ((conv_b_half, conv_b), (dt_bias, dt_proj_b), (d_skip, D)):
                for half in range(HALVES):
                    act.dma_start(dst[:, half:half + 1], src[P * half:P * half + P].rearrange("(p o) -> p o", o=1))\
                       .then_inc(weights_in, 16)
            act.dma_start(a_log[:, :, :], A_log.rearrange("(h p) n -> p h n", p=P)).then_inc(weights_in, 16)
            act.dma_start(w_out[:, :, :], out_proj_w.rearrange("(h p) n -> p h n", p=P)).then_inc(weights_in, 16)
            act.dma_start(g_col[:, :], ln_g.rearrange("(p o) -> p o", o=1)).then_inc(weights_in, 16)
            act.dma_start(b_col[:, :], ln_b.rearrange("(p o) -> p o", o=1)).then_inc(weights_in, 16)
            for i, src in enumerate(small):
                act.dma_start(small_in[:, i, :], src).then_inc(small_landed, 16)
            act.wait_ge(weights_in, 16 * WEIGHT_LOADS)
            a.activation(a_neg[:, :, :], a_log[:, :, :], ACT.Exp).then_inc(aneg_ready, 1)

            def normalise(n):
                act.wait_ge(consts_ready, 1)
                act.wait_ge(norm_ready, 1 if isinstance(n, int) and n < 2 else 2)
                if not isinstance(n, int) or n >= 1:
                    act.wait_ge(tr_done, n)
                for b in range(CB):
                    i = n * CB + b
                    last = a.activation(xh[:, b, :], x_all[:, at(i, 1), :].rearrange("p o d -> p (o d)"), ACT.Identity,
                                        scale=scale_n[:, at(i, 1)], bias=shift_n[:, at(i, 1)])
                last.then_inc(xh_ready, 1)

            def norm_out(n):
                act.wait_ge(tr_done, n + 1)
                a.activation(xn_t[:, xn_cols(n, PAD)], pa[0][:, :], ACT.Identity, scale=g_col[:, :],
                             bias=b_col[:, :]).then_inc(xn_ready, 1)

            def tanh_u(n, half):
                pre = u[:, at(n % UZ, 1), half, :].rearrange("p o t -> p (o t)")
                th = zg[:, at(n % UZ, 1), half, :].rearrange("p o t -> p (o t)")
                act.wait_ge(consts_ready, 1)
                act.wait_ge(umm_done, 2 * n + half + 1)
                if not isinstance(n, int) or n >= UZ:
                    act.wait_ge(yg_done, 2 * (n - UZ) + half + 1)
                a.activation(pre, pa[1 - half][:, :], ACT.Identity, scale=0.5, bias=conv_b_half[:, half:half + 1])
                a.activation(th, pa[1 - half][:, :], ACT.Tanh, scale=0.5,
                             bias=conv_b_half[:, half:half + 1]).then_inc(uact_done, 1)

            def tanh_z(n, half, banks=pa):
                act.wait_ge(consts_ready, 1)
                act.wait_ge(zmm_done, 2 * n + half + 1)
                act.wait_ge(u_ready, n + 1)
                a.activation(zg[:, at(n % UZ, 1), half, :].rearrange("p o t -> p (o t)"), banks[half][:, :],
                             ACT.Tanh, scale=0.5).then_inc(zact_done, 1)

            def bc_out(n):
                act.wait_ge(xpmm_done, n + 1)
                if not isinstance(n, int) or n >= 1:
                    act.wait_ge(scr_written, 16 * n)
                    act.wait_ge(dmm_done, 2 * n)
                a.activation(bc[:, :], pa[1][:, :], ACT.Identity).then_inc(bc_ready, 1)

            def softplus_parts(n):
                for half in range(HALVES):
                    act.wait_ge(dmm_done, 2 * n + half + 1)
                    if half == 0 and (not isinstance(n, int) or n >= 1):
                        act.wait_ge(delta_ready, n)
                    a.activation(ln[:, half, :], pa[1 - half][:, :], ACT.Abs, bias=dt_bias[:, half:half + 1])
                    a.activation(relu[:, half, :], pa[1 - half][:, :], ACT.Relu,
                                 bias=dt_bias[:, half:half + 1]).then_inc(dact_done, 1)

            def softplus_logs(n):
                act.wait_ge(dact_done, 2 * n + 2)
                a.activation(e[:, :, :], ln[:, :, :], ACT.Exp, scale=-1.0).then_inc(e_ready, 1)
                act.wait_ge(e_ready, n + 1)
                if not isinstance(n, int) or n >= 1:
                    for gr in range(G):
                        act.wait_ge(drep_landed[gr], 16 * S * n)
                    act.wait_ge(w_ready, n)
                a.activation(delta[:, :, :], e[:, :, :], ACT.Identity, bias=1.0).then_inc(one_plus_ready, 1)
                a.activation(ln[:, :, :], e[:, :, :], ACT.Ln, bias=1.0).then_inc(ln_ready, 1)

            def base_out(f):
                if not isinstance(f, int) or f >= 1:
                    act.wait_ge(op_done, f)
                for b in range(CB):
                    i = f * CB + b
                    last = a.activation(base[:, b, :], x_all[:, at(i, 1), :].rearrange("p o d -> p (o d)"), ACT.Identity,
                                        scale=scale_b[:, at(i, 1)], bias=shift_b[:, at(i, 1)])
                last.then_inc(base_ready, 1)

            def skip(f, half):
                act.wait_ge(consts_ready, 1)
                if not isinstance(f, int) or f >= 1:
                    act.wait_ge(nsum_done, 4 * f - 2 + 2 * half)
                a.activation(du[:, half, :], u[:, at(f % UZ, 1), half, :].rearrange("p o t -> p (o t)"), ACT.Identity,
                             scale=d_skip[:, half:half + 1]).then_inc(du_ready, 1)

            def x1_out(f):
                act.wait_ge(consts_ready, 1)
                act.wait_ge(op_done, f + 1)
                a.activation(x_all[:, at(f * CB, CB), :], pa[1][:, :].rearrange("p (b d) -> p b d", b=CB),
                             ACT.Identity).then_inc(x1_done, 1)

            def exp_tile(f, k):
                gr, j = divmod(k, J)
                if j == 0:
                    act.wait_ge(drep_landed[gr], 16 * S * f + 16 * S)
                if not isinstance(f, int) or K * f + k >= DA_RING:
                    act.wait_ge(scan_done, K * f + k - DA_RING + 1)
                a.activation(da[:, k % DA_RING, :], delta_rep[:, gr, :], ACT.Exp,
                             scale=a_rep[:, gr, j:j + 1]).then_inc(exp_done, 1)

            normalise(0)
            norm_out(0)
            normalise(1)
            act.wait_ge(halfbias_ready, 1)
            tanh_u(0, 0)
            tanh_u(0, 1)
            bc_out(0)
            norm_out(1)
            softplus_parts(0)
            softplus_logs(0)
            tanh_z(0, 0, y_ps)
            tanh_z(0, 1, y_ps)
            tanh_u(1, 0)
            tanh_u(1, 1)
            act.wait_ge(small_mm, 1)
            a.activation(small_t[:, :, :].rearrange("p i e -> p (i e)"), y_ps[0][:, 0:3 * E], ACT.Identity).then_inc(small_ready, 1)
            tanh_z(1, 0)
            tanh_z(1, 1)
            act.wait_ge(arep_ready, 1)

            def score_out_step(m):
                if m < SCORED // 2:
                    act.wait_ge(xtr_done, m + 1)
                    if m >= 2:
                        act.wait_ge(score_mm, m - 1)
                    a.activation(x_t[:, m % 2, 0:2 * P], pa[0][:, 0:2 * P], ACT.Identity).then_inc(xt_ready, 1)
                else:
                    act.wait_ge(score_mm, SCORED // 2)
                    a.activation(score[:, 0:SCORED, :].rearrange("p b e -> p (b e)"),
                                 pa[0][:, SCORE_AT:SCORE_AT + SCORED * E], ACT.Identity).then_inc(score_out, 1)

            def turned_out(n):
                act.wait_ge(wtr_done, n + 1)
                stage = w2_stage if n < E else w1_stage
                a.activation(stage[:, n % E, :], pa[0][:, :], ACT.Identity).then_inc(wev_done, 1)

            def body(f, first, second, finish):
                for k in range(K):
                    exp_tile(f, k)
                    if first and k == 1:
                        normalise(f + 2)
                    if k == 7:
                        skip(f, 0)
                    if k == 19:
                        skip(f, 1)
                    if second and k == 6:
                        bc_out(f + 1)
                    if first and k == 6:
                        norm_out(f + 2)
                    if second and k == 8:
                        softplus_parts(f + 1)
                    if second and k == 16:
                        softplus_logs(f + 1)
                    if finish and k == (20 if first else 6):
                        base_out(f - 1)
                    if first and k == 16:
                        tanh_u(f + 2, 0)
                    if first and k == 24:
                        tanh_u(f + 2, 1)
                    if finish and k == 26:
                        x1_out(f - 1)
                    if first and k == 30:
                        tanh_z(f + 2, 0)
                        tanh_z(f + 2, 1)
                    if not first:
                        for gr in range(G):
                            for m in scored_in(f, gr):
                                if k == J * gr + (4 if gr < 3 else 7) + m % 3:
                                    score_out_step(m)
                            for n in turned_in(f, gr):
                                if k == min(J * gr + 8 + n % 2, K - 1):
                                    turned_out(n)
            walk(act, body)
            base_out(CHUNKS - 1)
            x1_out(CHUNKS - 1)

        @block.tensor
        def _(pe):
            t = nc.tensor

            def transpose_x(n):
                pe.wait_ge(xh_ready, n + 1)
                if isinstance(n, int) and n == 1:
                    pe.wait_ge(uact_done, 2)
                elif not isinstance(n, int) or n >= 2:
                    pe.wait_ge(zg_done, 2 * n - 1)
                for b in range(CB):
                    last = t.transpose(pa[0][:, P * b:P * b + P], xh[:, b, :], ident[:, :])
                last.then_inc(tr_done, 1)

            def project_u(n, half):
                pe.wait_ge(xn_ready, n + 1)
                if not isinstance(n, int) or n >= 1:
                    pe.wait_ge(dact_done, 2 * n + half - 1)
                for k in range(TAPS):
                    last = t.matmul(pa[1 - half][:, :], w_tap[:, k, P * half:P * half + P], xn_t[:, xn_cols(n, k)],
                                    start=(k == 0), stop=(k == TAPS - 1))
                last.then_inc(umm_done, 1)

            def project_z(n, banks=pa):
                pe.wait_ge(uact_done, 2 * n + 2)
                for half in range(HALVES):
                    if half == 1 and (not isinstance(n, int) or n >= 3):
                        pe.wait_ge(x1_done, n - 2)
                    t.matmul(banks[half][:, :], win[:, DIN + P * half:DIN + P * half + P], xn_t[:, xn_cols(n, PAD)],
                             start=True, stop=True).then_inc(zmm_done, 1)

            def project_bc_dt(n):
                pe.wait_ge(u_ready, n + 1)
                if not isinstance(n, int) or n >= 1:
                    pe.wait_ge(zg_done, 2 * n + 2)
                for half in range(HALVES):
                    last = t.matmul(pa[1][:, :], w_xproj[:, half, :],
                                    u[:, at(n % UZ, 1), half, :].rearrange("p o t -> p (o t)"),
                                    start=(half == 0), stop=(half == HALVES - 1))
                last.then_inc(xpmm_done, 1)

            def project_delta(n, first):
                pe.wait_ge(bc_ready, n + 1)
                for half in range(HALVES):
                    if half == 1 and first:
                        pe.wait_ge(xn_ready, n + 2)
                    t.matmul(pa[1 - half][:, :], w_dt[:, P * half:P * half + P], bc[:, :],
                             start=True, stop=True).then_inc(dmm_done, 1)

            def spread_w(f, gr):
                half, q = divmod(gr, Q)
                if gr == 0:
                    pe.wait_ge(w_ready, f + 1)
                if not isinstance(f, int) or f >= 1 or gr >= 2:
                    pe.wait_ge(mul_done, K * f + J * gr - J)
                t.matmul(w_ps[gr % 2][:, :], spread[:, q, :], w[:, at(f % 2, 1), half, :].rearrange("p o t -> p (o t)"),
                         start=True, stop=True).then_inc(wrep_ready, 1)

            def sum_states(f, pair):
                half = pair // 2
                pe.wait_ge(hc_done, K * f + 8 * pair + 8)
                if pair % 2 == 0:
                    if isinstance(f, int) and f == 0 and pair == 0:
                        pe.wait_ge(small_ready, 1)
                    pe.wait_ge(du_ready, 2 * f + half + 1)
                    if not isinstance(f, int) or f >= 1:
                        pe.wait_ge(yg_done, 2 * f - 1 + half)
                for q in (2 * (pair % 2), 2 * (pair % 2) + 1):
                    t.matmul(y_ps[half][DG * q:DG * q + DG, :], ident[:, DG * q:DG * q + DG], du[:, half, :],
                             start=True, stop=False)
                for j in range(J):
                    for i in range(2):
                        q = 2 * (pair % 2) + i
                        k = J * (2 * pair + i) + j
                        last = t.matmul(y_ps[half][DG * q:DG * q + DG, :], gather[:, :], h[:, k % H_RING, :],
                                        start=False, stop=(j == J - 1))
                last.then_inc(nsum_done, 1)

            def project_out(f):
                pe.wait_ge(base_ready, f + 1)
                pe.wait_ge(yg_done, 2 * f + 2)
                for b in range(CB):
                    t.matmul(pa[1][:, P * b:P * b + P], ident[:, :], base[:, b, :], start=True, stop=False)
                    for half in range(HALVES):
                        last = t.matmul(pa[1][:, P * b:P * b + P], yg[:, half, P * b:P * b + P], w_out[:, half, :],
                                        start=False, stop=(half == HALVES - 1))
                last.then_inc(op_done, 1)

            pe.wait_ge(consts_ready, 1)
            transpose_x(0)
            pe.wait_ge(wtap_ready, 1)
            project_u(0, 0)
            project_u(0, 1)
            project_bc_dt(0)
            transpose_x(1)
            project_delta(0, first=True)
            project_z(0, y_ps)
            pe.wait_ge(aneg_ready, 2)
            for gr in range(G):
                last = t.matmul(dbu[0][:, N * gr:N * gr + N], spread[:, gr % Q, :], a_neg[:, gr // Q, :], start=True, stop=True)
            last.then_inc(arep_mm, 1)
            project_u(1, 0)
            project_u(1, 1)
            pe.wait_ge(small_landed, 48)
            pe.wait_ge(centred, 3)
            pe.wait_ge(zg_done, 2)
            for i in range(3):
                last = t.transpose(y_ps[0][:, E * i:E * i + E], small_in[:, i, :], ident[0:E, 0:E])
            last.then_inc(small_mm, 1)
            spread_w(0, 0)
            project_z(1)

            def score_step(m):
                if m:
                    pe.wait_ge(xt_ready, m)
                    for b in range(2):
                        i = 2 * (m - 1) + b
                        last = t.matmul(pa[0][:, SCORE_AT + E * i:SCORE_AT + E * i + E], x_t[:, (m - 1) % 2, P * b:P * b + P],
                                        small_t[:, 0, :], start=True, stop=True)
                    last.then_inc(score_mm, 1)
                else:
                    pe.wait_ge(wev_done, E)
                    pe.wait_ge(x1_done, CHUNKS - 2)
                if m < SCORED // 2:
                    for b in range(2):
                        last = t.transpose(pa[0][:, P * b:P * b + P], x_all[:, 2 * m + b, :], ident[:, :])
                    last.then_inc(xtr_done, 1)

            def turn(n):
                if n == 0:
                    pe.wait_ge(w2_in, 16)
                    pe.wait_ge(dact_done, 2 * CHUNKS)
                elif n == E:
                    pe.wait_ge(w1_in, 16)
                    pe.wait_ge(score_out, 1)
                else:
                    pe.wait_ge(wev_done, n)
                stage = w2_stage if n < E else w1_stage
                for c in range(FC):
                    last = t.transpose(pa[0][:, P * c:P * c + P], stage[:, n % E, P * c:P * c + P], ident[:, :])
                last.then_inc(wtr_done, 1)

            def body(f, first, second, finish):
                for gr in range(G):
                    if gr + 1 < G:
                        spread_w(f, gr + 1)
                    elif second:
                        spread_w(f + 1, 0)
                    if second and gr == 0:
                        project_bc_dt(f + 1)
                        if first:
                            transpose_x(f + 2)
                        project_delta(f + 1, first)
                    if finish and gr == 1:
                        sum_states(f - 1, 3)
                    if first and gr == 2:
                        project_u(f + 2, 0)
                    if first and gr == 4:
                        project_u(f + 2, 1)
                    if finish and gr == 4:
                        if first:
                            pe.wait_ge(uact_done, 2 * f + 5)
                        elif second:
                            pe.wait_ge(dact_done, 2 * f + 3)
                        else:
                            pe.wait_ge(x1_done, f - 1)
                        project_out(f - 1)
                    if gr >= 3 and gr % 2:
                        sum_states(f, (gr - 3) // 2)
                    if first and gr == 6:
                        project_z(f + 2)
                    if not first:
                        for m in scored_in(f, gr):
                            score_step(m)
                        for n in turned_in(f, gr):
                            turn(n)
            walk(pe, body)
            sum_states(CHUNKS - 1, 3)
            pe.wait_ge(x1_done, CHUNKS - 1)
            project_out(CHUNKS - 1)


def expert_layer(nc, x_ext, small_t, score, x1_mv, SCORED, W1, b1, W2, b2, w1_turned, w2_turned, x_rows, out):
    F32, I32, BF16 = mybir.dt.float32, mybir.dt.int32, mybir.dt.bfloat16
    U32 = mybir.dt.uint32
    E, F, D = W1.shape
    BLOCKS = x_ext.shape[1]
    T = BLOCKS * P
    EXT = x_ext.shape[2]
    MEAN, SCALE_N, SCALE_B, SHIFT_B, ALPHA = range(D, D + 5)
    MAX_TILES = (T + E * (P - 1)) // P
    FC = F // P
    W1_AT, W2_AT, B2_AT = 0, F, 2 * F
    B1_AT = B2_AT + D
    GAMMA_AT, BETA_AT = B1_AT + FC, B1_AT + FC + 1
    REC = BETA_AT + 1
    CB = 512 // P
    CHUNKS = BLOCKS // CB
    UNUSED = 2 * T
    RING = 8
    AHEAD = 6
    IndexOn = bass.IndirectOffsetOnAxis

    with ExitStack() as ctx:
        def sb(name, shape, dt=F32):
            return ctx.enter_context(nc.sbuf_tensor(name, shape, dt))

        def sem(name):
            return ctx.enter_context(nc.semaphore(name))

        record = sb("record", [P, E, REC])
        now = sb("now", [P, RING, REC])
        b1_in = sb("b1_in", [E * FC, P])
        f_ident = sb("f_ident", [P, P])
        before = sb("before", [P, P])
        ones = sb("ones", [P, P])
        io_e = sb("io_e", [P, E], I32)
        io_b = sb("io_b", [P, BLOCKS], I32)
        io_j = sb("io_j", [P, MAX_TILES], I32)
        io_p = sb("io_p", [P, P], I32)
        io_q = sb("io_q", [P, 1], I32)
        io_c = sb("io_c", [P, BLOCKS], I32)
        e_of = sb("e_of", [P, E])
        rows_of = sb("rows_of", [P, BLOCKS])
        tile_of = sb("tile_of", [P, MAX_TILES])
        place_of = sb("place_of", [P, P], BF16)
        part_of = sb("part_of", [P, 1])
        block_of = sb("block_of", [P, BLOCKS])
        f_stats = sb("f_stats", [P, BLOCKS, 6])
        f_var = sb("f_var", [P, BLOCKS])
        f_var2 = sb("f_var2", [P, BLOCKS])
        f_half = sb("f_half", [P, BLOCKS])
        f_rstd = sb("f_rstd", [P, BLOCKS])
        f_rstd2 = sb("f_rstd2", [P, BLOCKS])
        x_t = sb("x_t", [P, 2, CB * P])
        best = sb("best", [P, BLOCKS])
        less = sb("less", [P, BLOCKS, E])
        first = sb("first", [P, BLOCKS])
        onehot = sb("onehot", [P, BLOCKS, E])
        neg_exp = sb("neg_exp", [P, BLOCKS])
        block_count = sb("block_count", [P, E, BLOCKS])
        upto = sb("upto", [P, E, BLOCKS])
        more = sb("more", [P, E, BLOCKS])
        tiles = sb("tiles", [P, E])
        tiles_upto = sb("tiles_upto", [P, E])
        start = sb("start", [P, E])
        offset = sb("offset", [P, E, BLOCKS])
        place = sb("place", [P, BLOCKS, E])
        slot_f = sb("slot_f", [P, BLOCKS])
        tile_at = sb("tile_at", [P, BLOCKS])
        place_at = sb("place_at", [P, BLOCKS], BF16)
        is_place = sb("is_place", [P, BLOCKS, P], BF16)
        is_tile = sb("is_tile", [P, BLOCKS, MAX_TILES])
        carried = sb("carried", [P, BLOCKS, 2, MAX_TILES], BF16)
        parts = sb("parts", [P, 2, MAX_TILES])
        id_f = sb("id_f", [P, MAX_TILES])
        id_in_f = sb("id_in_f", [P, MAX_TILES])
        id_out = sb("id_out", [P, MAX_TILES], U32)
        id_in = sb("id_in", [P, MAX_TILES], U32)
        passed = sb("passed", [P, MAX_TILES, E])
        expert_f = sb("expert_f", [P, MAX_TILES])
        expert_i = sb("expert_i", [P, MAX_TILES], I32)
        rows = sb("rows", [P, RING, EXT])
        xhat = sb("xhat", [P, 2, D])
        xhat_t = sb("xhat_t", [P, 2, P])
        hidden_t = sb("hidden_t", [P, 2, F])
        base2 = sb("base2", [P, 2, D])
        y2 = sb("y2", [P, 2, D])
        done_rows = sb("done_rows", [P, RING, D])
        bk = [ctx.enter_context(nc.psum_tensor(f"f_bank{i}", [P, 512], F32)) for i in range(8)]

        weights_landed = sem("f_weights_landed")
        alpha_ready = sem("f_alpha_ready")
        b1_landed = sem("f_b1_landed")
        setup_done = sem("f_setup_done")
        consts_done = sem("f_consts_done")
        smallt_ready = sem("f_smallt_ready")
        fst_done = sem("f_fst_done")
        fmv_done = sem("f_fmv_done")
        fvar_done = sem("f_fvar_done")
        frstd_done = sem("f_frstd_done")
        fv1 = sem("f_fv1")
        fvar2_done = sem("f_fvar2_done")
        frstd2_done = sem("f_frstd2_done")
        fscale_done = sem("f_fscale_done")
        fsn_done = sem("f_fsn_done")
        best_ready = sem("f_best_ready")
        ftr_done = sem("f_ftr_done")
        ftev_done = sem("f_ftev_done")
        score_done = sem("f_score_done")
        route = sem("f_route")
        onehot_ready = sem("f_onehot_ready")
        prefix_done = sem("f_prefix_done")
        expert_ready = sem("f_expert_ready")
        negexp_done = sem("f_negexp_done")
        b1t_done = sem("f_b1t_done")
        b1t_ready = sem("f_b1t_ready")
        ext_written = sem("f_ext_written")
        place_ready = sem("f_place_ready")
        place_step = sem("f_place_step")
        is_tile_ready = sem("f_is_tile_ready")
        parts_carried = sem("f_parts_carried")
        blocks_carried = sem("f_blocks_carried")
        ids_mm = sem("f_ids_mm")
        ids_ready = sem("f_ids_ready")
        rows_in = [sem(f"f_rows_in{i}") for i in range(RING)]
        now_in = [sem(f"f_now_in{i}") for i in range(RING)]
        out_written = [sem(f"f_out_written{i}") for i in range(RING)]
        up0_done = sem("f_up0_done")
        up1_done = sem("f_up1_done")
        relu0_done = sem("f_relu0_done")
        relu1_done = sem("f_relu1_done")
        xhat_ready = sem("f_xhat_ready")
        xt_done = sem("f_xt_done")
        xtev_done = sem("f_xtev_done")
        mm2_done = sem("f_mm2_done")
        base2_ready = sem("f_base2_ready")
        y2_ready = sem("f_y2_ready")
        done_ready = sem("f_done_ready")

        block = ctx.enter_context(nc.Block())
        N_T = MAX_TILES

        def walk_tiles(eng, step):
            for i in range(RING):
                step(i, i)
            rounds = (N_T - 2) // RING
            with eng.Fori(1, rounds) as k:
                for u in range(RING):
                    step(RING * k + u, u)
            for i in range(RING * rounds, N_T):
                step(i, i % RING)

        def e_at(reg):
            return bass.ds(reg, 1)

        @block.sync
        def _(sp):
            sp.dma_start(b1_in[:, :], b1.rearrange("e (c p) -> (e c) p", p=P)).then_inc(b1_landed, 16)
            sp.wait_ge(b1_landed, 16)
            sp.dma_start(record[:, :, W1_AT:W1_AT + F], w1_turned).then_inc(weights_landed, 16)
            sp.dma_start(record[:, :, W2_AT:W2_AT + F], w2_turned).then_inc(weights_landed, 16)
            sp.dma_start(record[:, :, B2_AT:B2_AT + D],
                         b2.rearrange("(o e) d -> o e d", o=1).broadcast_to([P, E, D])).then_inc(weights_landed, 16)
            sp.wait_ge(fscale_done, 4)
            sp.wait_ge(fsn_done, 2)
            sp.wait_ge(alpha_ready, 1)
            for i in range(0, BLOCKS, 8):
                sp.dma_start(x_rows[P * i:P * (i + 8), :].rearrange("(b p) d -> p b d", p=P), x_ext[:, i:i + 8, :])\
                  .then_inc(ext_written, 16)
            sp.wait_ge(expert_ready, 1)
            sp.wait_ge(weights_landed, 48)
            sp.wait_ge(smallt_ready, 1)
            sp.wait_ge(b1t_ready, 1)

            def copy_record(i, u):
                sp.wait_ge(consts_done, 1)
                if not isinstance(i, int) or i >= RING:
                    sp.wait_ge(done_ready, i - RING + 1)
                e = sp.value_load(expert_i[0:1, e_at(i)], min_val=0, max_val=E - 1)
                sp.dma_start(now[:, u, :], record[:, e_at(e), :].rearrange("p o f -> p (o f)")).then_inc(now_in[u], 16)
            walk_tiles(sp, copy_record)
            for u in range(RING):
                sp.wait_ge(out_written[u], 16 * len(range(u, N_T, RING)))

        @block.gpsimd
        def _(pool):
            g = nc.gpsimd
            g.memset(f_half[:, :], -0.5)
            g.memset(f_ident[:, :], 0.0)
            g.memset(before[:, :], 1.0)
            g.memset(ones[:, :], 1.0)
            g.iota(io_e[:, :], [[1, E]], base=0, channel_multiplier=0)
            g.iota(io_b[:, :], [[P, BLOCKS]], base=0, channel_multiplier=0)
            g.iota(io_j[:, :], [[1, MAX_TILES]], base=0, channel_multiplier=0)
            g.iota(io_p[:, :], [[1, P]], base=0, channel_multiplier=0)
            g.iota(io_q[:, :], [[0, 1]], base=0, channel_multiplier=1)
            g.iota(io_c[:, :], [[1, BLOCKS]], base=-UNUSED // P, channel_multiplier=0).then_inc(setup_done, 1)
            pool.wait_ge(setup_done, 1)
            g.affine_select(out=f_ident[:, :], in_=f_ident[:, :], compare_op=ALU.not_equal, fill=1.0, base=0,
                            pattern=[[-1, P]], channel_multiplier=1)
            g.affine_select(out=before[:, :], in_=before[:, :], compare_op=ALU.is_gt, fill=0.0, base=0,
                            pattern=[[1, P]], channel_multiplier=-1).then_inc(consts_done, 1)
            for part in range(2):
                some = slice(BLOCKS // 2 * part, BLOCKS // 2 * (part + 1))
                pool.wait_ge(fvar_done, part + 1)
                g.tensor_tensor(f_rstd[:, some], f_var[:, some], f_half[:, some], ALU.pow).then_inc(frstd_done, 1)
            for part in range(2):
                some = slice(BLOCKS // 2 * part, BLOCKS // 2 * (part + 1))
                pool.wait_ge(fvar2_done, part + 1)
                g.tensor_tensor(f_rstd2[:, some], f_var2[:, some], f_half[:, some], ALU.pow).then_inc(frstd2_done, 1)
            pool.wait_ge(is_tile_ready, 1)
            g.tensor_tensor(carried[:, :, 1, :], is_tile[:, :, :],
                            block_of[:, :].unsqueeze(2).broadcast_to([P, BLOCKS, MAX_TILES]), ALU.mult)\
             .then_inc(blocks_carried, 1)

            def gather_rows(i):
                u = i % RING
                if i >= RING:
                    pool.wait_ge(done_ready, i - RING + 1)
                g.indirect_dma_start(out=rows[:, u, :], out_offset=None, in_=x_rows,
                                     in_offset=IndexOn(id_in[:, i:i + 1], 0)).then_inc(rows_in[u], 16)

            pool.wait_ge(ids_ready, 1)
            pool.wait_ge(ext_written, 16 * (BLOCKS // 8))
            for i in range(AHEAD):
                gather_rows(i)
            for i in range(N_T):
                if i + AHEAD < N_T:
                    gather_rows(i + AHEAD)
                pool.wait_ge(done_ready, i + 1)
                g.indirect_dma_start(out=out, out_offset=IndexOn(id_out[:, i:i + 1], 0),
                                     in_=done_rows[:, i % RING, :], in_offset=None, bounds_check=T - 1,
                                     oob_is_err=False).then_inc(out_written[i % RING], 16)

        @block.vector
        def _(dve):
            v = nc.vector
            halves = [slice(BLOCKS // 2 * part, BLOCKS // 2 * (part + 1)) for part in range(2)]
            for i in range(SCORED, BLOCKS):
                last = v.bn_stats(f_stats[:, i, :], x_ext[:, i, 0:D])
            last.then_inc(fst_done, 1)
            dve.wait_ge(fst_done, 1)
            for i in range(SCORED, BLOCKS):
                last = v.bn_aggr(x1_mv[:, i, :], f_stats[:, i, :])
            last.then_inc(fmv_done, 1)
            dve.wait_ge(fmv_done, 1)
            for part, some in enumerate(halves):
                v.tensor_scalar(f_var[:, some], x1_mv[:, some, 1], EPS, None, ALU.add).then_inc(fvar_done, 1)
                v.tensor_copy(x_ext[:, some, MEAN], x1_mv[:, some, 0])
            dve.wait_ge(setup_done, 1)
            v.tensor_copy(e_of[:, :], io_e[:, :])
            v.tensor_copy(rows_of[:, :], io_b[:, :])
            v.tensor_copy(place_of[:, :], io_p[:, :])
            v.tensor_copy(part_of[:, :], io_q[:, :])
            v.tensor_copy(block_of[:, :], io_c[:, :])
            v.tensor_copy(tile_of[:, :], io_j[:, :]).then_inc(route, 1)

            steps = [1]

            def then(ins):
                steps[0] += 1
                ins.then_inc(route, 1)
                dve.wait_ge(route, steps[0])

            def over_blocks(ap):
                return ap.unsqueeze(1).broadcast_to([P, BLOCKS, E])

            def over_experts(ap, n):
                return ap.unsqueeze(2).broadcast_to([P, n, E])

            dve.wait_ge(score_done, CHUNKS - SCORED // CB)
            dve.wait_ge(route, 1)
            then(v.tensor_copy(score[:, SCORED:, :].rearrange("p b e -> p (b e)"), bk[6][:, SCORED * E:BLOCKS * E]))
            then(v.tensor_reduce(best[:, :], score[:, :, :], AX.X, ALU.max))
            then(v.tensor_tensor(less[:, :, :], score[:, :, :], over_experts(best[:, :], BLOCKS), ALU.is_lt))
            then(v.scalar_tensor_tensor(out=less[:, :, :], in0=less[:, :, :], scalar=float(E), in1=over_blocks(e_of[:, :]),
                                        op0=ALU.mult, op1=ALU.add))
            then(v.tensor_reduce(first[:, :], less[:, :, :], AX.X, ALU.min))
            v.tensor_tensor(onehot[:, :, :], over_blocks(e_of[:, :]), over_experts(first[:, :], BLOCKS),
                            ALU.is_equal).then_inc(onehot_ready, 1)
            for part, some in enumerate(halves):
                dve.wait_ge(frstd_done, part + 1)
                v.tensor_tensor(f_var2[:, some], x1_mv[:, some, 1], f_rstd[:, some], ALU.mult).then_inc(fv1, 1)
                v.tensor_scalar(x_ext[:, some, SCALE_B], f_rstd[:, some], 1.0, None, ALU.add).then_inc(fscale_done, 1)
                v.scalar_tensor_tensor(out=x_ext[:, some, SHIFT_B], in0=x1_mv[:, some, 0], scalar=-1.0, in1=f_rstd[:, some],
                                       op0=ALU.mult, op1=ALU.mult).then_inc(fscale_done, 1)
                dve.wait_ge(fv1, 2 * part + 1)
                v.tensor_tensor(f_var2[:, some], f_var2[:, some], f_rstd[:, some], ALU.mult).then_inc(fv1, 1)
                dve.wait_ge(fv1, 2 * part + 2)
                v.tensor_scalar(f_var2[:, some], f_var2[:, some], EPS, None, ALU.add).then_inc(fvar2_done, 1)
            v.tensor_tensor(neg_exp[:, :], best[:, :], f_rstd[:, :], ALU.mult).then_inc(best_ready, 1)
            dve.wait_ge(prefix_done, 2)
            then(v.tensor_copy(block_count[:, :, :], bk[5][:, 0:BLOCKS * E].rearrange("p (b e) -> p e b", e=E)))
            for e in range(E):
                last = v.tensor_tensor_scan(upto[:, e, :], ones[:, 0:BLOCKS], block_count[:, e, :], 0.0, ALU.mult, ALU.add)
            then(last)
            then(v.tensor_tensor(more[:, :, :], upto[:, :, BLOCKS - 1:BLOCKS].broadcast_to([P, E, BLOCKS]),
                                 rows_of[:, :].unsqueeze(1).broadcast_to([P, E, BLOCKS]), ALU.is_gt))
            then(v.tensor_reduce(tiles[:, :], more[:, :, :], AX.X, ALU.add))
            then(v.tensor_tensor_scan(tiles_upto[:, :], ones[:, 0:E], tiles[:, :], 0.0, ALU.mult, ALU.add))
            then(v.tensor_tensor(start[:, :], tiles_upto[:, :], tiles[:, :], ALU.subtract))
            then(v.tensor_scalar(start[:, :], start[:, :], float(P), None, ALU.mult))
            dve.wait_ge(negexp_done, 1)
            then(v.tensor_scalar(neg_exp[:, :], neg_exp[:, :], 1.0, None, ALU.add))
            v.reciprocal(x_ext[:, :, ALPHA], neg_exp[:, :]).then_inc(alpha_ready, 1)
            then(v.tensor_tensor(offset[:, :, :], upto[:, :, :], block_count[:, :, :], ALU.subtract))
            then(v.tensor_tensor(offset[:, :, :], offset[:, :, :], start[:, :].unsqueeze(2).broadcast_to([P, E, BLOCKS]), ALU.add))
            then(v.tensor_tensor(place[:, :, :], bk[4][:, 0:BLOCKS * E].rearrange("p (b e) -> p b e", e=E),
                                 offset[:, :, :].rearrange("p e b -> p b e"), ALU.add))
            then(v.tensor_tensor(place[:, :, :], place[:, :, :], onehot[:, :, :], ALU.mult))
            then(v.tensor_reduce(slot_f[:, :], place[:, :, :], AX.X, ALU.add))
            for part, some in enumerate(halves):
                dve.wait_ge(frstd2_done, part + 1)
                v.tensor_tensor(x_ext[:, some, SCALE_N], f_rstd[:, some], f_rstd2[:, some], ALU.mult).then_inc(fsn_done, 1)
            then(v.tensor_scalar(tile_at[:, :], slot_f[:, :], 1.0 / P, (1 - P) / (2 * P), ALU.mult, ALU.add))
            then(v.tensor_scalar(tile_at[:, :], tile_at[:, :], float(3 << 22), float(3 << 22), ALU.add, ALU.subtract))
            v.scalar_tensor_tensor(out=place_at[:, :], in0=tile_at[:, :], scalar=-float(P), in1=slot_f[:, :],
                                   op0=ALU.mult, op1=ALU.add).then_inc(place_step, 1)
            v.tensor_tensor(is_tile[:, :, :], tile_of[:, :].unsqueeze(1).broadcast_to([P, BLOCKS, MAX_TILES]),
                            tile_at[:, :].unsqueeze(2).broadcast_to([P, BLOCKS, MAX_TILES]), ALU.is_equal)\
             .then_inc(is_tile_ready, 1)
            dve.wait_ge(is_tile_ready, 1)
            v.tensor_scalar(carried[:, :, 0, :], is_tile[:, :, :], part_of[:, 0:1], None, ALU.mult).then_inc(parts_carried, 1)
            dve.wait_ge(place_step, 1)
            for i in range(0, BLOCKS, 8):
                v.tensor_tensor(is_place[:, i:i + 8, :], place_of[:, :].unsqueeze(1).broadcast_to([P, 8, P]),
                                place_at[:, i:i + 8].unsqueeze(2).broadcast_to([P, 8, P]), ALU.is_equal)\
                 .then_inc(place_ready, 1)
            dve.wait_ge(ids_mm, 1)
            then(v.tensor_copy(parts[:, :, :].rearrange("p o j -> p (o j)"), bk[6][:, 0:2 * MAX_TILES]))
            then(v.scalar_tensor_tensor(out=id_f[:, :], in0=parts[:, 1, :], scalar=float(P), in1=parts[:, 0, :],
                                        op0=ALU.mult, op1=ALU.add))
            then(v.tensor_scalar(id_f[:, :], id_f[:, :], float(UNUSED), None, ALU.add))
            then(v.tensor_scalar(id_in_f[:, :], id_f[:, :], float(T - 1), None, ALU.min))
            v.tensor_copy(id_out[:, :], id_f[:, :])
            v.tensor_copy(id_in[:, :], id_in_f[:, :]).then_inc(ids_ready, 1)
            then(v.tensor_tensor(passed[:, :, :], tiles_upto[:, :].unsqueeze(1).broadcast_to([P, MAX_TILES, E]),
                                 over_experts(tile_of[:, :], MAX_TILES), ALU.is_le))
            then(v.tensor_reduce(expert_f[:, :], passed[:, :, :], AX.X, ALU.add))
            then(v.tensor_scalar(expert_f[:, :], expert_f[:, :], float(E - 1), None, ALU.min))
            v.tensor_copy(expert_i[:, :], expert_f[:, :]).then_inc(expert_ready, 1)

            def normalise(i, u):
                dve.wait_ge(rows_in[u], 16 * (i // RING) + 16)
                if not isinstance(i, int) or i >= 2:
                    dve.wait_ge(xt_done, i - 1)
                v.tensor_scalar(xhat[:, u % 2, :], rows[:, u, 0:D], rows[:, u, MEAN:MEAN + 1], rows[:, u, SCALE_N:SCALE_N + 1],
                                ALU.subtract, ALU.mult).then_inc(xhat_ready, 1)

            def relu(i, u):
                dve.wait_ge(up1_done, i + 1)
                if not isinstance(i, int) or i >= 2:
                    dve.wait_ge(mm2_done, i - 1)
                for c in range(FC // 2, FC):
                    last = v.tensor_scalar(hidden_t[:, u % 2, P * c:P * c + P], bk[4 + u % 2][:, P * (c % 2):P * (c % 2) + P],
                                           now[:, u, B1_AT + c:B1_AT + c + 1], 0.0, ALU.add, ALU.max)
                last.then_inc(relu1_done, 1)

            def finish(i, u):
                dve.wait_ge(mm2_done, i + 1)
                v.tensor_tensor(y2[:, u % 2, :], bk[6 + u % 2][:, 0:D], now[:, u, B2_AT:B2_AT + D],
                                ALU.add).then_inc(y2_ready, 1)
                dve.wait_ge(y2_ready, i + 1)
                dve.wait_ge(base2_ready, i + 1)
                if not isinstance(i, int) or i >= RING:
                    dve.wait_ge(out_written[u], 16 * (i // RING))
                v.scalar_tensor_tensor(out=done_rows[:, u, :], in0=y2[:, u % 2, :], scalar=rows[:, u, ALPHA:ALPHA + 1],
                                       in1=base2[:, u % 2, :], op0=ALU.mult, op1=ALU.add).then_inc(done_ready, 1)

            def step(i, u):
                relu(i, u)
                if not isinstance(i, int) or i + 2 < N_T:
                    normalise(i + 2, (u + 2) % RING)
                if not isinstance(i, int) or i >= 1:
                    finish(i - 1, (u - 1) % RING)
            normalise(0, 0)
            normalise(1, 1)
            walk_tiles(dve, step)
            finish(N_T - 1, (N_T - 1) % RING)

        @block.scalar
        def _(act):
            a = nc.scalar
            a.activation(record[:, :, GAMMA_AT], small_t[:, 1, :], ACT.Identity)
            a.activation(record[:, :, BETA_AT], small_t[:, 2, :], ACT.Identity).then_inc(smallt_ready, 1)
            for c in range(CHUNKS - SCORED // CB):
                act.wait_ge(ftr_done, c + 1)
                if c >= 2:
                    act.wait_ge(score_done, c - 1)
                a.activation(x_t[:, c % 2, :], bk[4 + c % 2][:, :], ACT.Identity).then_inc(ftev_done, 1)
            act.wait_ge(b1t_done, 1)
            a.activation(record[:, :, B1_AT:B1_AT + FC], bk[3][:, 0:E * FC].rearrange("p (e c) -> p e c", e=E), ACT.Identity)\
             .then_inc(b1t_ready, 1)
            act.wait_ge(best_ready, 1)
            a.activation(neg_exp[:, :], neg_exp[:, :], ACT.Exp, scale=-1.0).then_inc(negexp_done, 1)

            def to_columns(i, u):
                act.wait_ge(xt_done, i + 1)
                if not isinstance(i, int) or i >= 2:
                    act.wait_ge(up1_done, i - 1)
                act.wait_ge(now_in[u], 16 * (i // RING) + 16)
                a.activation(xhat_t[:, u % 2, :], bk[u % 2][:, 0:P], ACT.Identity, scale=now[:, u, GAMMA_AT:GAMMA_AT + 1],
                             bias=now[:, u, BETA_AT:BETA_AT + 1]).then_inc(xtev_done, 1)

            def residual(i, u):
                act.wait_ge(rows_in[u], 16 * (i // RING) + 16)
                if not isinstance(i, int) or i >= 2:
                    act.wait_ge(done_ready, i - 1)
                a.activation(base2[:, u % 2, :], rows[:, u, 0:D], ACT.Identity,
                             scale=rows[:, u, SCALE_B:SCALE_B + 1], bias=rows[:, u, SHIFT_B:SHIFT_B + 1]).then_inc(base2_ready, 1)

            def relu(i, u):
                act.wait_ge(up0_done, i + 1)
                if not isinstance(i, int) or i >= 2:
                    act.wait_ge(mm2_done, i - 1)
                for c in range(FC // 2):
                    last = a.activation(hidden_t[:, u % 2, P * c:P * c + P], bk[2 + u % 2][:, P * c:P * c + P], ACT.Relu,
                                        bias=now[:, u, B1_AT + c:B1_AT + c + 1])
                last.then_inc(relu0_done, 1)

            def step(i, u):
                relu(i, u)
                if not isinstance(i, int) or i + 1 < N_T:
                    to_columns(i + 1, (u + 1) % RING)
                residual(i, u)
            to_columns(0, 0)
            walk_tiles(act, step)

        @block.tensor
        def _(pe):
            t = nc.tensor
            pe.wait_ge(consts_done, 1)
            REST = CHUNKS - SCORED // CB

            def score_blocks(c):
                pe.wait_ge(ftev_done, c + 1)
                for b in range(CB):
                    i = SCORED + CB * c + b
                    last = t.matmul(bk[6][:, E * i:E * i + E], x_t[:, c % 2, P * b:P * b + P], small_t[:, 0, :],
                                    start=True, stop=True)
                last.then_inc(score_done, 1)

            for c in range(REST):
                if c >= 2:
                    pe.wait_ge(ftev_done, c - 1)
                for b in range(CB):
                    last = t.transpose(bk[4 + c % 2][:, P * b:P * b + P], x_ext[:, SCORED + CB * c + b, 0:D], f_ident[:, :])
                last.then_inc(ftr_done, 1)
                if c:
                    score_blocks(c - 1)
            score_blocks(REST - 1)
            pe.wait_ge(b1_landed, 16)
            t.transpose(bk[3][:, 0:E * FC], b1_in[:, :], f_ident[0:E * FC, 0:E * FC]).then_inc(b1t_done, 1)
            pe.wait_ge(onehot_ready, 1)
            flat = onehot[:, :, :].rearrange("p b e -> p (b e)")
            t.matmul(bk[4][:, 0:BLOCKS * E], before[:, :], flat, start=True, stop=True).then_inc(prefix_done, 1)
            t.matmul(bk[5][:, 0:BLOCKS * E], ones[:, :], flat, start=True, stop=True).then_inc(prefix_done, 1)
            pe.wait_ge(parts_carried, 1)
            pe.wait_ge(blocks_carried, 1)
            for i in range(BLOCKS):
                if i % 8 == 0:
                    pe.wait_ge(place_ready, i // 8 + 1)
                last = t.matmul(bk[6][:, 0:2 * MAX_TILES], is_place[:, i, :], carried[:, i, :, :].rearrange("p o j -> p (o j)"),
                                start=(i == 0), stop=(i == BLOCKS - 1))
            last.then_inc(ids_mm, 1)
            pe.wait_ge(ids_ready, 1)

            def rows_t(i, u):
                pe.wait_ge(xhat_ready, i + 1)
                if not isinstance(i, int) or i >= 2:
                    pe.wait_ge(xtev_done, i - 1)
                t.transpose(bk[u % 2][:, 0:P], xhat[:, u % 2, :], f_ident[:, :]).then_inc(xt_done, 1)

            def up(i, u):
                pe.wait_ge(now_in[u], 16 * (i // RING) + 16)
                pe.wait_ge(xtev_done, i + 1)
                for half, (read, done) in enumerate(((relu0_done, up0_done), (relu1_done, up1_done))):
                    if not isinstance(i, int) or i >= 2:
                        pe.wait_ge(read, i - 1)
                    for c in range(FC // 2):
                        f0 = (FC // 2 * half + c) * P
                        last = t.matmul(bk[2 + 2 * half + u % 2][:, P * c:P * c + P],
                                        now[:, u, W1_AT + f0:W1_AT + f0 + P], xhat_t[:, u % 2, :],
                                        start=True, stop=True)
                    last.then_inc(done, 1)

            def down(i, u):
                pe.wait_ge(relu0_done, i + 1)
                pe.wait_ge(relu1_done, i + 1)
                if not isinstance(i, int) or i >= 2:
                    pe.wait_ge(y2_ready, i - 1)
                for c in range(FC):
                    last = t.matmul(bk[6 + u % 2][:, 0:D], hidden_t[:, u % 2, P * c:P * c + P],
                                    now[:, u, W2_AT + D * c:W2_AT + D * c + D], start=(c == 0), stop=(c == FC - 1))
                last.then_inc(mm2_done, 1)

            def step(i, u):
                up(i, u)
                if not isinstance(i, int) or i + 1 < N_T:
                    rows_t(i + 1, (u + 1) % RING)
                if not isinstance(i, int) or i >= 1:
                    down(i - 1, (u - 1) % RING)
            rows_t(0, 0)
            walk_tiles(pe, step)
            down(N_T - 1, (N_T - 1) % RING)


def program(nc, mamba_inputs, ffn_inputs, out):
    x = mamba_inputs[0]
    T, DM = x.shape[0] * x.shape[1], x.shape[2]
    EXT = DM + 5
    bc_scratch = nc.dram_tensor("bc_scratch", (32, 512), F32, kind="Internal").ap()
    x_rows = nc.dram_tensor("x_rows", (T, EXT), F32, kind="Internal").ap()
    E, F, D = ffn_inputs[3].shape
    w1_turned = nc.dram_tensor("w1_turned", (D, E, F), F32, kind="Internal").ap()
    w2_turned = nc.dram_tensor("w2_turned", (D, E, F), F32, kind="Internal").ap()
    blocks = T // P
    scored = blocks - 2 * (512 // P)
    centroids, gamma, beta, W1, b1, W2, b2 = ffn_inputs
    with ExitStack() as ctx:
        x_ext = ctx.enter_context(nc.sbuf_tensor("x_ext", [P, blocks, EXT], F32))
        small_t = ctx.enter_context(nc.sbuf_tensor("small_t", [P, 3, E], F32))
        score = ctx.enter_context(nc.sbuf_tensor("score", [P, blocks, E], F32))
        x1_mv = ctx.enter_context(nc.sbuf_tensor("x1_mv", [P, blocks, 2], F32))
        mamba_layer(nc, *mamba_inputs, W1, W2, w1_turned, w2_turned, bc_scratch, x_ext[:, :, 0:DM],
                    (centroids, gamma, beta), small_t, score, x1_mv)
        expert_layer(nc, x_ext, small_t, score, x1_mv, scored, W1, b1, W2, b2, w1_turned, w2_turned, x_rows, out)


_MAMBA = ['x', 'in_proj_w', 'conv_w', 'conv_b', 'x_proj_w', 'dt_proj_w', 'dt_proj_b', 'A_log', 'D', 'out_proj_w',
          'ln_g', 'ln_b']
_FFN = ['centroids', 'gamma', 'beta', 'W1', 'b1', 'W2', 'b2']


def kernel(**inputs):
    import numpy as _np
    import concourse.bacc as _bacc
    from concourse.bass_utils import run_bass_kernel_spmd as _run

    nc = _bacc.Bacc("TRN2", target_bir_lowering=False, num_devices=1)
    arrays = {}

    def declare(name):
        a = _np.ascontiguousarray(inputs[name])
        arrays["in_" + name] = a
        return nc.dram_tensor("in_" + name, a.shape, F32, kind="ExternalInput").ap()
    mamba_inputs = [declare("L0_attn_" + n) for n in _MAMBA]
    ffn_inputs = [declare("L0_ffn_" + n) for n in _FFN]
    shape = inputs["L0_attn_x"].shape
    out = nc.dram_tensor("out", (shape[0] * shape[1], shape[2]), F32, kind="ExternalOutput").ap()
    program(nc, mamba_inputs, ffn_inputs, out)
    r = _run(nc, [arrays], core_ids=[0])
    return r.results[0]["out"].reshape(shape)
```
